# Optimizing a Trainium2 kernel written in Bass

```python
import numpy as np
import jax
import jax.numpy as jnp

def _softmax(x, axis=-1):
    return jax.nn.softmax(x, axis=axis)

def _gelu(x):
    return jax.nn.gelu(x, approximate=True)

def _silu(x):
    return jax.nn.silu(x)

def _sigmoid(x):
    return jax.nn.sigmoid(x)

def _layernorm(x, axis=-1, eps=1e-05):
    m = jnp.mean(x, axis=axis, keepdims=True)
    v = jnp.var(x, axis=axis, keepdims=True)
    return (x - m) / jnp.sqrt(v + eps)

def _scatter_add(tgt, idx, src, axis=0):
    return tgt.at[idx].add(src)

def _segment_sum(src, seg, n):
    return jax.ops.segment_sum(src, seg, n)
kernel_name = 'mk_seq_postln_d1_jaxref_r4_d1227e'

def setup_inputs(seed: int=0):
    np.random.seed(seed)
    _w = jnp.asarray

    def _L0_attn_setup():
        import jax, jax.numpy as jnp
        import numpy as np
        import math
        N_HEAD = 16
        N_EMBD = 512
        HEAD_DIM = 128
        N_LAYER = 24
        EPS = 1e-05

        def _get_alibi_slopes(n_heads):

            def pow2(n):
                start = 2 ** (-2 ** (-(math.log2(n) - 3)))
                return [start * start ** i for i in range(n)]
            if math.log2(n_heads).is_integer():
                return pow2(n_heads)
            c = 2 ** math.floor(math.log2(n_heads))
            s = pow2(c)
            extra = _get_alibi_slopes(2 * c)
            return s + extra[0::2][:n_heads - c]
        ALIBI_SLOPES = jnp.asarray(np.array(_get_alibi_slopes(N_HEAD), dtype=np.float32))

        def rmsnorm(x, w, eps=EPS):
            xf = x.astype(jnp.float32)
            out = xf * jax.lax.rsqrt(jnp.mean(xf * xf, axis=-1, keepdims=True) + eps)
            return (out * w.astype(jnp.float32)).astype(x.dtype)
        key = jax.random.key(seed)
        ks = jax.random.split(key, 8)
        B, T, C, H, D = (2, 512, N_EMBD, N_HEAD, HEAD_DIM)
        sc = 1.0 / math.sqrt(C)
        proj_std = 0.5 / math.sqrt(C) / math.sqrt(N_LAYER)
        return {'x': jax.random.normal(ks[0], (B, T, C), jnp.float32), 'Wq': jax.random.normal(ks[1], (C, H * D), jnp.float32) * sc, 'Wk': jax.random.normal(ks[2], (C, H * D), jnp.float32) * sc, 'Wv': jax.random.normal(ks[3], (C, H * D), jnp.float32) * sc, 'Wproj': jax.random.normal(ks[4], (H * D, C), jnp.float32) * proj_std, 'q_rms_w': jnp.ones((D,), jnp.float32), 'k_rms_w': jnp.ones((D,), jnp.float32), 'subln_w': jnp.ones((D,), jnp.float32)}
    _L0_attn_in = _L0_attn_setup()

    def _L0_ffn_setup():
        import jax, jax.numpy as jnp
        import numpy as np
        NUM_EXPERTS = 8
        TOP_K = 2
        key = jax.random.key(seed)
        k1, k2, k3, k4 = jax.random.split(key, 4)
        B, T, C, E, D = (4, 512, 512, NUM_EXPERTS, 512)
        scale = 0.02
        return {'x': jax.random.normal(k1, (B, T, C), dtype=jnp.float32), 'w_router': jax.random.normal(k2, (C, E), dtype=jnp.float32) * scale, 'w_fc': jax.random.normal(k3, (E, C, D), dtype=jnp.float32) * scale, 'w_proj': jax.random.normal(k4, (E, D, C), dtype=jnp.float32) * scale}
    _L0_ffn_in = _L0_ffn_setup()
    _d = {'L0_attn_x': _L0_attn_in['x'], 'L0_attn_Wq': _L0_attn_in['Wq'], 'L0_attn_Wk': _L0_attn_in['Wk'], 'L0_attn_Wv': _L0_attn_in['Wv'], 'L0_attn_Wproj': _L0_attn_in['Wproj'], 'L0_attn_q_rms_w': _L0_attn_in['q_rms_w'], 'L0_attn_k_rms_w': _L0_attn_in['k_rms_w'], 'L0_attn_subln_w': _L0_attn_in['subln_w'], 'L0_ffn_w_router': _L0_ffn_in['w_router'], 'L0_ffn_w_fc': _L0_ffn_in['w_fc'], 'L0_ffn_w_proj': _L0_ffn_in['w_proj']}
    _x0 = _d['L0_attn_x']
    _d['L0_attn_x'] = jax.random.normal(jax.random.fold_in(jax.random.key(seed), 1), (4, 512, 512), dtype=_x0.dtype)
    del _x0
    return _d

def reference(L0_attn_x, L0_attn_Wq, L0_attn_Wk, L0_attn_Wv, L0_attn_Wproj, L0_attn_q_rms_w, L0_attn_k_rms_w, L0_attn_subln_w, L0_ffn_w_router, L0_ffn_w_fc, L0_ffn_w_proj):

    def _L0_attn_ref(x, Wq, Wk, Wv, Wproj, q_rms_w, k_rms_w, subln_w):
        import jax, jax.numpy as jnp
        import numpy as np
        import math
        N_HEAD = 16
        N_EMBD = 512
        HEAD_DIM = 128
        N_LAYER = 24
        EPS = 1e-05

        def _get_alibi_slopes(n_heads):

            def pow2(n):
                start = 2 ** (-2 ** (-(math.log2(n) - 3)))
                return [start * start ** i for i in range(n)]
            if math.log2(n_heads).is_integer():
                return pow2(n_heads)
            c = 2 ** math.floor(math.log2(n_heads))
            s = pow2(c)
            extra = _get_alibi_slopes(2 * c)
            return s + extra[0::2][:n_heads - c]
        ALIBI_SLOPES = jnp.asarray(np.array(_get_alibi_slopes(N_HEAD), dtype=np.float32))

        def rmsnorm(x, w, eps=EPS):
            xf = x.astype(jnp.float32)
            out = xf * jax.lax.rsqrt(jnp.mean(xf * xf, axis=-1, keepdims=True) + eps)
            return (out * w.astype(jnp.float32)).astype(x.dtype)
        B, T, C = x.shape
        H, D = (N_HEAD, HEAD_DIM)
        q = (x @ Wq).reshape(B, T, H, D)
        k = (x @ Wk).reshape(B, T, H, D)
        v = (x @ Wv).reshape(B, T, H, D)
        q = rmsnorm(q, q_rms_w)
        k = rmsnorm(k, k_rms_w)
        idx = jnp.arange(T)
        dist = jnp.maximum(idx[:, None] - idx[None, :], 0).astype(jnp.float32)
        bias = -dist[None, :, :] * ALIBI_SLOPES[:, None, None]
        causal = idx[:, None] >= idx[None, :]
        scale = 1.0 / math.sqrt(D)
        scores = jnp.einsum('bthd,bshd->bhts', q, k) * scale + bias[None]
        scores = jnp.where(causal[None, None], scores, -jnp.inf)
        attn = jax.nn.softmax(scores, axis=-1)
        y = jnp.einsum('bhts,bshd->bhtd', attn, v)
        y = rmsnorm(y, subln_w)
        y = y.transpose(0, 2, 1, 3).reshape(B, T, H * D)
        return y @ Wproj

    def _L0_ffn_ref(x, w_router, w_fc, w_proj):
        import jax, jax.numpy as jnp
        import numpy as np
        NUM_EXPERTS = 8
        TOP_K = 2
        B, T, C = x.shape
        E = w_fc.shape[0]
        x_flat = x.reshape(-1, C)
        N = x_flat.shape[0]
        router_logits = x_flat @ w_router
        top_vals, top_idx = jax.lax.top_k(router_logits, TOP_K)
        probs = jax.nn.softmax(top_vals, axis=-1)
        rows = jnp.arange(N)[:, None]
        w_tok = jnp.zeros((N, E), dtype=x.dtype).at[rows, top_idx].add(probs)
        h = jnp.einsum('nc,ecd->ned', x_flat, w_fc)
        h = jnp.square(jax.nn.relu(h))
        y = jnp.einsum('ned,edc->nec', h, w_proj)
        out = jnp.einsum('nec,ne->nc', y, w_tok)
        return out.reshape(B, T, C)
    x = L0_attn_x
    x = _layernorm(x + _L0_attn_ref(x, L0_attn_Wq, L0_attn_Wk, L0_attn_Wv, L0_attn_Wproj, L0_attn_q_rms_w, L0_attn_k_rms_w, L0_attn_subln_w), axis=-1)
    x = _layernorm(x + _L0_ffn_ref(x, L0_ffn_w_router, L0_ffn_w_fc, L0_ffn_w_proj), axis=-1)
    return x

_drawn_inputs = setup_inputs


def setup_inputs(seed=0):
    import zlib

    import numpy as np

    out = dict(_drawn_inputs(seed))
    spreads = {'L0_attn_q_rms_w': (1.0, 0.2),
     'L0_attn_k_rms_w': (1.0, 0.2),
     'L0_attn_subln_w': (1.0, 0.2)}
    factors = {}
    for name, (base, spread) in spreads.items():
        noise = np.random.default_rng([zlib.crc32(name.encode()), seed]).standard_normal(out[name].shape)
        drawn = base * np.exp(spread * noise) if base else spread * noise
        out[name] = jnp.asarray(drawn.astype(out[name].dtype))
    for name, factor in factors.items():
        out[name] = (out[name] * factor).astype(out[name].dtype)
    return out
```

```python
from contextlib import ExitStack

import numpy as np
import concourse.bass as bass
from concourse import mybir

dt = mybir.dt
F32, F32R = dt.float32, dt.float32r
ALU = mybir.AluOpType
ACT = mybir.ActivationFunctionType
AX = mybir.AxisListType

P = 128
B, T, C = 4, 512, 512
H, D = 16, 128
EPS = 1e-5
NT = B * T // P
TB = T // P
CT = C // P
HG = 4
NHG = H // HG
GW = HG * D
MASKED = 1e30
E = 8
F = 512
FT = F // P
SLOT_TILES = 2 * NT + E


def attention_phase(nc, sem, x_t, wq, wk, wv, qk_w, consts, y_scratch, slots_x):
    ident_d, dist_d, slopes_d = consts
    ctx = ExitStack()
    with ctx:
        def sb(name, shape, dtype=F32):
            return ctx.enter_context(nc.sbuf_tensor(name, shape, dtype))

        ident = sb("ident", [P, P])
        dist = sb("dist", [P, T])
        slopes = sb("slopes", [P, H])
        qkw = sb("qkw", [P, 2])
        q_scale = sb("q_scale", [P, 1])
        half = sb("half", [P, HG])
        eps = sb("eps", [P, HG])
        w_raw = sb("w_raw", [P, 2, 3, GW])
        w_hi = sb("w_hi", [P, 2, 3, CT, GW], F32R)
        w_lo = sb("w_lo", [P, 2, 3, CT, GW], F32R)
        x_raw = sb("x_raw", [P, 2, CT * P])
        x_hi = sb("x_hi", [P, 2, CT * P], F32R)
        x_lo = sb("x_lo", [P, 2, CT * P], F32R)
        kt_hi = sb("kt_hi", [P, 2, HG, T], F32R)
        kt_lo = sb("kt_lo", [P, 2, HG, T], F32R)
        vs = sb("vs", [P, 2, TB, GW])
        qt_hi = sb("qt_hi", [P, HG, P], F32R)
        qt_lo = sb("qt_lo", [P, HG, P], F32R)
        ksq = sb("ksq", [P, GW])
        qsq = sb("qsq", [P, GW])
        ysq = sb("ysq", [P, GW])
        kn = sb("kn", [P, GW])
        qn = sb("qn", [P, GW])
        yn = sb("yn", [P, 2, GW])
        bias = sb("bias", [P, HG, T])
        logit = sb("logit", [P, T])
        prob = sb("prob", [P, T])
        prob_t = sb("prob_t", [P, T])
        zeros = sb("zeros", [P, C])
        small = sb("small", [P, 64])
        k_ms, q_ms, y_ms = small[:, 0:4], small[:, 4:8], small[:, 8:12]
        k_me, q_me, y_me = small[:, 12:16], small[:, 16:20], small[:, 20:24]
        k_r, q_r, y_r = small[:, 24:28], small[:, 28:32], small[:, 32:36]
        least = small[:, 36:40]
        row_sum = small[:, 40:48]
        sum_eps = small[:, 48:56]

        def ps(name):
            return ctx.enter_context(nc.psum_tensor(name, [P, GW], F32))

        k_ps, q_ps, v_ps = ps("k_ps"), ps("q_ps"), ps("v_ps")
        kt_ps, qt_ps = ps("kt_ps"), ps("qt_ps")
        score_ps, prob_ps, y_ps = ps("score_ps"), ps("prob_ps"), ps("y_ps")

        const_loaded = sem("const_loaded")
        x_loaded = [sem("x_loaded0"), sem("x_loaded1")]
        w_loaded = sem("w_loaded")
        w_rounded, w_ready = sem("w_rounded"), sem("w_ready")
        x_rounded, x_ready = sem("x_rounded"), sem("x_ready")
        k_projected, q_projected, v_projected = sem("k_projected"), sem("q_projected"), sem("v_projected")
        k_squared, q_squared, y_squared = sem("k_squared"), sem("q_squared"), sem("y_squared")
        k_summed, q_summed, y_summed = sem("k_summed"), sem("q_summed"), sem("y_summed")
        k_biased, q_biased, y_biased = sem("k_biased"), sem("q_biased"), sem("y_biased")
        k_rstd, q_rstd, y_rstd = sem("k_rstd"), sem("q_rstd"), sem("y_rstd")
        k_normed, q_normed, y_normed = sem("k_normed"), sem("q_normed"), sem("y_normed")
        k_turned, q_turned = sem("k_turned"), sem("q_turned")
        k_rounded, q_rounded = sem("k_rounded"), sem("q_rounded")
        k_ready, q_ready, v_ready = sem("k_ready"), sem("q_ready"), sem("v_ready")
        scored, logits_ready, probs_ready = sem("scored"), sem("logits_ready"), sem("probs_ready")
        probs_turned, prob_t_ready = sem("probs_turned"), sem("prob_t_ready")
        y_done = sem("y_done")
        slots_cleared = sem("slots_cleared")
        y_stored = [sem("y_stored0"), sem("y_stored1")]
        set_up, scale_set, biases_set = sem("set_up"), sem("scale_set"), sem("biases_set")

        block = ctx.enter_context(nc.Block())
        its = NHG * B
        RB = 3

        @block.sync
        def _(sp):
            for b in range(2):
                sp.nop(nofuse=True).then_inc(y_stored[b], 16)
            sp.dma_start(ident[:, :], ident_d).then_inc(const_loaded, 16)
            sp.dma_start(dist[:, :], dist_d).then_inc(const_loaded, 16)
            sp.dma_start(slopes[:, :], slopes_d).then_inc(const_loaded, 16)
            sp.dma_start(qkw[:, :], qk_w).then_inc(const_loaded, 16)

            def load_w(rnd, parity):
                hg, c = (rnd // CT) % NHG, rnd % CT
                for m, w in enumerate((wq, wk, wv)):
                    sp.dma_start(w_raw[:, parity, m, :],
                                 w[bass.ds(c * P, P), bass.ds(hg * GW, GW)]).then_inc(w_loaded, 16)

            def load_x(tile, parity):
                sp.dma_start(x_raw[:, parity, :], x_t[tile]).then_inc(x_loaded[parity], 16)

            load_w(0, 0)
            load_x(0, 0)
            load_x(1, 1)
            for rnd in range(1, CT):
                sp.wait_ge(w_ready, RB * (rnd - 1) + 1)
                load_w(rnd, rnd % 2)
            for n in (2, 3):
                sp.wait_ge(x_ready, n - 1)
                load_x(n, n % 2)
            sp.wait_ge(set_up, 5)
            sp.dma_start(slots_x.rearrange("(k p) c -> p k c", p=P),
                         zeros[:, :].unsqueeze(1).to_broadcast([P, SLOT_TILES, C])).then_inc(slots_cleared, 16)
            with sp.Fori(0, its) as it:
                sp.wait_ge(w_ready, it * RB + (CT - 1) * RB + 1)
                w_rnd = it + CT
                for m, w in enumerate((wq, wk, wv)):
                    sp.dma_start(w_raw[:, bass.ds(it % 2, 1), m, :],
                                 w[bass.ds((w_rnd % CT) * P, P), bass.ds(((w_rnd // CT) % NHG) * GW, GW)])\
                        .then_inc(w_loaded, 16)
                for i in range(TB):
                    sp.wait_ge(x_ready, it * TB + i + 3)
                    sp.dma_start(x_raw[:, i % 2, :],
                                 x_t[bass.ds((it * TB + i + 4) % NT, 1), :, :].rearrange("o p c -> (o p) c"))\
                        .then_inc(x_loaded[i % 2], 16)
                    sp.wait_ge(y_normed, it * TB + i + 1)
                    sp.dma_start(y_scratch[bass.ds(it * TB + i, 1), :, :].rearrange("o p c -> (o p) c"),
                                 yn[:, i % 2, :]).then_inc(y_stored[i % 2], 16)
            sp.wait_ge(y_normed, its * TB + 1)
            sp.dma_start(y_scratch[its * TB, :, :], yn[:, 0, :]).then_inc(y_stored[0], 16)
            sp.wait_ge(slots_cleared, 16)
            sp.wait_ge(x_loaded[0], 16 * (its * TB // 2 + 2))
            sp.wait_ge(x_loaded[1], 16 * (its * TB // 2 + 2))
            sp.wait_ge(y_stored[0], 16 * (its * TB // 2 + 2))
            sp.wait_ge(y_stored[1], 16 * (its * TB // 2 + 1))

        @block.scalar
        def _(act):
            def round_w(m, rnd_parity, hg_parity, c, count):
                act.wait_ge(w_loaded, count)
                nc.scalar.activation(w_hi[:, hg_parity, m, c, :], w_raw[:, rnd_parity, m, :], ACT.Copy)\
                    .then_inc(w_rounded, 1)

            def round_x(parity, count):
                act.wait_ge(x_loaded[parity], count)
                nc.scalar.activation(x_hi[:, parity, :], x_raw[:, parity, :], ACT.Copy).then_inc(x_rounded, 1)

            def square(out, src, projected, count, done):
                act.wait_ge(projected, count)
                nc.scalar.activation(out[:, :], src[:, :], ACT.Square, scale=float(D) ** -0.5).then_inc(done, 1)

            def round_k(parity, i, count):
                act.wait_ge(k_turned, count)
                nc.scalar.activation(kt_hi[:, parity, :, i * P:(i + 1) * P],
                                     kt_ps[:, :].rearrange("p (h t) -> p h t", h=HG), ACT.Copy)\
                    .then_inc(k_rounded, 1)

            def round_q(count):
                act.wait_ge(q_turned, count)
                nc.scalar.activation(qt_hi[:, :, :], qt_ps[:, :].rearrange("p (h t) -> p h t", h=HG),
                                     ACT.Copy, scale=q_scale[:, 0:1]).then_inc(q_rounded, 1)

            def keep_v(parity, i, count):
                act.wait_ge(v_projected, count)
                nc.scalar.activation(vs[:, parity, i, :], v_ps[:, :], ACT.Copy).then_inc(v_ready, 1)

            for rnd in range(CT):
                for m in range(3):
                    round_w(m, rnd % 2, 0, rnd, 48 * (rnd + 1))
                if rnd < 2:
                    round_x(rnd, 16)
            square(ksq, k_ps, k_projected, 1, k_squared)
            square(qsq, q_ps, q_projected, 1, q_squared)
            round_k(0, 0, 1)
            act.wait_ge(scale_set, 2)
            round_q(1)
            keep_v(0, 0, 1)
            act.wait_ge(set_up, 5)
            nc.scalar.activation(sum_eps[:, 4:8], row_sum[:, 4:8], ACT.Square, scale=EPS ** 0.5)
            nc.scalar.activation(ysq[:, :], y_ps[:, :], ACT.Square, scale=float(D) ** -0.5).then_inc(y_squared, 1)

            with act.Fori(0, its) as it:
                for i in range(TB):
                    n = it * TB + i
                    width = P * (i + 1)
                    now = it % 2
                    nxt, nxt_i = (now, i + 1) if i < TB - 1 else ((it + 1) % 2, 0)

                    def softmax(h):
                        act.wait_ge(logits_ready, n * HG + h + 1)
                        nc.scalar.activation(prob[:, 0:width], logit[:, 0:width], ACT.Exp, scale=-1.0,
                                             bias=least[:, h:h + 1],
                                             accum_out=row_sum[:, (i % 2) * HG + h:(i % 2) * HG + h + 1])\
                            .then_inc(probs_ready, 1)

                    def keep_prob_t(h):
                        act.wait_ge(probs_turned, n * HG + h + 1)
                        nc.scalar.activation(prob_t[:, 0:width], prob_ps[:, 0:width], ACT.Copy)\
                            .then_inc(prob_t_ready, 1)

                    softmax(0)
                    square(ksq, k_ps, k_projected, n + 2, k_squared)
                    keep_prob_t(0)
                    act.wait_ge(x_loaded[i % 2], it * 32 + 16 * (i // 2 + 2))
                    nc.scalar.activation(x_hi[:, i % 2, :], x_raw[:, i % 2, :], ACT.Copy).then_inc(x_rounded, 1)
                    softmax(1)
                    square(qsq, q_ps, q_projected, n + 2, q_squared)
                    keep_prob_t(1)
                    if i < RB:
                        act.wait_ge(w_loaded, it * 48 + 48 * (CT + 1))
                        nc.scalar.activation(
                            w_hi[:, bass.ds((it // CT + 1) % 2, 1), i, bass.ds(it % CT, 1), :].rearrange("p a b c -> p (a b c)"),
                            w_raw[:, bass.ds(it % 2, 1), i, :].rearrange("p a c -> p (a c)"), ACT.Copy)\
                            .then_inc(w_rounded, 1)
                    softmax(2)
                    act.wait_ge(k_turned, n + 2)
                    nc.scalar.activation(
                        kt_hi[:, bass.ds(nxt, 1), :, nxt_i * P:(nxt_i + 1) * P].rearrange("p a h t -> p (a h) t"),
                        kt_ps[:, :].rearrange("p (h t) -> p h t", h=HG), ACT.Copy).then_inc(k_rounded, 1)
                    keep_prob_t(2)
                    softmax(3)
                    round_q(n + 2)
                    keep_prob_t(3)
                    act.wait_ge(v_projected, n + 2)
                    nc.scalar.activation(vs[:, bass.ds(nxt, 1), nxt_i, :].rearrange("p a c -> p (a c)"),
                                         v_ps[:, :], ACT.Copy).then_inc(v_ready, 1)
                    half_ = slice((i % 2) * HG, (i % 2 + 1) * HG)
                    act.wait_ge(probs_ready, n * HG + HG)
                    nc.scalar.activation(sum_eps[:, half_], row_sum[:, half_], ACT.Square, scale=EPS ** 0.5)
                    square(ysq, y_ps, y_done, n + 1, y_squared)

        @block.gpsimd
        def _(pool):
            def rstd(ms, me, r, summed, biased, ready, count, add):
                pool.wait_ge(summed, count)
                nc.gpsimd.tensor_tensor(me, ms, add, ALU.add).then_inc(biased, 1)
                pool.wait_ge(biased, count)
                nc.gpsimd.tensor_tensor(r, me, half[:, :], ALU.pow).then_inc(ready, 1)

            pool.wait_ge(set_up, 5)
            rstd(k_ms, k_me, k_r, k_summed, k_biased, k_rstd, 1, eps[:, :])
            rstd(q_ms, q_me, q_r, q_summed, q_biased, q_rstd, 1, eps[:, :])
            with pool.Fori(0, its) as it:
                for i in range(TB):
                    n = it * TB + i
                    rstd(y_ms, y_me, y_r, y_summed, y_biased, y_rstd, n + 1,
                         sum_eps[:, ((i + 1) % 2) * HG:((i + 1) % 2 + 1) * HG])
                    rstd(k_ms, k_me, k_r, k_summed, k_biased, k_rstd, n + 2, eps[:, :])
                    rstd(q_ms, q_me, q_r, q_summed, q_biased, q_rstd, n + 2, eps[:, :])
            rstd(y_ms, y_me, y_r, y_summed, y_biased, y_rstd, its * TB + 1, sum_eps[:, HG:2 * HG])

        @block.vector
        def _(dve):
            def heads(ap):
                return ap.rearrange("p (h d) -> p h d", h=HG)

            def row_means(sq, ms, squared, count, done):
                dve.wait_ge(squared, count)
                nc.vector.tensor_reduce(ms, heads(sq[:, :]), AX.X, ALU.add).then_inc(done, 1)

            def normalise(out, src, r, ready, count, done):
                dve.wait_ge(ready, count)
                nc.vector.tensor_tensor(heads(out), heads(src[:, :]),
                                        r.unsqueeze(2).to_broadcast([P, HG, D]), ALU.mult).then_inc(done, 1)

            def split_q(count):
                dve.wait_ge(q_rounded, count)
                nc.vector.scalar_tensor_tensor(qt_lo[:, :, :].rearrange("p h t -> p (h t)"), qt_ps[:, :], q_scale[:, 0:1],
                                               qt_hi[:, :, :].rearrange("p h t -> p (h t)"), ALU.mult, ALU.subtract)\
                    .then_inc(q_ready, 1)

            nc.vector.memset(half[:, :], -0.5).then_inc(set_up, 1)
            nc.vector.memset(eps[:, :], EPS).then_inc(set_up, 1)
            nc.vector.memset(y_ps[:, :], 0.0).then_inc(set_up, 1)
            nc.vector.memset(row_sum, 1.0).then_inc(set_up, 1)
            nc.vector.memset(zeros[:, :], 0.0).then_inc(set_up, 1)
            dve.wait_ge(const_loaded, 64)
            nc.vector.tensor_tensor(q_scale[:, :], qkw[:, 0:1], qkw[:, 1:2], ALU.mult).then_inc(scale_set, 1)
            dve.wait_ge(scale_set, 1)
            nc.vector.tensor_scalar(q_scale[:, :], q_scale[:, :], -float(D) ** -0.5, None, ALU.mult)\
                .then_inc(scale_set, 1)
            for rnd in range(CT):
                for m in range(3):
                    dve.wait_ge(w_rounded, rnd * 3 + m + 1)
                    nc.vector.tensor_tensor(w_lo[:, 0, m, rnd, :], w_raw[:, rnd % 2, m, :], w_hi[:, 0, m, rnd, :],
                                            ALU.subtract).then_inc(w_ready, 1)
                if rnd < 2:
                    dve.wait_ge(x_rounded, rnd + 1)
                    nc.vector.tensor_tensor(x_lo[:, rnd, :], x_raw[:, rnd, :], x_hi[:, rnd, :], ALU.subtract)\
                        .then_inc(x_ready, 1)
            row_means(ksq, k_ms, k_squared, 1, k_summed)
            row_means(qsq, q_ms, q_squared, 1, q_summed)
            normalise(kn[:, :], k_ps, k_r, k_rstd, 1, k_normed)
            normalise(qn[:, :], q_ps, q_r, q_rstd, 1, q_normed)
            dve.wait_ge(k_rounded, 1)
            nc.vector.tensor_tensor(kt_lo[:, 0, :, 0:P], kt_ps[:, :].rearrange("p (h t) -> p h t", h=HG),
                                    kt_hi[:, 0, :, 0:P], ALU.subtract).then_inc(k_ready, 1)
            dve.wait_ge(scale_set, 2)
            split_q(1)

            with dve.Fori(0, NHG) as hg:
                for h in range(HG):
                    nc.vector.tensor_scalar(bias[:, h, :], dist[:, :], slopes[:, bass.ds(hg * HG + h, 1)], None,
                                            ALU.mult).then_inc(biases_set, 1)
                dve.wait_ge(biases_set, hg * HG + HG)
                dve.nop(nofuse=True)
                with dve.Fori(0, B) as b:
                    it = hg * B + b
                    for i in range(TB):
                        n = it * TB + i
                        width = P * (i + 1)
                        nxt, nxt_i = (it % 2, i + 1) if i < TB - 1 else ((it + 1) % 2, 0)

                        def logits(h):
                            dve.wait_ge(scored, n * HG + h + 1)
                            dve.nop(nofuse=True)
                            nc.vector.tensor_tensor_reduce(
                                out=logit[:, 0:width], in0=score_ps[:, 0:width],
                                in1=bias[:, h, T - width:T], scale=1.0, scalar=3e38,
                                op0=ALU.add, op1=ALU.min, accum_out=least[:, h:h + 1]).then_inc(logits_ready, 1)

                        logits(0)
                        row_means(ysq, y_ms, y_squared, n + 1, y_summed)
                        dve.wait_ge(y_stored[i % 2], it * 32 + 16 * (i // 2 + 1))
                        normalise(yn[:, i % 2, :], y_ps, y_r, y_rstd, n + 1, y_normed)
                        row_means(ksq, k_ms, k_squared, n + 2, k_summed)
                        logits(1)
                        normalise(kn[:, :], k_ps, k_r, k_rstd, n + 2, k_normed)
                        dve.wait_ge(x_rounded, n + 3)
                        nc.vector.tensor_tensor(x_lo[:, i % 2, :], x_raw[:, i % 2, :], x_hi[:, i % 2, :],
                                                ALU.subtract).then_inc(x_ready, 1)
                        row_means(qsq, q_ms, q_squared, n + 2, q_summed)
                        logits(2)
                        normalise(qn[:, :], q_ps, q_r, q_rstd, n + 2, q_normed)
                        dve.wait_ge(k_rounded, n + 2)
                        nxt_k = slice(nxt_i * P, (nxt_i + 1) * P)
                        nc.vector.tensor_tensor(
                            kt_lo[:, bass.ds(nxt, 1), :, nxt_k].rearrange("p a h t -> p (a h) t"),
                            kt_ps[:, :].rearrange("p (h t) -> p h t", h=HG),
                            kt_hi[:, bass.ds(nxt, 1), :, nxt_k].rearrange("p a h t -> p (a h) t"),
                            ALU.subtract).then_inc(k_ready, 1)
                        logits(3)
                        split_q(n + 2)
                        if i < RB:
                            dve.wait_ge(w_rounded, it * RB + CT * RB + i + 1)
                            blk = (slice(None), bass.ds((hg + 1) % 2, 1), i, bass.ds(b, 1), slice(None))
                            nc.vector.tensor_tensor(
                                w_lo[blk].rearrange("p a b c -> p (a b c)"),
                                w_raw[:, bass.ds(it % 2, 1), i, :].rearrange("p a c -> p (a c)"),
                                w_hi[blk].rearrange("p a b c -> p (a b c)"), ALU.subtract).then_inc(w_ready, 1)
            row_means(ysq, y_ms, y_squared, its * TB + 1, y_summed)
            dve.wait_ge(y_stored[0], 16 * (its * TB // 2 + 1))
            normalise(yn[:, 0, :], y_ps, y_r, y_rstd, its * TB + 1, y_normed)

        @block.tensor
        def _(pe):
            def project(out, m, x_buf, parity, first=0, last=3 * CT):
                for s in range(first, last):
                    c, part = divmod(s, 3)
                    xs = (x_hi, x_hi, x_lo)[part][:, x_buf, c * P:(c + 1) * P]
                    w = (w_hi, w_lo, w_hi)[part]
                    if isinstance(parity, int):
                        ws = w[:, parity, m, c, :]
                    else:
                        ws = w[:, bass.ds(parity, 1), m, c, :].rearrange("p a c -> p (a c)")
                    mm = nc.tensor.matmul(out[:, :], xs, ws, start=(s == 0), stop=(s == 3 * CT - 1))
                return mm

            def turn(out, src, done):
                for h in range(HG):
                    mm = nc.tensor.transpose(out[:, h * P:(h + 1) * P], src[:, h * D:(h + 1) * D], ident[:, :])
                mm.then_inc(done, 1)

            pe.wait_ge(const_loaded, 64)
            pe.wait_ge(set_up, 5)
            pe.wait_ge(x_ready, 1)
            pe.wait_ge(w_ready, 3 * CT)
            project(k_ps, 1, 0, 0).then_inc(k_projected, 1)
            project(q_ps, 0, 0, 0).then_inc(q_projected, 1)
            project(v_ps, 2, 0, 0).then_inc(v_projected, 1)
            pe.wait_ge(k_normed, 1)
            turn(kt_ps, kn, k_turned)
            pe.wait_ge(q_normed, 1)
            turn(qt_ps, qn, q_turned)

            with pe.Fori(0, its) as it:
                for i in range(TB):
                    n = it * TB + i
                    now = it % 2
                    xb = (i + 1) % 2
                    wp = (it // B) % 2 if i < TB - 1 else ((it + 1) // B) % 2
                    width = P * (i + 1)

                    def score(h):
                        for part in range(3):
                            qs = (qt_hi, qt_hi, qt_lo)[part][:, h, :]
                            ks = (kt_hi, kt_lo, kt_hi)[part]
                            keys = ks[:, bass.ds(now, 1), h, 0:width]
                            keys = keys.to_broadcast([P, 2, P]) if i == 0 else keys.rearrange("p a c -> p (a c)")
                            mm = nc.tensor.matmul(score_ps[:, 0:max(width, 2 * P)], qs, keys,
                                                  start=(part == 0), stop=(part == 2))
                        mm.then_inc(scored, 1)

                    def turn_probs(h):
                        pe.wait_ge(probs_ready, n * HG + h + 1)
                        for j in range(i + 1):
                            mm = nc.tensor.transpose(prob_ps[:, j * P:(j + 1) * P], prob[:, j * P:(j + 1) * P],
                                                     ident[:, :])
                        mm.then_inc(probs_turned, 1)

                    def attend(h):
                        pe.wait_ge(prob_t_ready, n * HG + h + 1)
                        for j in range(i + 1):
                            mm = nc.tensor.matmul(
                                y_ps[:, h * D:(h + 1) * D], prob_t[:, j * P:(j + 1) * P],
                                vs[:, bass.ds(now, 1), j, h * D:(h + 1) * D].rearrange("p a c -> p (a c)"),
                                start=(j == 0), stop=(j == i))
                        return mm

                    pe.wait_ge(k_ready, n + 1)
                    pe.wait_ge(q_ready, n + 1)
                    score(0)
                    pe.wait_ge(x_ready, n + 2)
                    if i == TB - 1:
                        pe.wait_ge(w_ready, it * RB + (CT + 1) * RB)
                    project(k_ps, 1, xb, wp).then_inc(k_projected, 1)
                    turn_probs(0)
                    score(1)
                    pe.wait_ge(v_ready, n + 1)
                    pe.wait_ge(y_normed, n + 1)
                    attend(0)
                    project(q_ps, 0, xb, wp).then_inc(q_projected, 1)
                    turn_probs(1)
                    score(2)
                    attend(1)
                    pe.wait_ge(k_normed, n + 2)
                    turn(kt_ps, kn, k_turned)
                    project(v_ps, 2, xb, wp, 0, 5)
                    turn_probs(2)
                    score(3)
                    attend(2)
                    project(v_ps, 2, xb, wp, 5, 8)
                    pe.wait_ge(q_normed, n + 2)
                    turn(qt_ps, qn, q_turned)
                    turn_probs(3)
                    project(v_ps, 2, xb, wp, 8, 12).then_inc(v_projected, 1)
                    attend(3).then_inc(y_done, 1)


def residual_phase(nc, sem, y_scratch, w_proj, subln_w, x_d, ident_d, w_router, x1, logits):
    ctx = ExitStack()
    with ctx:
        def sb(name, shape, dtype=F32):
            return ctx.enter_context(nc.sbuf_tensor(name, shape, dtype))

        ident = sb("ident2", [P, P])
        subln = sb("subln", [P, 1])
        w_r = sb("w_r", [P, CT, E])
        wp_raw = sb("wp_raw", [P, 2, HG, C])
        wp_hi = sb("wp_hi", [P, H, C], F32R)
        wp_lo = sb("wp_lo", [P, H, C], F32R)
        y_raw = sb("y_raw", [P, 2, NHG, GW])
        yt_hi = sb("yt_hi", [P, 2, NHG, GW], F32R)
        yt_lo = sb("yt_lo", [P, 2, NHG, GW], F32R)
        x_nat = sb("x_nat", [P, 2, C])
        res = sb("res", [P, C])
        stats = sb("stats", [P, 6])
        mean_var = sb("mean_var", [P, 2])
        var_eps = sb("var_eps", [P, 1])
        rstd = sb("rstd", [P, 1])
        half = sb("half2", [P, 1])
        eps = sb("eps2", [P, 1])
        x1_now = sb("x1_now", [P, C])
        x1_t = sb("x1_t", [P, C])

        def ps(name):
            return ctx.enter_context(nc.psum_tensor(name, [P, C], F32))

        turn_ps = [ps(f"turn_ps{g}") for g in range(NHG)]
        out_ps = [ps("out_ps0"), ps("out_ps1")]
        x1_ps, router_ps = ps("x1_ps"), ps("router_ps")

        const_loaded = sem("p_const_loaded")
        wp_loaded, wp_rounded, wp_ready = sem("wp_loaded"), sem("wp_rounded"), sem("wp_ready")
        y_loaded = [sem("y_loaded0"), sem("y_loaded1")]
        x_loaded = [sem("xn_loaded0"), sem("xn_loaded1")]
        set_up = sem("p_set_up")
        y_turned, yt_rounded, yt_ready = sem("y_turned"), sem("yt_rounded"), sem("yt_ready")
        projected, summed, stats_done = sem("projected"), sem("res_summed"), sem("stats_done")
        var_ready, var_biased, rstd_ready = sem("var_ready"), sem("var_biased"), sem("rstd_ready")
        x1_ready, x1_turned, x1_t_ready = sem("x1_ready"), sem("x1_turned"), sem("x1_t_ready")
        x1_kept = sem("x1_kept")
        routed, logits_kept = sem("routed"), sem("logits_kept")
        block = ctx.enter_context(nc.Block())
        pairs = NT // 2

        y_tiles = y_scratch[1:1 + NHG * NT, :, :].rearrange("(g t) p c -> t p g c", g=NHG)
        x_tiles = x_d.rearrange("(t p) c -> t p c", p=P)
        wp_tiles = w_proj.rearrange("(g h p) c -> g p h c", h=HG, p=P)

        @block.sync
        def _(sp):
            sp.nop(nofuse=True).then_inc(x_loaded[1], 16)
            sp.dma_start(wp_raw[:, 0, :, :], wp_tiles[0]).then_inc(wp_loaded, 16)
            sp.dma_start(y_raw[:, 0, :, :], y_tiles[0]).then_inc(y_loaded[0], 16)
            sp.dma_start(ident[:, :], ident_d).then_inc(const_loaded, 16)
            sp.dma_start(subln[:, :], subln_w).then_inc(const_loaded, 16)
            sp.dma_start(w_r[:, :, :], w_router.rearrange("(c p) e -> p c e", p=P)).then_inc(const_loaded, 16)
            for g in range(1, NHG):
                sp.wait_ge(wp_ready, HG * (g - 1) + 1)
                sp.dma_start(wp_raw[:, g % 2, :, :], wp_tiles[g]).then_inc(wp_loaded, 16)
            sp.dma_start(x_nat[:, 0, :], x_tiles[0]).then_inc(x_loaded[0], 16)
            with sp.Fori(0, pairs) as pair:
                for b in range(2):
                    t = pair * 2 + b
                    sp.wait_ge(y_turned, t * NHG + NHG)
                    if b == 0:
                        sp.dma_start(y_raw[:, 1, :, :],
                                     y_tiles[bass.ds(t + 1, 1), :, :, :].rearrange("o p g c -> (o p) g c"))\
                            .then_inc(y_loaded[1], 16)
                        sp.wait_ge(summed, t + 1)
                        sp.nop(nofuse=True)
                        sp.dma_start(x_nat[:, 1, :],
                                     x_tiles[bass.ds(t + 1, 1), :, :].rearrange("o p c -> (o p) c"))\
                            .then_inc(x_loaded[1], 16)
                    else:
                        nxt = (t + 1) % NT
                        sp.dma_start(y_raw[:, 0, :, :],
                                     y_tiles[bass.ds(nxt, 1), :, :, :].rearrange("o p g c -> (o p) g c"))\
                            .then_inc(y_loaded[0], 16)
                        sp.wait_ge(summed, t + 1)
                        sp.nop(nofuse=True)
                        sp.dma_start(x_nat[:, 0, :],
                                     x_tiles[bass.ds(nxt, 1), :, :].rearrange("o p c -> (o p) c"))\
                            .then_inc(x_loaded[0], 16)
            sp.wait_ge(y_loaded[0], 16 * (pairs + 1))
            sp.wait_ge(x_loaded[0], 16 * (pairs + 1))

        @block.scalar
        def _(act):
            def round_y(buf, g, count):
                act.wait_ge(y_turned, count)
                nc.scalar.activation(yt_hi[:, buf, g, :], turn_ps[g][:, :], ACT.Copy, scale=subln[:, 0:1])\
                    .then_inc(yt_rounded, 1)

            def keep_x1(slot, count):
                act.wait_ge(x1_ready, count)
                out = x1[:, slot, :] if isinstance(slot, int) else \
                    x1[:, bass.ds(slot, 1), :].rearrange("p a c -> p (a c)")
                nc.scalar.activation(out, x1_now[:, :], ACT.Copy).then_inc(x1_kept, 1)

            def keep_x1_t(count):
                act.wait_ge(x1_turned, count)
                nc.scalar.activation(x1_t[:, :], x1_ps[:, :], ACT.Copy).then_inc(x1_t_ready, 1)

            act.nop(nofuse=True).then_inc(x1_kept, 1)
            for g in range(NHG):
                act.wait_ge(wp_loaded, 16 * (g + 1))
                for h in range(HG):
                    nc.scalar.activation(wp_hi[:, g * HG + h, :], wp_raw[:, g % 2, h, :], ACT.Copy)\
                        .then_inc(wp_rounded, 1)
            act.wait_ge(const_loaded, 48)
            for g in range(NHG):
                round_y(0, g, g + 1)
            with act.Fori(0, pairs) as pair:
                for b in range(2):
                    t = pair * 2 + b
                    for g in range(NHG):
                        round_y(1 - b, g, (t + 1) * NHG + g + 1)
                        if g == 1:
                            keep_x1(t, t + 1)
                            keep_x1_t(t + 1)
            keep_x1(NT, NT + 1)
            keep_x1_t(NT + 1)
            act.wait_ge(x1_kept, NT + 2)

        @block.gpsimd
        def _(pool):
            def inverse_std(count):
                pool.wait_ge(var_ready, count)
                nc.gpsimd.tensor_tensor(var_eps[:, :], mean_var[:, 1:2], eps[:, :], ALU.add).then_inc(var_biased, 1)
                pool.wait_ge(var_biased, count)
                nc.gpsimd.tensor_tensor(rstd[:, :], var_eps[:, :], half[:, :], ALU.pow).then_inc(rstd_ready, 1)

            pool.wait_ge(set_up, 4)
            with pool.Fori(0, NT + 1) as t:
                inverse_std(t + 1)

        @block.vector
        def _(dve):
            def split_y(buf, g, count):
                dve.wait_ge(yt_rounded, count)
                nc.vector.scalar_tensor_tensor(yt_lo[:, buf, g, :], turn_ps[g][:, :], subln[:, 0:1],
                                               yt_hi[:, buf, g, :], ALU.mult, ALU.subtract).then_inc(yt_ready, 1)

            def add_residual(buf, count):
                nc.vector.tensor_tensor(res[:, :], out_ps[buf][:, :], x_nat[:, buf, :], ALU.add).then_inc(summed, 1)
                dve.wait_ge(summed, count)
                nc.vector.bn_stats(stats[:, :], res[:, :]).then_inc(stats_done, 1)
                dve.wait_ge(stats_done, count)
                dve.nop(nofuse=True)
                nc.vector.bn_aggr(mean_var[:, :], stats[:, :]).then_inc(var_ready, 1)

            def layernorm(count):
                dve.wait_ge(rstd_ready, count)
                dve.wait_ge(x1_kept, count)
                nc.vector.tensor_scalar(x1_now[:, :], res[:, :], mean_var[:, 0:1], rstd[:, 0:1],
                                        ALU.subtract, ALU.mult).then_inc(x1_ready, 1)

            def keep_logits(slot, count):
                dve.wait_ge(routed, count)
                out = logits[:, bass.ds(slot, 1), :].rearrange("p a c -> p (a c)")
                nc.vector.tensor_copy(out, router_ps[:, 0:E]).then_inc(logits_kept, 1)

            nc.vector.memset(half[:, :], -0.5).then_inc(set_up, 1)
            nc.vector.memset(eps[:, :], EPS).then_inc(set_up, 1)
            dve.nop(nofuse=True).then_inc(logits_kept, 1)
            nc.vector.memset(x_nat[:, 1, :], 0.0).then_inc(set_up, 1)
            nc.vector.memset(out_ps[1][:, :], 0.0).then_inc(set_up, 1)
            for g in range(NHG):
                for h in range(HG):
                    dve.wait_ge(wp_rounded, g * HG + h + 1)
                    nc.vector.tensor_tensor(wp_lo[:, g * HG + h, :], wp_raw[:, g % 2, h, :],
                                            wp_hi[:, g * HG + h, :], ALU.subtract).then_inc(wp_ready, 1)
            dve.wait_ge(const_loaded, 48)
            for g in range(NHG):
                split_y(0, g, g + 1)
            dve.wait_ge(set_up, 4)
            with dve.Fori(0, pairs) as pair:
                for b in range(2):
                    t = pair * 2 + b
                    dve.wait_ge(projected, t + 1)
                    dve.wait_ge(x_loaded[1 - b], pair * 16 + 16)
                    add_residual(1 - b, t + 1)
                    split_y(1 - b, 0, (t + 1) * NHG + 1)
                    layernorm(t + 1)
                    split_y(1 - b, 1, (t + 1) * NHG + 2)
                    split_y(1 - b, 2, (t + 1) * NHG + 3)
                    keep_logits(t, t + 1)
                    split_y(1 - b, 3, (t + 1) * NHG + 4)
            dve.wait_ge(projected, NT + 1)
            dve.wait_ge(x_loaded[1], 16 * (pairs + 1))
            add_residual(1, NT + 1)
            layernorm(NT + 1)
            dve.wait_ge(routed, NT + 1)
            nc.vector.tensor_copy(logits[:, NT, :], router_ps[:, 0:E]).then_inc(logits_kept, 1)
            dve.wait_ge(logits_kept, NT + 2)

        @block.tensor
        def _(pe):
            def turn_y(buf, g):
                for h in range(HG):
                    mm = nc.tensor.transpose(turn_ps[g][:, h * P:(h + 1) * P],
                                             y_raw[:, buf, g, h * P:(h + 1) * P], ident[:, :])
                mm.then_inc(y_turned, 1)

            def project(buf, g):
                for h in range(HG):
                    for part in range(3):
                        ys = (yt_hi, yt_hi, yt_lo)[part][:, buf, g, h * P:(h + 1) * P]
                        ws = (wp_hi, wp_lo, wp_hi)[part][:, g * HG + h, :]
                        mm = nc.tensor.matmul(out_ps[buf][:, :], ys, ws, start=(g == h == part == 0),
                                              stop=(g == NHG - 1 and h == HG - 1 and part == 2))
                return mm

            def turn_x1(count):
                pe.wait_ge(x1_ready, count)
                for c in range(CT):
                    mm = nc.tensor.transpose(x1_ps[:, c * P:(c + 1) * P], x1_now[:, c * P:(c + 1) * P], ident[:, :])
                mm.then_inc(x1_turned, 1)

            def route(count):
                pe.wait_ge(x1_t_ready, count)
                pe.wait_ge(logits_kept, count)
                for c in range(CT):
                    mm = nc.tensor.matmul(router_ps[:, 0:E], x1_t[:, c * P:(c + 1) * P], w_r[:, c, :],
                                          start=(c == 0), stop=(c == CT - 1))
                mm.then_inc(routed, 1)

            pe.nop(nofuse=True).then_inc(projected, 1)
            pe.wait_ge(const_loaded, 48)
            pe.wait_ge(set_up, 4)
            pe.wait_ge(y_loaded[0], 16)
            for g in range(NHG):
                turn_y(0, g)
            pe.wait_ge(wp_ready, H)
            with pe.Fori(0, pairs) as pair:
                for b in range(2):
                    t = pair * 2 + b
                    for g in range(NHG):
                        pe.wait_ge(yt_ready, t * NHG + g + 1)
                        mm = project(b, g)
                        if g == NHG - 1:
                            mm.then_inc(projected, 1)
                        if g == 0:
                            pe.wait_ge(y_loaded[1 - b], pair * 16 + 16 * (b + 1))
                        turn_y(1 - b, g)
                        if g == 1:
                            turn_x1(t + 1)
                        if g == 2:
                            route(t + 1)
            turn_x1(NT + 1)
            route(NT + 1)


def expert_phase(nc, sem, x1, logits, w_fc, w_down, moe_consts, ident_d, slots_x, slots_y, out_d):
    before_d, experts_d, floors_d, restart_d, tiles_d = moe_consts
    ctx = ExitStack()
    with ctx:
        def sb(name, shape, dtype=F32):
            return ctx.enter_context(nc.sbuf_tensor(name, shape, dtype))

        WT = CT + FT
        ident = sb("ident3", [P, P])
        before = sb("before", [P, P])
        ones = sb("ones", [P, P])
        experts = sb("experts", [P, NT * E])
        floors = sb("floors", [P, E * NT])
        restart = sb("restart", [P, E * NT])
        tiles = sb("tiles", [P, SLOT_TILES * E])
        half = sb("half3", [P, 1])
        eps = sb("eps3", [P, 1])
        best = sb("best", [P, NT, 8])
        best_at = sb("best_at", [P, NT, 8], dt.uint32)
        choice = sb("choice", [P, 2, NT])
        taken = [sb(f"taken{j}", [P, NT, E]) for j in range(2)]
        both = sb("both", [P, NT, E])
        gap = sb("gap", [P, NT])
        gate = sb("gate", [P, 2, NT])
        total = sb("total", [P, E, NT])
        upto = sb("upto", [P, E, NT])
        slot_of = sb("slot_of", [P, E, NT])
        over = sb("over", [P, E, NT])
        n_tiles = sb("n_tiles", [P, E])
        end_tile = sb("end_tile", [P, E])
        base = sb("base", [P, E])
        pick = sb("pick", [P, NT, E])
        slot_f = sb("slot_f", [P, 2, NT])
        slot = sb("slot", [P, 2, NT], dt.uint32)
        past = sb("past", [P, SLOT_TILES, E])
        owner_f = sb("owner_f", [P, SLOT_TILES])
        owner = sb("owner", [P, SLOT_TILES + 1], dt.int32)
        end_i = sb("end_i", [P, E], dt.int32)
        w_raw = sb("we_raw", [P, WT, F])
        w_hi = sb("we_hi", [P, 2, WT, F], F32R)
        w_lo = sb("we_lo", [P, 2, WT, F], F32R)
        xs = sb("xs", [P, 2, C])
        xt_hi = sb("xt_hi", [P, 2, C], F32R)
        xt_lo = sb("xt_lo", [P, 2, C], F32R)
        relu = sb("relu", [P, F])
        hid = sb("hid", [P, 2, F])
        ht_hi = sb("ht_hi", [P, 2, F], F32R)
        ht_lo = sb("ht_lo", [P, 2, F], F32R)
        yo = sb("yo", [P, 2, C])
        GB = 2
        got = [sb(f"got{j}", [P, GB, C]) for j in range(2)]
        acc = sb("acc", [P, C])
        res = sb("res3", [P, C])
        stats = sb("stats3", [P, 6])
        mean_var = sb("mean_var3", [P, 2])
        var_eps = sb("var_eps3", [P, 1])
        rstd = sb("rstd3", [P, 1])
        fin = sb("fin", [P, 2, C])

        def ps(name):
            return ctx.enter_context(nc.psum_tensor(name, [P, C], F32))

        xt_ps, h_ps, ht_ps, ye_ps = ([ps(f"{n}{b}") for b in range(2)] for n in ("xt_ps", "h_ps", "ht_ps", "ye_ps"))
        rank_ps, total_ps = xt_ps[0], xt_ps[1]

        const_loaded, set_up = sem("e_const_loaded"), sem("e_set_up")
        step = sem("routing_step")
        masks_ready, ranked = sem("masks_ready"), sem("ranked")
        gap_ready, gap_exp = sem("gap_ready"), sem("gap_exp")
        slots_known = sem("slots_known")
        we_loaded, we_rounded, we_split, we_ready = sem("we_loaded"), sem("we_rounded"), sem("we_split"), sem("we_ready")
        dispatched = sem("dispatched")
        xs_loaded = [sem("xs_loaded0"), sem("xs_loaded1")]
        xs_turned, xt_rounded, xt_ready = sem("xs_turned"), sem("xt_rounded"), sem("xt_ready")
        up_done, relu_done, hid_ready = sem("up_done"), sem("relu_done"), sem("hid_ready")
        hid_turned, ht_rounded, ht_ready = sem("hid_turned"), sem("ht_rounded"), sem("ht_ready")
        down_done, yo_ready = sem("down_done"), sem("yo_ready")
        yo_stored = [sem("yo_stored0"), sem("yo_stored1")]
        gathered = [sem(f"gathered{b}") for b in range(GB)]
        acc_done, summed, stats_done = sem("acc_done"), sem("e_summed"), sem("e_stats_done")
        var_ready, var_biased, rstd_ready = sem("e_var_ready"), sem("e_var_biased"), sem("e_rstd_ready")
        fin_ready = sem("fin_ready")
        fin_stored = [sem("fin_stored0"), sem("fin_stored1")]
        block = ctx.enter_context(nc.Block())
        pairs = SLOT_TILES // 2
        x_slots = slots_x.rearrange("(k p) c -> k p c", p=P)
        y_slots = slots_y.rearrange("(k p) c -> k p c", p=P)
        out_tiles = out_d.rearrange("(t p) c -> t p c", p=P)

        @block.sync
        def _(sp):
            for b in range(2):
                sp.nop(nofuse=True).then_inc(yo_stored[b], 16)
            for dst, src in ((ident, ident_d), (before, before_d), (experts, experts_d), (floors, floors_d),
                             (restart, restart_d), (tiles, tiles_d)):
                sp.dma_start(dst[:, :], src).then_inc(const_loaded, 16)
            sp.wait_ge(dispatched, 16 * 2 * NT)
            sp.dma_start(xs[:, 0, :], x_slots[0]).then_inc(xs_loaded[0], 16)
            sp.dma_start(xs[:, 1, :], x_slots[1]).then_inc(xs_loaded[1], 16)
            with sp.Fori(0, pairs) as pair:
                for b in range(2):
                    k = pair * 2 + b
                    sp.wait_ge(xs_turned, k + 1)
                    sp.dma_start(xs[:, b, :], x_slots[bass.ds((k + 2) % SLOT_TILES, 1), :, :]
                                 .rearrange("o p c -> (o p) c")).then_inc(xs_loaded[b], 16)
                    sp.wait_ge(yo_ready, k + 2)
                    sp.dma_start(y_slots[bass.ds(k, 1), :, :].rearrange("o p c -> (o p) c"), yo[:, b, :])\
                        .then_inc(yo_stored[b], 16)
            with sp.Fori(0, NT // 2) as pair:
                for b in range(2):
                    sp.wait_ge(fin_ready, pair * 2 + b + 1)
                    sp.dma_start(out_tiles[bass.ds(pair * 2 + b, 1), :, :].rearrange("o p c -> (o p) c"),
                                 fin[:, b, :]).then_inc(fin_stored[b], 16)
            for b in range(2):
                sp.wait_ge(xs_loaded[b], 16 * (pairs + 1))
                sp.wait_ge(yo_stored[b], 16 * (pairs + 1))
                sp.wait_ge(fin_stored[b], 16 * (NT // 2))

        @block.gpsimd
        def _(pool):
            def load_weights(e, first):
                parity = e % 2
                for m, w in enumerate((w_fc, w_down)):
                    if first:
                        src = w[e].rearrange("(c p) f -> p c f", p=P)
                        hi = w_hi[:, parity, m * CT:(m + 1) * CT, :]
                    else:
                        src = w[bass.ds(e, 1), :, :].rearrange("o (c p) f -> (o p) c f", p=P)
                        hi = w_hi[:, bass.ds(parity, 1), m * CT:(m + 1) * CT, :].rearrange("p o c f -> p (o c) f")
                    pool.dma_start(hi, src).then_inc(we_loaded, 16)
                    pool.dma_start(w_raw[:, m * CT:(m + 1) * CT, :], src).then_inc(we_loaded, 16)

            def split_weights(e, first):
                pool.wait_ge(we_loaded, 64 * e + 64)
                for s in range(WT):
                    if first:
                        hi, lo = w_hi[:, e % 2, s, :], w_lo[:, e % 2, s, :]
                    else:
                        hi, lo = (w[:, bass.ds(e % 2, 1), s, :].rearrange("p o f -> p (o f)") for w in (w_hi, w_lo))
                    op = nc.gpsimd.tensor_tensor(lo, w_raw[:, s, :], hi, ALU.subtract)
                    op.then_inc(we_split, 1)
                pool.wait_ge(we_split, WT * e + WT)

            load_weights(0, True)
            split_weights(0, True)
            load_weights(1, True)
            pool.wait_ge(slots_known, 2)
            for t in range(NT):
                for j in range(2):
                    pool.indirect_dma_start(slots_x, bass.IndirectOffsetOnAxis(ap=slot[:, j, t:t + 1], axis=0),
                                            x1[:, t + 1, :], None).then_inc(dispatched, 16)
            split_weights(1, True)
            with pool.Fori(2, E) as e:
                end = pool.value_load(end_i[0:1, bass.ds(e - 2, 1)], min_val=1, max_val=SLOT_TILES)
                pool.wait_ge(down_done, end)
                load_weights(e, False)
                split_weights(e, False)
            for b in range(2):
                pool.wait_ge(yo_stored[b], 16 * (pairs + 1))

            def gather(t):
                if t >= GB:
                    pool.wait_ge(summed, t - GB + 1)
                for j in range(2):
                    pool.indirect_dma_start(got[j][:, t % GB, :], None, slots_y,
                                            bass.IndirectOffsetOnAxis(ap=slot[:, j, t:t + 1], axis=0))\
                        .then_inc(gathered[t % GB], 16)

            gather(0)
            for t in range(NT):
                if t + 1 < NT:
                    gather(t + 1)
                pool.wait_ge(var_ready, t + 1)
                nc.gpsimd.tensor_tensor(var_eps[:, :], mean_var[:, 1:2], eps[:, :], ALU.add).then_inc(var_biased, 1)
                pool.wait_ge(var_biased, t + 1)
                nc.gpsimd.tensor_tensor(rstd[:, :], var_eps[:, :], half[:, :], ALU.pow).then_inc(rstd_ready, 1)

        @block.scalar
        def _(act):
            act.nop(nofuse=True).then_inc(yo_ready, 1)
            act.wait_ge(gap_ready, 1)
            nc.scalar.activation(gate[:, 1, :], gap[:, :], ACT.Exp).then_inc(gap_exp, 1)

            def round_x(b, count):
                act.wait_ge(xs_turned, count)
                nc.scalar.activation(xt_hi[:, b, :], xt_ps[b][:, :], ACT.Copy).then_inc(xt_rounded, 1)

            def rectify(b, count):
                act.wait_ge(up_done, count)
                if not isinstance(count, int):
                    act.wait_ge(hid_ready, count - 1)
                nc.scalar.activation(relu[:, :], h_ps[b][:, :], ACT.Relu).then_inc(relu_done, 1)

            round_x(0, 1)
            rectify(0, 1)
            round_x(1, 2)
            with act.Fori(0, pairs) as pair:
                for b in range(2):
                    k = pair * 2 + b
                    act.wait_ge(hid_turned, k + 1)
                    nc.scalar.activation(ht_hi[:, b, :], ht_ps[b][:, :], ACT.Copy).then_inc(ht_rounded, 1)
                    round_x(b, k + 3)
                    rectify(1 - b, k + 2)
                    act.wait_ge(down_done, k + 1)
                    act.wait_ge(yo_stored[b], pair * 16 + 16)
                    nc.scalar.activation(yo[:, b, :], ye_ps[b][:, :], ACT.Copy).then_inc(yo_ready, 1)

        @block.vector
        def _(dve):
            steps = [0]

            def then(op):
                steps[0] += 1
                op.then_inc(step, 1)
                dve.wait_ge(step, steps[0])

            nc.vector.memset(half[:, :], -0.5).then_inc(set_up, 1)
            nc.vector.memset(eps[:, :], EPS).then_inc(set_up, 1)
            nc.vector.memset(owner[:, :], E - 1).then_inc(set_up, 1)
            nc.vector.memset(ones[:, :], 1.0).then_inc(set_up, 1)
            for t in range(NT):
                op = nc.vector.max(best[:, t, :], logits[:, t + 1, :])
            then(op)
            for t in range(NT):
                op = nc.vector.max_index(best_at[:, t, :], best[:, t, :], logits[:, t + 1, :])
            then(op)
            for j in range(2):
                op = nc.vector.tensor_copy(choice[:, j, :], best_at[:, :, j])
            then(op)
            dve.wait_ge(const_loaded, 96)
            dve.wait_ge(set_up, 4)
            for j in range(2):
                op = nc.vector.tensor_tensor(taken[j][:, :, :], experts[:, :].rearrange("p (t e) -> p t e", e=E),
                                             choice[:, j, :].unsqueeze(2).to_broadcast([P, NT, E]), ALU.is_equal)
            then(op)
            nc.vector.tensor_tensor(both[:, :, :], taken[0][:, :, :], taken[1][:, :, :], ALU.add)\
                .then_inc(masks_ready, 1)
            nc.vector.tensor_tensor(gap[:, :], best[:, :, 1], best[:, :, 0], ALU.subtract).then_inc(gap_ready, 1)
            dve.wait_ge(gap_exp, 1)
            then(nc.vector.tensor_scalar(gap[:, :], gate[:, 1, :], 1.0, None, ALU.add))
            then(nc.vector.reciprocal(gate[:, 0, :], gap[:, :]))
            then(nc.vector.tensor_tensor(gate[:, 1, :], gate[:, 1, :], gate[:, 0, :], ALU.mult))
            dve.wait_ge(ranked, 1)
            then(nc.vector.tensor_copy(total[:, :, :], total_ps[:, 0:P].rearrange("p (t e) -> p e t", e=E)))
            then(nc.vector.tensor_tensor_scan(upto[:, :, :].rearrange("p e t -> p (e t)"), restart[:, :],
                                              total[:, :, :].rearrange("p e t -> p (e t)"), 0.0, ALU.mult, ALU.add))
            then(nc.vector.tensor_tensor(over[:, :, :], upto[:, :, NT - 1:NT].to_broadcast([P, E, NT]),
                                         floors[:, :].rearrange("p (e t) -> p e t", e=E), ALU.is_gt))
            then(nc.vector.tensor_reduce(n_tiles[:, :], over[:, :, :], AX.X, ALU.add))
            then(nc.vector.tensor_tensor_scan(end_tile[:, :], ones[:, 0:E], n_tiles[:, :], 0.0, ALU.mult, ALU.add))
            then(nc.vector.tensor_tensor(base[:, :], end_tile[:, :], n_tiles[:, :], ALU.subtract))
            then(nc.vector.tensor_scalar(base[:, :], base[:, :], float(P), None, ALU.mult))
            then(nc.vector.tensor_tensor(slot_of[:, :, :], upto[:, :, :], total[:, :, :], ALU.subtract))
            then(nc.vector.tensor_tensor(slot_of[:, :, :], slot_of[:, :, :],
                                         base[:, :].unsqueeze(2).to_broadcast([P, E, NT]), ALU.add))
            then(nc.vector.tensor_tensor(slot_of[:, :, :], rank_ps[:, 0:P].rearrange("p (t e) -> p e t", e=E),
                                         slot_of[:, :, :], ALU.add))
            for j in range(2):
                then(nc.vector.tensor_tensor(pick[:, :, :], taken[j][:, :, :],
                                             slot_of[:, :, :].rearrange("p e t -> p t e"), ALU.mult))
                then(nc.vector.tensor_reduce(slot_f[:, j, :], pick[:, :, :], AX.X, ALU.add))
            nc.vector.tensor_copy(slot[:, :, :], slot_f[:, :, :]).then_inc(slots_known, 1)
            nc.vector.tensor_copy(end_i[:, :], end_tile[:, :]).then_inc(slots_known, 1)
            then(nc.vector.tensor_tensor(past[:, :, :], tiles[:, :].rearrange("p (k e) -> p k e", e=E),
                                         end_tile[:, :].unsqueeze(1).to_broadcast([P, SLOT_TILES, E]), ALU.is_ge))
            then(nc.vector.tensor_reduce(owner_f[:, :], past[:, :, :], AX.X, ALU.add))
            nc.vector.tensor_scalar(owner[:, 0:SLOT_TILES], owner_f[:, :], float(E - 1), None, ALU.min)\
                .then_inc(slots_known, 1)

            def split_x(b, count):
                dve.wait_ge(xt_rounded, count)
                nc.vector.tensor_tensor(xt_lo[:, b, :], xt_ps[b][:, :], xt_hi[:, b, :], ALU.subtract)\
                    .then_inc(xt_ready, 1)

            def square(b, count):
                dve.wait_ge(relu_done, count)
                nc.vector.tensor_tensor(hid[:, b, :], relu[:, :], relu[:, :], ALU.mult).then_inc(hid_ready, 1)

            split_x(0, 1)
            square(0, 1)
            split_x(1, 2)
            with dve.Fori(0, pairs) as pair:
                for b in range(2):
                    k = pair * 2 + b
                    dve.wait_ge(ht_rounded, k + 1)
                    nc.vector.tensor_tensor(ht_lo[:, b, :], ht_ps[b][:, :], ht_hi[:, b, :], ALU.subtract)\
                        .then_inc(ht_ready, 1)
                    split_x(b, k + 3)
                    square(1 - b, k + 2)
            for t in range(NT):
                b = t % 2
                dve.wait_ge(gathered[t % GB], 32 * (t // GB + 1))
                nc.vector.scalar_tensor_tensor(acc[:, :], got[0][:, t % GB, :], gate[:, 0, t:t + 1],
                                               x1[:, t + 1, :], ALU.mult, ALU.add).then_inc(acc_done, 1)
                dve.wait_ge(acc_done, t + 1)
                nc.vector.scalar_tensor_tensor(res[:, :], got[1][:, t % GB, :], gate[:, 1, t:t + 1],
                                               acc[:, :], ALU.mult, ALU.add).then_inc(summed, 1)
                dve.wait_ge(summed, t + 1)
                nc.vector.bn_stats(stats[:, :], res[:, :]).then_inc(stats_done, 1)
                dve.wait_ge(stats_done, t + 1)
                nc.vector.bn_aggr(mean_var[:, :], stats[:, :]).then_inc(var_ready, 1)
                dve.wait_ge(rstd_ready, t + 1)
                if t >= 2:
                    dve.wait_ge(fin_stored[b], 16 * (t // 2))
                nc.vector.tensor_scalar(fin[:, b, :], res[:, :], mean_var[:, 0:1], rstd[:, 0:1],
                                        ALU.subtract, ALU.mult).then_inc(fin_ready, 1)

        @block.tensor
        def _(pe):
            pe.wait_ge(const_loaded, 96)
            pe.wait_ge(set_up, 4)
            pe.wait_ge(masks_ready, 1)
            flat = both[:, :, :].rearrange("p t e -> p (t e)")
            nc.tensor.matmul(rank_ps[:, 0:P], before[:, :], flat, start=True, stop=True)
            nc.tensor.matmul(total_ps[:, 0:P], ones[:, :], flat, start=True, stop=True).then_inc(ranked, 1)
            pe.wait_ge(slots_known, 3)

            def turn_x(b, loaded):
                pe.wait_ge(xs_loaded[b], loaded)
                for c in range(CT):
                    mm = nc.tensor.transpose(xt_ps[b][:, c * P:(c + 1) * P], xs[:, b, c * P:(c + 1) * P], ident[:, :])
                mm.then_inc(xs_turned, 1)

            def times(out, b, hi, lo, parity, first_tile):
                for c in range(CT):
                    for part in range(3):
                        a = (hi, hi, lo)[part][:, b, c * P:(c + 1) * P]
                        w = (w_hi, w_lo, w_hi)[part]
                        w = w[:, bass.ds(parity, 1), first_tile + c, :].rearrange("p o f -> p (o f)")
                        mm = nc.tensor.matmul(out[:, :], a, w, start=(c == part == 0), stop=(c == CT - 1 and part == 2))
                return mm

            def load_owner(k):
                return pe.value_load(owner[0:1, bass.ds(k, 1)], min_val=0, max_val=E - 1)

            def up(b, e, count):
                pe.wait_ge(xt_ready, count)
                pe.wait_ge(we_split, WT * e + WT)
                times(h_ps[b], b, xt_hi, xt_lo, e % 2, 0).then_inc(up_done, 1)

            turn_x(0, 16)
            up(0, load_owner(0), 1)
            turn_x(1, 16)
            with pe.Fori(0, pairs) as pair:
                for b in range(2):
                    k = pair * 2 + b
                    pe.wait_ge(hid_ready, k + 1)
                    for c in range(FT):
                        mm = nc.tensor.transpose(ht_ps[b][:, c * P:(c + 1) * P], hid[:, b, c * P:(c + 1) * P], ident[:, :])
                    mm.then_inc(hid_turned, 1)
                    turn_x(b, pair * 16 + 32)
                    up(1 - b, load_owner(k + 1), k + 2)
                    e = load_owner(k)
                    pe.wait_ge(ht_ready, k + 1)
                    pe.wait_ge(yo_ready, k + 1)
                    times(ye_ps[b], b, ht_hi, ht_lo, e % 2, CT).then_inc(down_done, 1)


def build(nc, a, out_d):
    y_scratch = nc.dram_tensor("y_scratch", [NHG * NT + 1, P, GW], F32).ap()
    slots_x = nc.dram_tensor("slots_x", [SLOT_TILES * P, C], F32).ap()
    slots_y = nc.dram_tensor("slots_y", [SLOT_TILES * P, C], F32).ap()
    ctx = ExitStack()
    with ctx:
        def sem(name):
            return ctx.enter_context(nc.semaphore(name))

        attention_phase(nc, sem, a["x_t"], a["Wq"], a["Wk"], a["Wv"], a["qk_w"],
                        (a["ident"], a["dist"], a["slopes"]), y_scratch, slots_x)
        x1 = ctx.enter_context(nc.sbuf_tensor("x1", [P, NT + 1, C], F32))
        logits = ctx.enter_context(nc.sbuf_tensor("logits", [P, NT + 1, E], F32))
        residual_phase(nc, sem, y_scratch, a["Wproj"], a["subln_w"], a["x"], a["ident"], a["w_router"], x1, logits)
        expert_phase(nc, sem, x1, logits, a["w_fc"], a["w_proj"],
                     tuple(a[n] for n in ("before", "experts", "floors", "restart", "tiles")),
                     a["ident"], slots_x, slots_y, out_d)


def layout(inputs):
    x = np.ascontiguousarray(inputs["L0_attn_x"]).reshape(B * T, C)
    row, col = np.arange(P)[:, None], np.arange(T)[None, :]
    dist = (T - P + row - col).astype(np.float32)
    dist[dist < 0] = MASKED
    slopes = np.array([2.0 ** (-(i + 1) / 2) for i in range(H)], np.float32)
    def rows(v):
        return np.ascontiguousarray(np.broadcast_to(np.asarray(v, np.float32).reshape(1, -1), (P, np.size(v))))
    return {
        "x_t": np.ascontiguousarray(x.reshape(NT, P, CT, P).transpose(0, 3, 2, 1)).reshape(NT, P, CT * P),
        "x": x,
        "Wq": np.ascontiguousarray(inputs["L0_attn_Wq"]), "Wk": np.ascontiguousarray(inputs["L0_attn_Wk"]),
        "Wv": np.ascontiguousarray(inputs["L0_attn_Wv"]), "Wproj": np.ascontiguousarray(inputs["L0_attn_Wproj"]),
        "qk_w": np.ascontiguousarray(np.stack([inputs["L0_attn_q_rms_w"], inputs["L0_attn_k_rms_w"]], axis=1)),
        "subln_w": np.ascontiguousarray(inputs["L0_attn_subln_w"]).reshape(D, 1),
        "w_router": np.ascontiguousarray(inputs["L0_ffn_w_router"]),
        "w_fc": np.ascontiguousarray(inputs["L0_ffn_w_fc"]), "w_proj": np.ascontiguousarray(inputs["L0_ffn_w_proj"]),
        "ident": np.eye(P, dtype=np.float32), "dist": dist, "slopes": rows(slopes),
        "before": np.triu(np.ones((P, P), np.float32), 1),
        "experts": rows(np.tile(np.arange(E), NT)),
        "floors": rows(np.tile(np.concatenate([[-1], P * np.arange(1, NT)]), E)),
        "restart": rows(np.tile(np.concatenate([[0], np.ones(NT - 1)]), E)),
        "tiles": rows(np.repeat(np.arange(SLOT_TILES), E)),
    }


def kernel(**inputs):
    from concourse import bacc
    from concourse.bass_utils import run_bass_kernel_spmd

    nc = bacc.Bacc("TRN2", target_bir_lowering=False, num_devices=1)
    arrays = layout(inputs)
    aps = {n: nc.dram_tensor(f"in_{n}", v.shape, F32, kind="ExternalInput").ap() for n, v in arrays.items()}
    out_d = nc.dram_tensor("out", [B * T, C], F32, kind="ExternalOutput").ap()
    build(nc, aps, out_d)
    result = run_bass_kernel_spmd(nc, [{f"in_{n}": v for n, v in arrays.items()}], core_ids=[0])
    return result.results[0]["out"].reshape(B, T, C)
```

```python
from contextlib import ExitStack

import numpy as np
import concourse.bass as bass
from concourse import mybir

dt = mybir.dt
F32, F32R = dt.float32, dt.float32r
ALU = mybir.AluOpType
ACT = mybir.ActivationFunctionType
AX = mybir.AxisListType

P = 128
B, T, C = 4, 512, 512
H, D = 16, 128
EPS = 1e-5
NT = B * T // P
TB = T // P
CT = C // P
HG = 4
NHG = H // HG
GW = HG * D
MASKED = 1e30
E = 8
F = 512
FT = F // P
SLOT_TILES = 2 * NT + E - 1
REGION_TILES = NT + 1
SPARE_TILE = E * REGION_TILES
WB = 24
RAW = 8
W_ROUNDS = NHG * CT


def proj_block(s):
    return (s % 3) * CT + s // 3 if s < 3 * CT else s


def expert_block(e):
    return (CT + FT) * ((e + 2) % 3)


def one(ap):
    return ap.rearrange("p o c -> p (o c)")


def rows_of(ap):
    return ap.rearrange("o p c -> (o p) c")


def attention_phase(nc, sem, x_t, w_all, qk_w, consts, y_scratch, ident, w_raw, w_hi, w_lo):
    ident_d, dist_d, slopes_d = consts
    ctx = ExitStack()
    with ctx:
        def sb(name, shape, dtype=F32):
            return ctx.enter_context(nc.sbuf_tensor(name, shape, dtype))

        dist = sb("dist", [P, T])
        slopes = sb("slopes", [P, H])
        qkw = sb("qkw", [P, 2])
        q_scale = sb("q_scale", [P, 1])
        half = sb("half", [P, HG])
        eps = sb("eps", [P, HG])
        x_raw = sb("x_raw", [P, 2, CT * P])
        x_hi = sb("x_hi", [P, 2, CT * P], F32R)
        x_lo = sb("x_lo", [P, 2, CT * P], F32R)
        kt_hi = sb("kt_hi", [P, 2, HG, T], F32R)
        kt_lo = sb("kt_lo", [P, 2, HG, T], F32R)
        vs = sb("vs", [P, 2, TB, GW])
        qt_hi = sb("qt_hi", [P, HG, P], F32R)
        qt_lo = sb("qt_lo", [P, HG, P], F32R)
        ksq = sb("ksq", [P, GW])
        qsq = sb("qsq", [P, GW])
        ysq = sb("ysq", [P, GW])
        kn = sb("kn", [P, GW])
        qn = sb("qn", [P, GW])
        yn = sb("yn", [P, 2, GW])
        bias = sb("bias", [P, HG, T])
        logit = sb("logit", [P, T])
        prob = sb("prob", [P, T])
        prob_t = sb("prob_t", [P, T])
        small = sb("small", [P, 64])
        k_ms, q_ms, y_ms = small[:, 0:4], small[:, 4:8], small[:, 8:12]
        k_me, q_me, y_me = small[:, 12:16], small[:, 16:20], small[:, 20:24]
        k_r, q_r, y_r = small[:, 24:28], small[:, 28:32], small[:, 32:36]
        least = small[:, 36:40]
        row_sum = small[:, 40:48]
        sum_eps = small[:, 48:56]

        def ps(name):
            return ctx.enter_context(nc.psum_tensor(name, [P, GW], F32))

        k_ps, q_ps, v_ps = ps("k_ps"), ps("q_ps"), ps("v_ps")
        kt_ps, qt_ps = ps("kt_ps"), ps("qt_ps")
        score_ps, prob_ps, y_ps = ps("score_ps"), ps("prob_ps"), ps("y_ps")

        const_loaded = sem("const_loaded")
        x_loaded = [sem("x_loaded0"), sem("x_loaded1")]
        w_loaded, w_first = sem("w_loaded"), [sem(f"w_first{m}") for m in range(3)]
        w_rounded, w_ready = sem("w_rounded"), sem("w_ready")
        x_rounded, x_ready = sem("x_rounded"), sem("x_ready")
        k_projected, q_projected, v_projected = sem("k_projected"), sem("q_projected"), sem("v_projected")
        k_squared, q_squared, y_squared = sem("k_squared"), sem("q_squared"), sem("y_squared")
        k_summed, q_summed, y_summed = sem("k_summed"), sem("q_summed"), sem("y_summed")
        k_biased, q_biased, y_biased = sem("k_biased"), sem("q_biased"), sem("y_biased")
        k_rstd, q_rstd, y_rstd = sem("k_rstd"), sem("q_rstd"), sem("y_rstd")
        k_normed, q_normed, y_normed = sem("k_normed"), sem("q_normed"), sem("y_normed")
        k_turned, q_turned = sem("k_turned"), sem("q_turned")
        k_rounded, q_rounded = sem("k_rounded"), sem("q_rounded")
        k_ready, q_ready, v_ready = sem("k_ready"), sem("q_ready"), sem("v_ready")
        scored, logits_ready, probs_ready = sem("scored"), sem("logits_ready"), sem("probs_ready")
        probs_turned, prob_t_ready = sem("probs_turned"), sem("prob_t_ready")
        y_done = sem("y_done")
        y_stored = [sem("y_stored0"), sem("y_stored1")]
        set_up, scale_set, biases_set = sem("set_up"), sem("scale_set"), sem("biases_set")

        block = ctx.enter_context(nc.Block())
        its = NHG * B
        RB = 3

        def w_block(group_parity, m, c):
            return group_parity * 3 * CT + m * CT + c

        def raw_block(it, m):
            return ((it + 1) % 2) * CT + m

        FIRST = ((1, 0), (0, CT), (2, 0))
        last_it = its - 1

        @block.sync
        def _(sp):
            for b in range(2):
                sp.nop(nofuse=True).then_inc(y_stored[b], 16)
            first = w_all[0:CT, :, :].rearrange("c p (m j) -> m p c j", m=3)
            for m, at in FIRST[0:2]:
                sp.dma_start(w_raw[:, at:at + CT, :], first[m]).then_inc(w_first[m], 16)
                if m == 1:
                    sp.dma_start(x_raw[:, 0, :], x_t[0]).then_inc(x_loaded[0], 16)
            sp.dma_start(ident[:, :], ident_d).then_inc(const_loaded, 16)
            sp.dma_start(qkw[:, :], qk_w).then_inc(const_loaded, 16)
            sp.dma_start(dist[:, :], dist_d).then_inc(const_loaded, 16)
            sp.dma_start(slopes[:, :], slopes_d).then_inc(const_loaded, 16)
            sp.dma_start(x_raw[:, 1, :], x_t[1]).then_inc(x_loaded[1], 16)
            sp.wait_ge(w_ready, CT)
            sp.dma_start(w_raw[:, 0:CT, :], first[2]).then_inc(w_first[2], 16)
            for n in (2, 3):
                sp.wait_ge(x_ready, n - 1)
                sp.dma_start(x_raw[:, n % 2, :], x_t[n]).then_inc(x_loaded[n % 2], 16)

            def body(it, last):
                sp.wait_ge(w_ready, it * 3 + 3 * (CT - 1) + 1)
                sp.dma_start(w_raw[:, bass.ds(raw_block(it, 0), 3), :].rearrange("p m j -> p (m j)"),
                             rows_of(w_all[bass.ds(it + CT, 1), :, :])).then_inc(w_loaded, 16)
                for i in range(TB):
                    if not last:
                        sp.wait_ge(x_ready, it * TB + i + 3)
                        sp.dma_start(x_raw[:, i % 2, :], rows_of(x_t[bass.ds((it * TB + i + 4) % NT, 1), :, :]))\
                            .then_inc(x_loaded[i % 2], 16)
                    sp.wait_ge(y_normed, it * TB + i + 1)
                    sp.dma_start(rows_of(y_scratch[bass.ds(it * TB + i, 1), :, :]),
                                 yn[:, i % 2, :]).then_inc(y_stored[i % 2], 16)

            with sp.Fori(0, last_it) as it:
                body(it, False)
            body(last_it, True)
            sp.wait_ge(y_normed, its * TB + 1)
            sp.dma_start(y_scratch[its * TB, :, :], yn[:, 0, :]).then_inc(y_stored[0], 16)
            sp.wait_ge(y_stored[0], 16 * (its * TB // 2 + 2))
            sp.wait_ge(y_stored[1], 16 * (its * TB // 2 + 1))

        @block.scalar
        def _(act):
            def square(out, src, projected, count, done):
                act.wait_ge(projected, count)
                nc.scalar.activation(out[:, :], src[:, :], ACT.Square, scale=float(D) ** -0.5).then_inc(done, 1)

            def round_x(parity, loaded):
                act.wait_ge(x_loaded[parity], loaded)
                nc.scalar.activation(x_hi[:, parity, :], x_raw[:, parity, :], ACT.Copy).then_inc(x_rounded, 1)

            def round_k(parity, i, count):
                act.wait_ge(k_turned, count)
                nc.scalar.activation(
                    kt_hi[:, bass.ds(parity, 1), :, i * P:(i + 1) * P].rearrange("p a h t -> p (a h) t"),
                    kt_ps[:, :].rearrange("p (h t) -> p h t", h=HG), ACT.Copy).then_inc(k_rounded, 1)

            def round_q(count):
                act.wait_ge(q_turned, count)
                nc.scalar.activation(qt_hi[:, :, :], qt_ps[:, :].rearrange("p (h t) -> p h t", h=HG),
                                     ACT.Copy, scale=q_scale[:, 0:1]).then_inc(q_rounded, 1)

            def keep_v(parity, i, count):
                act.wait_ge(v_projected, count)
                nc.scalar.activation(one(vs[:, bass.ds(parity, 1), i, :]), v_ps[:, :], ACT.Copy)\
                    .then_inc(v_ready, 1)

            for m, at in FIRST:
                act.wait_ge(w_first[m], 16)
                if m == 1:
                    round_x(0, 16)
                for c in range(CT):
                    if m == 2:
                        act.wait_ge(w_ready, 2 * CT)
                    nc.scalar.activation(w_hi[:, w_block(0, m, c), :], w_raw[:, at + c, :], ACT.Copy)\
                        .then_inc(w_rounded, 1)
            square(ksq, k_ps, k_projected, 1, k_squared)
            round_x(1, 16)
            square(qsq, q_ps, q_projected, 1, q_squared)
            round_k(0, 0, 1)
            act.wait_ge(scale_set, 2)
            round_q(1)
            keep_v(0, 0, 1)
            act.wait_ge(set_up, 4)
            nc.scalar.activation(sum_eps[:, 4:8], row_sum[:, 4:8], ACT.Square, scale=EPS ** 0.5)
            nc.scalar.activation(ysq[:, :], y_ps[:, :], ACT.Square, scale=float(D) ** -0.5).then_inc(y_squared, 1)

            def body(it, last):
                for i in range(TB):
                    n = it * TB + i
                    width = P * (i + 1)
                    nxt, nxt_i = (it % 2, i + 1) if i < TB - 1 else ((it + 1) % 2, 0)
                    ahead = not (last and i == TB - 1)

                    def softmax(h):
                        act.wait_ge(logits_ready, n * HG + h + 1)
                        nc.scalar.activation(prob[:, 0:width], logit[:, 0:width], ACT.Exp, scale=-1.0,
                                             bias=least[:, h:h + 1],
                                             accum_out=row_sum[:, (i % 2) * HG + h:(i % 2) * HG + h + 1])\
                            .then_inc(probs_ready, 1)

                    def keep_prob_t(h):
                        act.wait_ge(probs_turned, n * HG + h + 1)
                        nc.scalar.activation(prob_t[:, 0:width], prob_ps[:, 0:width], ACT.Copy)\
                            .then_inc(prob_t_ready, 1)

                    softmax(0)
                    if ahead:
                        square(ksq, k_ps, k_projected, n + 2, k_squared)
                    keep_prob_t(0)
                    if not (last and i >= 2):
                        round_x(i % 2, it * 32 + 16 * (i // 2 + 2))
                    softmax(1)
                    if ahead:
                        square(qsq, q_ps, q_projected, n + 2, q_squared)
                    keep_prob_t(1)
                    if i < 3:
                        act.wait_ge(w_loaded, it * 16 + 16)
                        nc.scalar.activation(
                            one(w_hi[:, bass.ds(w_block((it // CT + 1) % 2, i, it % CT), 1), :]),
                            one(w_raw[:, bass.ds(raw_block(it, i), 1), :]), ACT.Copy).then_inc(w_rounded, 1)
                    softmax(2)
                    if ahead:
                        round_k(nxt, nxt_i, n + 2)
                    keep_prob_t(2)
                    softmax(3)
                    if ahead:
                        round_q(n + 2)
                    keep_prob_t(3)
                    if ahead:
                        keep_v(nxt, nxt_i, n + 2)
                    half_ = slice((i % 2) * HG, (i % 2 + 1) * HG)
                    act.wait_ge(probs_ready, n * HG + HG)
                    nc.scalar.activation(sum_eps[:, half_], row_sum[:, half_], ACT.Square, scale=EPS ** 0.5)
                    square(ysq, y_ps, y_done, n + 1, y_squared)

            with act.Fori(0, last_it) as it:
                body(it, False)
            body(last_it, True)

        @block.gpsimd
        def _(pool):
            def rstd(ms, me, r, summed, biased, ready, count, add):
                pool.wait_ge(summed, count)
                nc.gpsimd.tensor_tensor(me, ms, add, ALU.add).then_inc(biased, 1)
                pool.wait_ge(biased, count)
                nc.gpsimd.tensor_tensor(r, me, half[:, :], ALU.pow).then_inc(ready, 1)

            def rstd_y(parity, count):
                rstd(y_ms, y_me, y_r, y_summed, y_biased, y_rstd, count, sum_eps[:, parity * HG:(parity + 1) * HG])

            def rstd_kq(count):
                rstd(k_ms, k_me, k_r, k_summed, k_biased, k_rstd, count, eps[:, :])
                rstd(q_ms, q_me, q_r, q_summed, q_biased, q_rstd, count, eps[:, :])

            def body(it, last):
                for i in range(TB):
                    rstd_y((i + 1) % 2, it * TB + i + 1)
                    if not (last and i == TB - 1):
                        rstd_kq(it * TB + i + 2)

            pool.wait_ge(set_up, 4)
            rstd_kq(1)
            with pool.Fori(0, last_it) as it:
                body(it, False)
            body(last_it, True)
            rstd_y(1, its * TB + 1)

        @block.vector
        def _(dve):
            def heads(ap):
                return ap.rearrange("p (h d) -> p h d", h=HG)

            def row_means(sq, ms, squared, count, done):
                dve.wait_ge(squared, count)
                nc.vector.tensor_reduce(ms, heads(sq[:, :]), AX.X, ALU.add).then_inc(done, 1)

            def normalise(out, src, r, ready, count, done):
                dve.wait_ge(ready, count)
                nc.vector.tensor_tensor(heads(out), heads(src[:, :]),
                                        r.unsqueeze(2).to_broadcast([P, HG, D]), ALU.mult).then_inc(done, 1)

            def split_x(parity, count):
                dve.wait_ge(x_rounded, count)
                nc.vector.tensor_tensor(x_lo[:, parity, :], x_raw[:, parity, :], x_hi[:, parity, :],
                                        ALU.subtract).then_inc(x_ready, 1)

            def split_q(count):
                dve.wait_ge(q_rounded, count)
                nc.vector.scalar_tensor_tensor(qt_lo[:, :, :].rearrange("p h t -> p (h t)"), qt_ps[:, :], q_scale[:, 0:1],
                                               qt_hi[:, :, :].rearrange("p h t -> p (h t)"), ALU.mult, ALU.subtract)\
                    .then_inc(q_ready, 1)

            def split_k(parity, i, count):
                dve.wait_ge(k_rounded, count)
                hi, lo = (t[:, bass.ds(parity, 1), :, i * P:(i + 1) * P].rearrange("p a h t -> p (a h) t")
                          for t in (kt_hi, kt_lo))
                nc.vector.tensor_tensor(lo, kt_ps[:, :].rearrange("p (h t) -> p h t", h=HG), hi, ALU.subtract)\
                    .then_inc(k_ready, 1)

            nc.vector.memset(half[:, :], -0.5).then_inc(set_up, 1)
            nc.vector.memset(eps[:, :], EPS).then_inc(set_up, 1)
            nc.vector.memset(y_ps[:, :], 0.0).then_inc(set_up, 1)
            nc.vector.memset(row_sum, 1.0).then_inc(set_up, 1)
            for s, (m, at) in enumerate(FIRST):
                if m == 1:
                    split_x(0, 1)
                for c in range(CT):
                    dve.wait_ge(w_rounded, s * CT + c + 1)
                    blk = w_block(0, m, c)
                    nc.vector.tensor_tensor(w_lo[:, blk, :], w_raw[:, at + c, :], w_hi[:, blk, :],
                                            ALU.subtract).then_inc(w_ready, 1)
            dve.wait_ge(const_loaded, 64)
            nc.vector.tensor_tensor(q_scale[:, :], qkw[:, 0:1], qkw[:, 1:2], ALU.mult).then_inc(scale_set, 1)
            dve.wait_ge(scale_set, 1)
            nc.vector.tensor_scalar(q_scale[:, :], q_scale[:, :], -float(D) ** -0.5, None, ALU.mult)\
                .then_inc(scale_set, 1)
            row_means(ksq, k_ms, k_squared, 1, k_summed)
            split_x(1, 2)
            row_means(qsq, q_ms, q_squared, 1, q_summed)
            normalise(kn[:, :], k_ps, k_r, k_rstd, 1, k_normed)
            normalise(qn[:, :], q_ps, q_r, q_rstd, 1, q_normed)
            split_k(0, 0, 1)
            dve.wait_ge(scale_set, 2)
            split_q(1)

            def set_biases(hg):
                for h in range(HG):
                    nc.vector.tensor_scalar(bias[:, h, :], dist[:, :], slopes[:, bass.ds(hg * HG + h, 1)], None,
                                            ALU.mult).then_inc(biases_set, 1)
                dve.wait_ge(biases_set, hg * HG + HG)
                dve.nop(nofuse=True)

            def body(hg, b, last):
                it = hg * B + b
                for i in range(TB):
                    n = it * TB + i
                    width = P * (i + 1)
                    nxt, nxt_i = (it % 2, i + 1) if i < TB - 1 else ((it + 1) % 2, 0)
                    ahead = not (last and i == TB - 1)

                    def logits(h):
                        dve.wait_ge(scored, n * HG + h + 1)
                        dve.nop(nofuse=True)
                        nc.vector.tensor_tensor_reduce(
                            out=logit[:, 0:width], in0=score_ps[:, 0:width],
                            in1=bias[:, h, T - width:T], scale=1.0, scalar=3e38,
                            op0=ALU.add, op1=ALU.min, accum_out=least[:, h:h + 1]).then_inc(logits_ready, 1)

                    logits(0)
                    row_means(ysq, y_ms, y_squared, n + 1, y_summed)
                    dve.wait_ge(y_stored[i % 2], it * 32 + 16 * (i // 2 + 1))
                    normalise(yn[:, i % 2, :], y_ps, y_r, y_rstd, n + 1, y_normed)
                    if ahead:
                        row_means(ksq, k_ms, k_squared, n + 2, k_summed)
                    logits(1)
                    if ahead:
                        normalise(kn[:, :], k_ps, k_r, k_rstd, n + 2, k_normed)
                    if not (last and i >= 2):
                        split_x(i % 2, n + 3)
                    if ahead:
                        row_means(qsq, q_ms, q_squared, n + 2, q_summed)
                    logits(2)
                    if ahead:
                        normalise(qn[:, :], q_ps, q_r, q_rstd, n + 2, q_normed)
                        split_k(nxt, nxt_i, n + 2)
                    logits(3)
                    if ahead:
                        split_q(n + 2)
                    if i < 3:
                        dve.wait_ge(w_rounded, it * 3 + 3 * CT + i + 1)
                        blk = w_block((hg + 1) % 2, i, b)
                        nc.vector.tensor_tensor(
                            one(w_lo[:, bass.ds(blk, 1), :]), one(w_raw[:, bass.ds(raw_block(it, i), 1), :]),
                            one(w_hi[:, bass.ds(blk, 1), :]), ALU.subtract).then_inc(w_ready, 1)

            with dve.Fori(0, NHG - 1) as hg:
                set_biases(hg)
                with dve.Fori(0, B) as b:
                    body(hg, b, False)
            set_biases(NHG - 1)
            with dve.Fori(0, B - 1) as b:
                body(NHG - 1, b, False)
            body(NHG - 1, B - 1, True)
            row_means(ysq, y_ms, y_squared, its * TB + 1, y_summed)
            dve.wait_ge(y_stored[0], 16 * (its * TB // 2 + 1))
            normalise(yn[:, 0, :], y_ps, y_r, y_rstd, its * TB + 1, y_normed)

        @block.tensor
        def _(pe):
            def project(out, m, x_buf, parity, first=0, last=3 * CT):
                for s in range(first, last):
                    c, part = divmod(s, 3)
                    xs = (x_hi, x_hi, x_lo)[part][:, x_buf, c * P:(c + 1) * P]
                    ws = one((w_hi, w_lo, w_hi)[part][:, bass.ds(w_block(parity, m, c), 1), :])
                    mm = nc.tensor.matmul(out[:, :], xs, ws, start=(s == 0), stop=(s == 3 * CT - 1))
                return mm

            def turn(out, src, done):
                for h in range(HG):
                    mm = nc.tensor.transpose(out[:, h * P:(h + 1) * P], src[:, h * D:(h + 1) * D], ident[:, :])
                mm.then_inc(done, 1)

            pe.wait_ge(set_up, 4)
            pe.wait_ge(x_ready, 1)
            for s, ((m, _at), out, done) in enumerate(zip(FIRST, (k_ps, q_ps, v_ps),
                                                          (k_projected, q_projected, v_projected))):
                for c in range(CT):
                    pe.wait_ge(w_ready, s * CT + c + 1)
                    mm = project(out, m, 0, 0, 3 * c, 3 * c + 3)
                mm.then_inc(done, 1)
            pe.wait_ge(const_loaded, 64)
            pe.wait_ge(k_normed, 1)
            turn(kt_ps, kn, k_turned)
            pe.wait_ge(q_normed, 1)
            turn(qt_ps, qn, q_turned)

            def body(it, last):
                for i in range(TB):
                    n = it * TB + i
                    now = it % 2
                    xb = (i + 1) % 2
                    wp = (it // B) % 2 if i < TB - 1 else ((it + 1) // B) % 2
                    width = P * (i + 1)
                    ahead = not (last and i == TB - 1)

                    def score(h):
                        for part in range(3):
                            qs = (qt_hi, qt_hi, qt_lo)[part][:, h, :]
                            ks = (kt_hi, kt_lo, kt_hi)[part]
                            keys = ks[:, bass.ds(now, 1), h, 0:width]
                            keys = keys.to_broadcast([P, 2, P]) if i == 0 else one(keys)
                            mm = nc.tensor.matmul(score_ps[:, 0:max(width, 2 * P)], qs, keys,
                                                  start=(part == 0), stop=(part == 2))
                        mm.then_inc(scored, 1)

                    def turn_probs(h):
                        pe.wait_ge(probs_ready, n * HG + h + 1)
                        for j in range(i + 1):
                            mm = nc.tensor.transpose(prob_ps[:, j * P:(j + 1) * P], prob[:, j * P:(j + 1) * P],
                                                     ident[:, :])
                        mm.then_inc(probs_turned, 1)

                    def attend(h):
                        pe.wait_ge(prob_t_ready, n * HG + h + 1)
                        for j in range(i + 1):
                            mm = nc.tensor.matmul(
                                y_ps[:, h * D:(h + 1) * D], prob_t[:, j * P:(j + 1) * P],
                                one(vs[:, bass.ds(now, 1), j, h * D:(h + 1) * D]),
                                start=(j == 0), stop=(j == i))
                        return mm

                    pe.wait_ge(k_ready, n + 1)
                    pe.wait_ge(q_ready, n + 1)
                    score(0)
                    if ahead:
                        pe.wait_ge(x_ready, n + 2)
                        if i == TB - 1:
                            pe.wait_ge(w_ready, it * 3 + (CT + 1) * 3)
                        project(k_ps, 1, xb, wp).then_inc(k_projected, 1)
                    turn_probs(0)
                    score(1)
                    if ahead:
                        project(q_ps, 0, xb, wp).then_inc(q_projected, 1)
                    pe.wait_ge(v_ready, n + 1)
                    pe.wait_ge(y_normed, n + 1)
                    attend(0)
                    turn_probs(1)
                    score(2)
                    if ahead:
                        pe.wait_ge(k_normed, n + 2)
                        turn(kt_ps, kn, k_turned)
                        project(v_ps, 2, xb, wp, 0, 4)
                    attend(1)
                    turn_probs(2)
                    score(3)
                    if ahead:
                        project(v_ps, 2, xb, wp, 4, 8)
                        pe.wait_ge(q_normed, n + 2)
                        turn(qt_ps, qn, q_turned)
                    attend(2)
                    turn_probs(3)
                    if ahead:
                        project(v_ps, 2, xb, wp, 8, 12).then_inc(v_projected, 1)
                    attend(3).then_inc(y_done, 1)

            with pe.Fori(0, last_it) as it:
                body(it, False)
            body(last_it, True)


def token_steps(engine, step):
    for s in (0, 1):
        step(s, s, 0)
    with engine.Fori(1, NT // 2 - 1) as half:
        for b in range(2):
            step(half * 2 + b, b, half)
    for s in (NT - 2, NT - 1):
        step(s, s % 2, s // 2)


def before_step(s, limit):
    return isinstance(s, int) and s < limit


def residual_phase(nc, sem, y_scratch, w_all, w_last, subln_w, x_d, w_router, route_consts, w_experts,
                   slots_x, shared):
    ident, w_raw, w_hi, w_lo, x1, x1_now, gap, slot, slot_now, run, we_split, dispatched = shared
    ctx = ExitStack()
    with ctx:
        def sb(name, shape, dtype=F32):
            return ctx.enter_context(nc.sbuf_tensor(name, shape, dtype))

        subln = sb("subln", [P, 1])
        w_r = sb("w_r", [P, CT, E])
        before = sb("before", [P, P])
        experts = sb("experts", [P, E])
        y_raw = sb("y_raw", [P, 2, NHG, GW])
        yt_hi = sb("yt_hi", [P, NHG, GW], F32R)
        yt_lo = sb("yt_lo", [P, NHG, GW], F32R)
        x_nat = sb("x_nat", [P, 2, C])
        res = sb("res", [P, C])
        stats = sb("stats", [P, 6])
        mean_var = sb("mean_var", [P, 2])
        var_eps = sb("var_eps", [P, 1])
        rstd = sb("rstd", [P, 1])
        half = sb("half2", [P, 1])
        eps = sb("eps2", [P, 1])
        x1_t = sb("x1_t", [P, C])
        ones = sb("ones", [P, P])
        logits = sb("logits", [P, E])
        best = sb("best", [P, 8])
        best_at = sb("best_at", [P, 8], dt.uint32)
        choice = sb("choice", [P, 2])
        taken = sb("taken", [P, 2, E])
        both = sb("both", [P, E])
        next_slot = sb("next_slot", [P, E])
        pick = sb("pick", [P, 2, E])
        slot_f = sb("slot_f", [P, 2])

        def ps(name):
            return ctx.enter_context(nc.psum_tensor(name, [P, C], F32))

        turn_ps = [ps(f"turn_ps{g}") for g in range(NHG)]
        out_ps = [ps("out_ps0"), ps("out_ps1")]
        x1_ps, router_ps = ps("x1_ps"), ps("router_ps")
        rank_ps, total_ps = router_ps[:, E:2 * E], router_ps[:, 2 * E:3 * E]

        subln_loaded, const_loaded = sem("subln_loaded"), sem("p_const_loaded")
        wp_loaded, wp_rounded, wp_ready = sem("wp_loaded"), sem("wp_rounded"), sem("wp_ready")
        y_loaded = [sem("y_loaded0"), sem("y_loaded1")]
        x_loaded = [sem("xn_loaded0"), sem("xn_loaded1")]
        set_up = sem("p_set_up")
        y_turned, yt_rounded, yt_ready = sem("y_turned"), sem("yt_rounded"), sem("yt_ready")
        projected, summed, stats_done = sem("projected"), sem("res_summed"), sem("stats_done")
        var_ready, var_biased, rstd_ready = sem("var_ready"), sem("var_biased"), sem("rstd_ready")
        x1_ready, x1_turned, x1_t_ready = sem("x1_ready"), sem("x1_turned"), sem("x1_t_ready")
        x1_kept = sem("x1_kept")
        routed, logits_kept, best_found = sem("routed"), sem("logits_kept"), sem("best_found")
        best_placed, chosen, taken_set = sem("best_placed"), sem("chosen"), sem("taken_set")
        both_ready, ranked, run_ready = sem("both_ready"), sem("ranked"), sem("run_ready")
        next_ready, picked, slot_summed = sem("next_ready"), sem("picked"), sem("slot_summed")
        slots_ready, we_loaded = sem("slots_ready"), sem("we0_loaded")
        block = ctx.enter_context(nc.Block())

        y_tiles = y_scratch[1:1 + NHG * NT, :, :].rearrange("(g t) p c -> t p g c", g=NHG)
        x_tiles = x_d.rearrange("(t p) c -> t p c", p=P)
        LAST = NHG - 1

        def tile_of(tiles, t):
            return tiles[t] if isinstance(t, int) else rows_of(tiles[bass.ds(t, 1), :, :])

        @block.sync
        def _(sp):
            def load_y(t, b):
                src = y_tiles[t] if isinstance(t, int) else \
                    y_tiles[bass.ds(t, 1), :, :, :].rearrange("o p g c -> (o p) g c")
                sp.dma_start(y_raw[:, b, :, :], src).then_inc(y_loaded[b], 16)

            def load_x(t, b):
                sp.dma_start(x_nat[:, b, :], tile_of(x_tiles, t)).then_inc(x_loaded[b], 16)

            load_y(0, 0)
            sp.dma_start(w_raw[:, CT:2 * CT, :], w_last).then_inc(wp_loaded, 16)
            load_y(1, 1)
            load_x(0, 0)
            load_x(1, 1)

            def step(s, b, h):
                if before_step(s, NT - 2) or not isinstance(s, int):
                    sp.wait_ge(y_turned, s * NHG + NHG)
                    load_y(s + 2, b)
                if not before_step(s, 1) and not (isinstance(s, int) and s == NT - 1):
                    sp.wait_ge(summed, s)
                    sp.nop(nofuse=True)
                    load_x(s + 1, 1 - b)

            token_steps(sp, step)

        @block.scalar
        def _(act):
            def round_y(g, count):
                act.wait_ge(y_turned, count)
                nc.scalar.activation(yt_hi[:, g, :], turn_ps[g][:, :], ACT.Copy, scale=subln[:, 0:1])\
                    .then_inc(yt_rounded, 1)

            def keep_x1(t, b):
                act.wait_ge(x1_turned, t + 1)
                nc.scalar.activation(x1_t[:, :], x1_ps[:, :], ACT.Copy).then_inc(x1_t_ready, 1)
                out = x1[:, t, :] if isinstance(t, int) else one(x1[:, bass.ds(t, 1), :])
                nc.scalar.activation(out, x1_now[:, b, :], ACT.Copy).then_inc(x1_kept, 1)

            act.dma_start(subln[:, :], subln_w).then_inc(subln_loaded, 16)
            act.dma_start(w_r[:, :, :], w_router.rearrange("(c p) e -> p c e", p=P)).then_inc(const_loaded, 16)
            for dst, src in zip((before, experts, run), route_consts):
                act.dma_start(dst[:, :], src).then_inc(const_loaded, 16)
            act.wait_ge(subln_loaded, 16)
            for g in range(NHG):
                round_y(g, g + 1)
            act.wait_ge(wp_loaded, 16)
            for h in range(HG):
                nc.scalar.activation(w_hi[:, proj_block(LAST * HG + h), :], w_raw[:, CT + h, :], ACT.Copy)\
                    .then_inc(wp_rounded, 1)

            def step(s, b, h):
                for g in range(NHG):
                    if not (isinstance(s, int) and s == NT - 1):
                        round_y(g, s * NHG + NHG + g + 1)
                    if g == 1 and not before_step(s, 1):
                        keep_x1(s - 1, 1 - b)

            token_steps(act, step)
            keep_x1(NT - 1, 1)

        @block.gpsimd
        def _(pool):
            first = expert_block(0)
            for m in range(2):
                part = slice(first + m * CT, first + (m + 1) * CT)
                src = w_experts[0, :, m * CT * F:(m + 1) * CT * F].rearrange("p (c f) -> p c f", c=CT)
                if m == 1:
                    pool.wait_ge(wp_ready, HG)
                pool.dma_start(w_hi[:, part, :], src).then_inc(we_loaded, 16)
                pool.dma_start(w_raw[:, m * CT:(m + 1) * CT, :], src).then_inc(we_loaded, 16)
                pool.wait_ge(we_loaded, 32 * m + 32)
                for c in range(CT):
                    blk = first + m * CT + c
                    nc.gpsimd.tensor_tensor(w_lo[:, blk, :], w_raw[:, m * CT + c, :], w_hi[:, blk, :],
                                            ALU.subtract).then_inc(we_split, 1)

            def inverse_std(t):
                pool.wait_ge(var_ready, t + 1)
                nc.gpsimd.tensor_tensor(var_eps[:, :], mean_var[:, 1:2], eps[:, :], ALU.add).then_inc(var_biased, 1)
                pool.wait_ge(var_biased, t + 1)
                nc.gpsimd.tensor_tensor(rstd[:, :], var_eps[:, :], half[:, :], ALU.pow).then_inc(rstd_ready, 1)

            def dispatch(t, b):
                pool.wait_ge(slots_ready, t + 1)
                pool.nop(nofuse=True)
                for j in range(2):
                    pool.indirect_dma_start(slots_x, bass.IndirectOffsetOnAxis(ap=slot_now[:, b, j:j + 1], axis=0),
                                            x1_now[:, b, :], None).then_inc(dispatched[b], 16)

            def step(s, b, h):
                if not before_step(s, 1):
                    inverse_std(s - 1)
                if not before_step(s, 2):
                    dispatch(s - 2, b)

            pool.wait_ge(set_up, 3)
            token_steps(pool, step)
            inverse_std(NT - 1)
            dispatch(NT - 2, 0)
            dispatch(NT - 1, 1)

        @block.vector
        def _(dve):
            def split_y(g, count):
                dve.wait_ge(yt_rounded, count)
                nc.vector.scalar_tensor_tensor(yt_lo[:, g, :], turn_ps[g][:, :], subln[:, 0:1],
                                               yt_hi[:, g, :], ALU.mult, ALU.subtract).then_inc(yt_ready, 1)

            def add_residual(t, b, loaded):
                dve.wait_ge(projected, t + 1)
                dve.wait_ge(x_loaded[b], loaded)
                nc.vector.tensor_tensor(res[:, :], out_ps[b][:, :], x_nat[:, b, :], ALU.add).then_inc(summed, 1)
                dve.wait_ge(summed, t + 1)
                nc.vector.bn_stats(stats[:, :], res[:, :]).then_inc(stats_done, 1)
                dve.wait_ge(stats_done, t + 1)
                dve.nop(nofuse=True)
                nc.vector.bn_aggr(mean_var[:, :], stats[:, :]).then_inc(var_ready, 1)

            def layernorm(t, b, sent):
                dve.wait_ge(rstd_ready, t + 1)
                if sent is not None:
                    dve.wait_ge(x1_kept, t - 1)
                    dve.wait_ge(dispatched[b], sent)
                nc.vector.tensor_scalar(x1_now[:, b, :], res[:, :], mean_var[:, 0:1], rstd[:, 0:1],
                                        ALU.subtract, ALU.mult).then_inc(x1_ready, 1)

            def choose(t):
                dve.wait_ge(routed, t + 1)
                nc.vector.tensor_copy(logits[:, :], router_ps[:, 0:E]).then_inc(logits_kept, 1)
                dve.wait_ge(logits_kept, t + 1)
                dve.nop(nofuse=True)
                nc.vector.max(best[:, :], logits[:, :]).then_inc(best_found, 1)
                dve.wait_ge(best_found, t + 1)
                dve.nop(nofuse=True)
                nc.vector.max_index(best_at[:, :], best[:, :], logits[:, :]).then_inc(best_placed, 1)
                out = gap[:, t:t + 1] if isinstance(t, int) else gap[:, bass.ds(t, 1)]
                nc.vector.tensor_tensor(out, best[:, 1:2], best[:, 0:1], ALU.subtract)
                dve.wait_ge(best_placed, t + 1)
                nc.vector.tensor_copy(choice[:, :], best_at[:, 0:2]).then_inc(chosen, 1)
                dve.wait_ge(chosen, t + 1)
                nc.vector.tensor_tensor(taken[:, :, :], experts[:, :].unsqueeze(1).to_broadcast([P, 2, E]),
                                        choice[:, :].unsqueeze(2).to_broadcast([P, 2, E]), ALU.is_equal)\
                    .then_inc(taken_set, 1)
                dve.wait_ge(taken_set, t + 1)
                nc.vector.tensor_tensor(both[:, :], taken[:, 0, :], taken[:, 1, :], ALU.add).then_inc(both_ready, 1)

            def place(t, b):
                dve.wait_ge(ranked, t + 1)
                dve.wait_ge(run_ready, t + 1)
                nc.vector.tensor_tensor(next_slot[:, :], rank_ps, run[:, :], ALU.add).then_inc(next_ready, 1)
                nc.vector.tensor_tensor(run[:, :], total_ps, run[:, :], ALU.add).then_inc(run_ready, 1)
                dve.wait_ge(next_ready, t + 1)
                nc.vector.tensor_tensor(pick[:, :, :], taken[:, :, :],
                                        next_slot[:, :].unsqueeze(1).to_broadcast([P, 2, E]), ALU.mult)\
                    .then_inc(picked, 1)
                dve.wait_ge(picked, t + 1)
                nc.vector.tensor_reduce(slot_f[:, :], pick[:, :, :], AX.X, ALU.add).then_inc(slot_summed, 1)
                dve.wait_ge(slot_summed, t + 1)
                nc.vector.tensor_copy(slot_now[:, b, :], slot_f[:, :]).then_inc(slots_ready, 1)
                out = slot[:, t, :] if isinstance(t, int) else one(slot[:, bass.ds(t, 1), :])
                nc.vector.tensor_copy(out, slot_f[:, :])

            nc.vector.memset(half[:, :], -0.5).then_inc(set_up, 1)
            nc.vector.memset(eps[:, :], EPS).then_inc(set_up, 1)
            nc.vector.memset(ones[:, :], 1.0).then_inc(set_up, 1)
            dve.wait_ge(subln_loaded, 16)
            for g in range(NHG):
                split_y(g, g + 1)
            for h in range(HG):
                dve.wait_ge(wp_rounded, h + 1)
                blk = proj_block(LAST * HG + h)
                nc.vector.tensor_tensor(w_lo[:, blk, :], w_raw[:, CT + h, :], w_hi[:, blk, :],
                                        ALU.subtract).then_inc(wp_ready, 1)
            dve.wait_ge(const_loaded, 64)
            dve.nop(nofuse=True).then_inc(run_ready, 1)

            def step(s, b, h):
                turning = not (isinstance(s, int) and s == NT - 1)
                if not before_step(s, 1):
                    add_residual(s - 1, 1 - b, 16 * h + 16 * b)
                if not before_step(s, 2):
                    place(s - 2, b)
                if turning:
                    split_y(0, s * NHG + NHG + 1)
                if not before_step(s, 1):
                    layernorm(s - 1, 1 - b, None if before_step(s, 3) else 32 * h - 32 + 32 * b)
                if turning:
                    split_y(1, s * NHG + NHG + 2)
                    split_y(2, s * NHG + NHG + 3)
                if not before_step(s, 1):
                    choose(s - 1)
                if turning:
                    split_y(3, s * NHG + NHG + 4)

            token_steps(dve, step)
            add_residual(NT - 1, 1, 16 * (NT // 2))
            place(NT - 2, 0)
            layernorm(NT - 1, 1, 32 * (NT // 2 - 1))
            choose(NT - 1)
            place(NT - 1, 1)

        @block.tensor
        def _(pe):
            def turn_y(buf, g):
                for h in range(HG):
                    mm = nc.tensor.transpose(turn_ps[g][:, h * P:(h + 1) * P],
                                             y_raw[:, buf, g, h * P:(h + 1) * P], ident[:, :])
                mm.then_inc(y_turned, 1)

            def project(b, g):
                for h in range(HG):
                    for part in range(3):
                        ys = (yt_hi, yt_hi, yt_lo)[part][:, g, h * P:(h + 1) * P]
                        ws = (w_hi, w_lo, w_hi)[part][:, proj_block(g * HG + h), :]
                        mm = nc.tensor.matmul(out_ps[b][:, :], ys, ws, start=(g == h == part == 0),
                                              stop=(g == NHG - 1 and h == HG - 1 and part == 2))
                return mm

            def turn_x1(t, b):
                pe.wait_ge(x1_ready, t + 1)
                for c in range(CT):
                    mm = nc.tensor.transpose(x1_ps[:, c * P:(c + 1) * P], x1_now[:, b, c * P:(c + 1) * P], ident[:, :])
                mm.then_inc(x1_turned, 1)

            def route(t):
                pe.wait_ge(x1_t_ready, t + 1)
                for c in range(CT):
                    mm = nc.tensor.matmul(router_ps[:, 0:E], x1_t[:, c * P:(c + 1) * P], w_r[:, c, :],
                                          start=(c == 0), stop=(c == CT - 1))
                mm.then_inc(routed, 1)

            def rank(t):
                pe.wait_ge(both_ready, t + 1)
                nc.tensor.matmul(rank_ps, before[:, :], both[:, :], start=True, stop=True)
                nc.tensor.matmul(total_ps, ones[:, :], both[:, :], start=True, stop=True).then_inc(ranked, 1)

            pe.wait_ge(y_loaded[0], 16)
            for g in range(NHG):
                turn_y(0, g)

            def step(s, b, h):
                for g in range(NHG):
                    pe.wait_ge(yt_ready, s * NHG + g + 1)
                    if before_step(s, 1) and g == LAST:
                        pe.wait_ge(wp_ready, HG)
                    mm = project(b, g)
                    if g == NHG - 1:
                        mm.then_inc(projected, 1)
                    if not (isinstance(s, int) and s == NT - 1):
                        if g == 0:
                            pe.wait_ge(y_loaded[1 - b], 16 * h + 16 + 16 * b)
                        turn_y(1 - b, g)
                    if not before_step(s, 1):
                        if g == 1:
                            turn_x1(s - 1, 1 - b)
                        if g == 2:
                            if before_step(s, 2):
                                pe.wait_ge(const_loaded, 64)
                                pe.wait_ge(set_up, 3)
                            route(s - 1)
                        if g == 3:
                            rank(s - 1)

            token_steps(pe, step)
            turn_x1(NT - 1, 1)
            route(NT - 1)
            rank(NT - 1)


def expert_phase(nc, sem, w_experts, moe_consts, slots_x, slots_y, out_d, shared):
    ident, w_raw, w_hi, w_lo, x1, x1_now, gap, slot, slot_now, run, we_split, dispatched = shared
    floors_d, tiles_d = moe_consts
    ctx = ExitStack()
    with ctx:
        def sb(name, shape, dtype=F32):
            return ctx.enter_context(nc.sbuf_tensor(name, shape, dtype))

        WT = CT + FT
        floors = sb("floors", [P, E * NT])
        tiles = sb("tiles", [P, SLOT_TILES * E])
        ones = sb("ones3", [P, E])
        zeros = sb("zeros", [P, C])
        gate = sb("gate", [P, 2, NT])
        over = sb("over", [P, E, NT])
        n_tiles = sb("n_tiles", [P, E])
        end_tile = sb("end_tile", [P, E])
        past = sb("past", [P, SLOT_TILES, E])
        past_n = sb("past_n", [P, SLOT_TILES, E])
        owner_f = sb("owner_f", [P, SLOT_TILES])
        start_f = sb("start_f", [P, SLOT_TILES])
        place_f = sb("place_f", [P, SLOT_TILES])
        owner = sb("owner", [P, SLOT_TILES], dt.int32)
        from_tile = sb("from_tile", [P, SLOT_TILES], dt.int32)
        beyond = sb("beyond", [P, 2 * NT, E - 1])
        shrink = sb("shrink", [P, E - 1])
        shift = sb("shift", [P, 2 * NT])
        slot_y = sb("slot_y", [P, 2 * NT], dt.uint32)
        run_i = sb("run_i", [P, E], dt.int32)
        end_i = sb("end_i", [P, E], dt.int32)
        xs = sb("xs", [P, 2, C])
        xt_hi = sb("xt_hi", [P, 2, C], F32R)
        xt_lo = sb("xt_lo", [P, 2, C], F32R)
        relu = sb("relu", [P, F])
        hid = sb("hid", [P, 2, F])
        ht_hi = sb("ht_hi", [P, 2, F], F32R)
        ht_lo = sb("ht_lo", [P, 2, F], F32R)
        yo = sb("yo", [P, 2, C])
        GB = RAW // 2
        acc = sb("acc", [P, C])
        res = sb("res3", [P, 2, C])
        stats = sb("stats3", [P, 6])
        mean_var = sb("mean_var3", [P, 2, 2])
        var_eps = sb("var_eps3", [P, 2])
        half = sb("half3", [P, 1])
        eps = sb("eps3", [P, 1])
        rstd = sb("rstd3", [P, 2])
        fin = sb("fin", [P, 2, C])

        def ps(name):
            return ctx.enter_context(nc.psum_tensor(name, [P, C], F32))

        xt_ps, h_ps, ht_ps, ye_ps = ([ps(f"{n}{b}") for b in range(2)] for n in ("xt_ps", "h_ps", "ht_ps", "ye_ps"))

        const_loaded, zeros_set, set_up = sem("e_const_loaded"), sem("zeros_set"), sem("e_set_up")
        step = sem("table_step")
        ends_known, tiles_known = sem("ends_known"), sem("tiles_known")
        slots_known = sem("slots_known")
        gap_exp, gates_known = sem("gap_exp"), sem("gates_known")
        padded = sem("padded")
        we_loaded = sem("we_loaded")
        xs_loaded = [sem("xs_loaded0"), sem("xs_loaded1")]
        xs_turned, xt_rounded, xt_ready = sem("xs_turned"), sem("xt_rounded"), sem("xt_ready")
        up_done, relu_done, hid_ready = sem("up_done"), sem("relu_done"), sem("hid_ready")
        hid_turned, ht_rounded, ht_ready = sem("hid_turned"), sem("ht_rounded"), sem("ht_ready")
        down_done, yo_ready = sem("down_done"), sem("yo_ready")
        yo_stored = [sem("yo_stored0"), sem("yo_stored1")]
        gathered = [sem(f"gathered{b}") for b in range(GB)]
        acc_done, summed, stats_done = sem("acc_done"), sem("e_summed"), sem("e_stats_done")
        var_ready, var_biased, rstd_ready = sem("e_var_ready"), sem("e_var_biased"), sem("e_rstd_ready")
        fin_ready = sem("fin_ready")
        fin_stored = [sem("fin_stored0"), sem("fin_stored1")]
        block = ctx.enter_context(nc.Block())
        x_slots = slots_x.rearrange("(k p) c -> k p c", p=P)
        y_slots = slots_y.rearrange("(k p) c -> k p c", p=P)
        out_tiles = out_d.rearrange("(t p) c -> t p c", p=P)

        LOOPED = (SLOT_TILES - 4) // 2

        def slot_steps(engine, slot_step):
            with engine.Fori(0, LOOPED) as pair:
                for b in range(2):
                    slot_step(pair * 2 + b, b, pair)
            for k in range(2 * LOOPED, SLOT_TILES):
                slot_step(k, k % 2, k // 2)

        def more(k, ahead):
            return (k if isinstance(k, int) else 2 * LOOPED - 1) + ahead < SLOT_TILES

        @block.sync
        def _(sp):
            for b in range(2):
                sp.nop(nofuse=True).then_inc(yo_stored[b], 16)
            for dst, src in ((floors, floors_d), (tiles, tiles_d)):
                sp.dma_start(dst[:, :], src).then_inc(const_loaded, 16)
            sp.wait_ge(zeros_set, 1)
            sp.dma_start(x_slots[SPARE_TILE], zeros[:, :]).then_inc(padded, 16)
            sp.wait_ge(ends_known, 2)
            for e in range(E):
                at = sp.value_load(run_i[0:1, e:e + 1], min_val=0, max_val=(SPARE_TILE - 1) * P)
                sp.dma_start(slots_x[bass.ds(at, P), :], zeros[:, :]).then_inc(padded, 16)

            def load(k, b):
                at = sp.value_load(from_tile[0:1, k:k + 1] if isinstance(k, int) else from_tile[0:1, bass.ds(k, 1)],
                                   min_val=0, max_val=SPARE_TILE)
                return lambda: sp.dma_start(xs[:, b, :], rows_of(x_slots[bass.ds(at, 1), :, :]))\
                    .then_inc(xs_loaded[b], 16)

            sp.wait_ge(tiles_known, 2)
            for b in range(2):
                sp.wait_ge(dispatched[b], 32 * (NT // 2))
            sp.wait_ge(padded, 16 * (E + 1))
            for k in range(4):
                start = load(k, k % 2)
                if k >= 2:
                    sp.wait_ge(xs_turned, k - 1)
                start()

            def slot_step(k, b, h):
                if more(k, 4):
                    start = load(k + 4, b)
                if more(k, 4):
                    sp.wait_ge(xs_turned, k + 3)
                    sp.nop(nofuse=True)
                    start()
                sp.wait_ge(yo_ready, k + 1)
                sp.nop(nofuse=True)
                out = y_slots[k] if isinstance(k, int) else rows_of(y_slots[bass.ds(k, 1), :, :])
                sp.dma_start(out, yo[:, b, :]).then_inc(yo_stored[b], 16)

            slot_steps(sp, slot_step)
            with sp.Fori(0, NT // 2) as pair:
                for b in range(2):
                    sp.wait_ge(fin_ready, pair * 2 + b + 1)
                    sp.dma_start(rows_of(out_tiles[bass.ds(pair * 2 + b, 1), :, :]), fin[:, b, :])\
                        .then_inc(fin_stored[b], 16)
            for b in range(2):
                sp.wait_ge(fin_stored[b], 16 * (NT // 2))

        @block.gpsimd
        def _(pool):
            def load_and_split(e, end):
                blk = expert_block(e)
                src = w_experts[e] if isinstance(e, int) else rows_of(w_experts[bass.ds(e, 1), :, :])
                if end is not None:
                    pool.dma_start(w_raw[:, :, :].rearrange("p s f -> p (s f)"), src).then_inc(we_loaded, 16)
                    pool.wait_ge(down_done, end)
                    pool.nop(nofuse=True)
                hi = w_hi[:, blk:blk + WT, :] if isinstance(e, int) else w_hi[:, bass.ds(blk, WT), :]
                pool.dma_start(hi.rearrange("p s f -> p (s f)"), src).then_inc(we_loaded, 16)
                if end is None:
                    pool.dma_start(w_raw[:, :, :].rearrange("p s f -> p (s f)"), src).then_inc(we_loaded, 16)
                pool.wait_ge(we_loaded, 32 * e)
                for s in range(WT):
                    hi, lo = (w[:, blk + s, :] if isinstance(e, int) else one(w[:, bass.ds(blk + s, 1), :])
                              for w in (w_hi, w_lo))
                    nc.gpsimd.tensor_tensor(lo, w_raw[:, s, :], hi, ALU.subtract).then_inc(we_split, 1)
                pool.wait_ge(we_split, WT * e + WT)

            for e in (1, 2):
                load_and_split(e, None)
            pool.wait_ge(ends_known, 2)
            with pool.Fori(3, E) as e:
                end = pool.value_load(end_i[0:1, bass.ds(e - 3, 1)], min_val=1, max_val=SLOT_TILES)
                load_and_split(e, end)
            pool.wait_ge(yo_stored[0], 16 * ((SLOT_TILES + 1) // 2 + 1))
            pool.wait_ge(yo_stored[1], 16 * (SLOT_TILES // 2 + 1))
            pool.wait_ge(slots_known, 1)

            def gather(t):
                if t >= GB:
                    pool.wait_ge(summed, t - GB + 1)
                for j in range(2):
                    pool.indirect_dma_start(w_raw[:, t % GB * 2 + j, :], None, slots_y,
                                            bass.IndirectOffsetOnAxis(ap=slot_y[:, 2 * t + j:2 * t + j + 1], axis=0))\
                        .then_inc(gathered[t % GB], 16)

            for t in range(GB - 1):
                gather(t)
            pool.wait_ge(set_up, 2)
            for t in range(NT):
                b = t % 2
                if t + GB - 1 < NT:
                    gather(t + GB - 1)
                pool.wait_ge(var_ready, t + 1)
                nc.gpsimd.tensor_tensor(var_eps[:, b:b + 1], mean_var[:, b, 1:2], eps[:, :], ALU.add)\
                    .then_inc(var_biased, 1)
                pool.wait_ge(var_biased, t + 1)
                nc.gpsimd.tensor_tensor(rstd[:, b:b + 1], var_eps[:, b:b + 1], half[:, :], ALU.pow)\
                    .then_inc(rstd_ready, 1)

        @block.scalar
        def _(act):
            act.nop(nofuse=True).then_inc(hid_ready, 1)
            nc.scalar.activation(gate[:, 1, :], gap[:, :], ACT.Exp).then_inc(gap_exp, 1)

            def round_x(b, count):
                act.wait_ge(xs_turned, count)
                nc.scalar.activation(xt_hi[:, b, :], xt_ps[b][:, :], ACT.Copy).then_inc(xt_rounded, 1)

            def rectify(b, k):
                act.wait_ge(up_done, k + 1)
                act.wait_ge(hid_ready, k + 1)
                nc.scalar.activation(relu[:, :], h_ps[b][:, :], ACT.Relu).then_inc(relu_done, 1)

            round_x(0, 1)
            rectify(0, 0)
            round_x(1, 2)

            def slot_step(k, b, h):
                act.wait_ge(hid_turned, k + 1)
                nc.scalar.activation(ht_hi[:, b, :], ht_ps[b][:, :], ACT.Copy).then_inc(ht_rounded, 1)
                if more(k, 1):
                    rectify(1 - b, k + 1)
                if more(k, 2):
                    round_x(b, k + 3)
                act.wait_ge(down_done, k + 1)
                act.wait_ge(yo_stored[b], h * 16 + 16)
                nc.scalar.activation(yo[:, b, :], ye_ps[b][:, :], ACT.Copy).then_inc(yo_ready, 1)

            slot_steps(act, slot_step)

        @block.vector
        def _(dve):
            steps = [0]

            def then(op):
                steps[0] += 1
                op.then_inc(step, 1)
                dve.wait_ge(step, steps[0])

            nc.vector.tensor_copy(run_i[:, :], run[:, :]).then_inc(ends_known, 1)
            nc.vector.memset(zeros[:, :], 0.0).then_inc(zeros_set, 1)
            nc.vector.memset(half[:, :], -0.5).then_inc(set_up, 1)
            nc.vector.memset(eps[:, :], EPS).then_inc(set_up, 1)
            then(nc.vector.memset(ones[:, :], 1.0))
            dve.wait_ge(const_loaded, 32)
            then(nc.vector.tensor_tensor(over[:, :, :], run[:, :].unsqueeze(2).to_broadcast([P, E, NT]),
                                         floors[:, :].rearrange("p (e t) -> p e t", e=E), ALU.is_gt))
            then(nc.vector.tensor_reduce(n_tiles[:, :], over[:, :, :], AX.X, ALU.add))
            then(nc.vector.tensor_tensor_scan(end_tile[:, :], ones[:, 0:E], n_tiles[:, :], 0.0, ALU.mult, ALU.add))
            nc.vector.tensor_copy(end_i[:, :], end_tile[:, :]).then_inc(ends_known, 1)
            tile_numbers = tiles[:, :].rearrange("p (k e) -> p k e", e=E)
            then(nc.vector.tensor_tensor(past[:, :, :], tile_numbers,
                                         end_tile[:, :].unsqueeze(1).to_broadcast([P, SLOT_TILES, E]), ALU.is_ge))
            then(nc.vector.tensor_reduce(owner_f[:, :], past[:, :, :], AX.X, ALU.add))
            nc.vector.tensor_scalar(owner[:, :], owner_f[:, :], float(E - 1), None, ALU.min).then_inc(tiles_known, 1)
            then(nc.vector.tensor_tensor(past_n[:, :, :], past[:, :, :],
                                         n_tiles[:, :].unsqueeze(1).to_broadcast([P, SLOT_TILES, E]), ALU.mult))
            then(nc.vector.tensor_reduce(start_f[:, :], past_n[:, :, :], AX.X, ALU.add))
            then(nc.vector.tensor_tensor(start_f[:, :], tile_numbers[:, :, 0], start_f[:, :], ALU.subtract))
            then(nc.vector.scalar_tensor_tensor(place_f[:, :], owner_f[:, :], float(REGION_TILES), start_f[:, :],
                                                ALU.mult, ALU.add))
            nc.vector.tensor_scalar(from_tile[:, :], place_f[:, :], float(SPARE_TILE), None, ALU.min)\
                .then_inc(tiles_known, 1)
            all_slots = slot[:, :, :].rearrange("p t j -> p (t j)")
            then(nc.vector.tensor_tensor(beyond[:, :, :], all_slots.unsqueeze(2).to_broadcast([P, 2 * NT, E - 1]),
                                         floors[:, :].rearrange("p (e t) -> p e t", e=E)[:, 1:E, 0].unsqueeze(1)
                                         .to_broadcast([P, 2 * NT, E - 1]), ALU.is_gt))
            then(nc.vector.tensor_scalar(shrink[:, :], n_tiles[:, 0:E - 1], -float(REGION_TILES), float(P),
                                         ALU.add, ALU.mult))
            then(nc.vector.tensor_tensor(beyond[:, :, :], beyond[:, :, :],
                                         shrink[:, :].unsqueeze(1).to_broadcast([P, 2 * NT, E - 1]), ALU.mult))
            then(nc.vector.tensor_reduce(shift[:, :], beyond[:, :, :], AX.X, ALU.add))
            nc.vector.tensor_tensor(slot_y[:, :], all_slots, shift[:, :], ALU.add).then_inc(slots_known, 1)
            dve.wait_ge(gap_exp, 1)
            then(nc.vector.tensor_scalar(gap[:, :], gate[:, 1, :], 1.0, None, ALU.add))
            then(nc.vector.reciprocal(gate[:, 0, :], gap[:, :]))
            nc.vector.tensor_tensor(gate[:, 1, :], gate[:, 1, :], gate[:, 0, :], ALU.mult).then_inc(gates_known, 1)

            def split_x(b, count):
                dve.wait_ge(xt_rounded, count)
                nc.vector.tensor_tensor(xt_lo[:, b, :], xt_ps[b][:, :], xt_hi[:, b, :], ALU.subtract)\
                    .then_inc(xt_ready, 1)

            def square(b, count):
                dve.wait_ge(relu_done, count)
                nc.vector.tensor_tensor(hid[:, b, :], relu[:, :], relu[:, :], ALU.mult).then_inc(hid_ready, 1)

            split_x(0, 1)
            square(0, 1)
            split_x(1, 2)

            def slot_step(k, b, h):
                dve.wait_ge(ht_rounded, k + 1)
                nc.vector.tensor_tensor(ht_lo[:, b, :], ht_ps[b][:, :], ht_hi[:, b, :], ALU.subtract)\
                    .then_inc(ht_ready, 1)
                if more(k, 1):
                    square(1 - b, k + 2)
                if more(k, 2):
                    split_x(b, k + 3)

            slot_steps(dve, slot_step)
            dve.wait_ge(gates_known, 1)

            def normalise(t):
                b = t % 2
                dve.wait_ge(rstd_ready, t + 1)
                if t >= 2:
                    dve.wait_ge(fin_stored[b], 16 * (t // 2))
                nc.vector.tensor_scalar(fin[:, b, :], res[:, b, :], mean_var[:, b, 0:1], rstd[:, b:b + 1],
                                        ALU.subtract, ALU.mult).then_inc(fin_ready, 1)

            for t in range(NT):
                b = t % 2
                dve.wait_ge(gathered[t % GB], 32 * (t // GB + 1))
                nc.vector.scalar_tensor_tensor(acc[:, :], w_raw[:, t % GB * 2, :], gate[:, 0, t:t + 1],
                                               x1[:, t, :], ALU.mult, ALU.add).then_inc(acc_done, 1)
                dve.wait_ge(acc_done, t + 1)
                nc.vector.scalar_tensor_tensor(res[:, b, :], w_raw[:, t % GB * 2 + 1, :], gate[:, 1, t:t + 1],
                                               acc[:, :], ALU.mult, ALU.add).then_inc(summed, 1)
                dve.wait_ge(summed, t + 1)
                nc.vector.bn_stats(stats[:, :], res[:, b, :]).then_inc(stats_done, 1)
                dve.wait_ge(stats_done, t + 1)
                nc.vector.bn_aggr(mean_var[:, b, :], stats[:, :]).then_inc(var_ready, 1)
                if t >= 1:
                    normalise(t - 1)
            normalise(NT - 1)

        @block.tensor
        def _(pe):
            def turn_x(b, loaded):
                pe.wait_ge(xs_loaded[b], loaded)
                for c in range(CT):
                    mm = nc.tensor.transpose(xt_ps[b][:, c * P:(c + 1) * P], xs[:, b, c * P:(c + 1) * P], ident[:, :])
                mm.then_inc(xs_turned, 1)

            def times(out, b, hi, lo, first_block):
                for c in range(CT):
                    for part in range(3):
                        a = (hi, hi, lo)[part][:, b, c * P:(c + 1) * P]
                        w = one((w_hi, w_lo, w_hi)[part][:, bass.ds(first_block + c, 1), :])
                        mm = nc.tensor.matmul(out[:, :], a, w, start=(c == part == 0), stop=(c == CT - 1 and part == 2))
                return mm

            def load_owner(k):
                at = owner[0:1, k:k + 1] if isinstance(k, int) else owner[0:1, bass.ds(k, 1)]
                return pe.value_load(at, min_val=0, max_val=E - 1)

            def up(b, e, count):
                pe.wait_ge(xt_ready, count)
                pe.wait_ge(we_split, WT * e + WT)
                times(h_ps[b], b, xt_hi, xt_lo, expert_block(e)).then_inc(up_done, 1)

            pe.wait_ge(tiles_known, 2)
            turn_x(0, 16)
            up(0, load_owner(0), 1)
            turn_x(1, 16)

            def slot_step(k, b, h):
                pe.wait_ge(hid_ready, k + 2)
                for c in range(FT):
                    mm = nc.tensor.transpose(ht_ps[b][:, c * P:(c + 1) * P], hid[:, b, c * P:(c + 1) * P], ident[:, :])
                mm.then_inc(hid_turned, 1)
                if more(k, 1):
                    up(1 - b, load_owner(k + 1), k + 2)
                if more(k, 2):
                    turn_x(b, h * 16 + 32)
                e = load_owner(k)
                pe.wait_ge(ht_ready, k + 1)
                times(ye_ps[b], b, ht_hi, ht_lo, expert_block(e) + CT).then_inc(down_done, 1)

            slot_steps(pe, slot_step)


def build(nc, a, out_d):
    y_scratch = nc.dram_tensor("y_scratch", [NHG * NT + 1, P, GW], F32).ap()
    slots_x = nc.dram_tensor("slots_x", [(SPARE_TILE + 1) * P, C], F32).ap()
    slots_y = nc.dram_tensor("slots_y", [SLOT_TILES * P, C], F32).ap()
    ctx = ExitStack()
    with ctx:
        def sem(name):
            return ctx.enter_context(nc.semaphore(name))

        def sb(name, shape, dtype=F32):
            return ctx.enter_context(nc.sbuf_tensor(name, shape, dtype))

        w_raw = sb("w_raw", [P, RAW, GW])
        w_hi = sb("w_hi", [P, WB, GW], F32R)
        w_lo = sb("w_lo", [P, WB, GW], F32R)
        ident = sb("ident", [P, P])
        attention_phase(nc, sem, a["x_t"], a["w_all"], a["qk_w"], (a["ident"], a["dist"], a["slopes"]),
                        y_scratch, ident, w_raw, w_hi, w_lo)
        shared = (ident, w_raw, w_hi, w_lo,
                  sb("x1", [P, NT, C]), sb("x1_now", [P, 2, C]),
                  sb("gap", [P, NT]),
                  sb("slot", [P, NT, 2]),
                  sb("slot_now", [P, 2, 2], dt.uint32),
                  sb("run", [P, E]),
                  sem("we_split"), [sem("dispatched0"), sem("dispatched1")])
        residual_phase(nc, sem, y_scratch, a["w_all"], a["w_last"], a["subln_w"], a["x"], a["w_router"],
                       (a["before"], a["experts"], a["bases"]), a["w_experts"], slots_x, shared)
        expert_phase(nc, sem, a["w_experts"], (a["floors"], a["tiles"]), slots_x, slots_y, out_d, shared)


def layout(inputs):
    x = np.ascontiguousarray(inputs["L0_attn_x"]).reshape(B * T, C)
    row, col = np.arange(P)[:, None], np.arange(T)[None, :]
    dist = (T - P + row - col).astype(np.float32)
    dist[dist < 0] = MASKED
    slopes = np.array([2.0 ** (-(i + 1) / 2) for i in range(H)], np.float32)

    def rows(v):
        return np.ascontiguousarray(np.broadcast_to(np.asarray(v, np.float32).reshape(1, -1), (P, np.size(v))))

    qkv = np.stack([np.asarray(inputs["L0_attn_W" + m]).reshape(CT, P, NHG, GW) for m in "qkv"])
    proj = np.asarray(inputs["L0_attn_Wproj"]).reshape(NHG * HG, P, C)
    w_all = np.concatenate([qkv.transpose(3, 1, 2, 0, 4).reshape(W_ROUNDS, P, 3 * GW),
                            proj[:3 * CT].reshape(CT, 3, P, C).transpose(0, 2, 1, 3).reshape(CT, P, 3 * C)])
    experts = np.concatenate([np.asarray(inputs["L0_ffn_w_fc"]).reshape(E, CT, P, F),
                              np.asarray(inputs["L0_ffn_w_proj"]).reshape(E, FT, P, C)], axis=1)
    bases = np.arange(E) * REGION_TILES * P
    floors = bases[:, None] + np.concatenate([[-1], P * np.arange(1, NT)])[None, :]
    return {
        "x_t": np.ascontiguousarray(x.reshape(NT, P, CT, P).transpose(0, 3, 2, 1)).reshape(NT, P, CT * P),
        "x": x,
        "w_all": np.ascontiguousarray(w_all),
        "w_last": np.ascontiguousarray(proj[3 * CT:].transpose(1, 0, 2)),
        "w_experts": np.ascontiguousarray(experts.transpose(0, 2, 1, 3)).reshape(E, P, (CT + FT) * F),
        "qk_w": np.ascontiguousarray(np.stack([inputs["L0_attn_q_rms_w"], inputs["L0_attn_k_rms_w"]], axis=1)),
        "subln_w": np.ascontiguousarray(inputs["L0_attn_subln_w"]).reshape(D, 1),
        "w_router": np.ascontiguousarray(inputs["L0_ffn_w_router"]),
        "ident": np.eye(P, dtype=np.float32), "dist": dist, "slopes": rows(slopes),
        "before": np.triu(np.ones((P, P), np.float32), 1),
        "experts": rows(np.arange(E)), "bases": rows(bases), "floors": rows(floors),
        "tiles": rows(np.repeat(np.arange(SLOT_TILES), E)),
    }


def kernel(**inputs):
    from concourse import bacc
    from concourse.bass_utils import run_bass_kernel_spmd

    nc = bacc.Bacc("TRN2", target_bir_lowering=False, num_devices=1)
    arrays = layout(inputs)
    aps = {n: nc.dram_tensor(f"in_{n}", v.shape, F32, kind="ExternalInput").ap() for n, v in arrays.items()}
    out_d = nc.dram_tensor("out", [B * T, C], F32, kind="ExternalOutput").ap()
    build(nc, aps, out_d)
    result = run_bass_kernel_spmd(nc, [{f"in_{n}": v for n, v in arrays.items()}], core_ids=[0])
    return result.results[0]["out"].reshape(B, T, C)
```

```python
from contextlib import ExitStack

import numpy as np
import concourse.bass as bass
from concourse import mybir

dt = mybir.dt
F32, F32R = dt.float32, dt.float32r
ALU = mybir.AluOpType
ACT = mybir.ActivationFunctionType
AX = mybir.AxisListType

P = 128
B, T, C = 4, 512, 512
H, D = 16, 128
EPS = 1e-5
NT = B * T // P
TB = T // P
CT = C // P
HG = 4
NHG = H // HG
GW = HG * D
MASKED = 1e30
E = 8
F = 512
FT = F // P
SLOT_TILES = 2 * NT + E - 1
REGION_TILES = NT + 1
SPARE_TILE = E * REGION_TILES
CLEAR_STEPS = NT - 3
CLEARED = SLOT_TILES // CLEAR_STEPS
EARLY_PADS = 3
WB = 24
RAW = 8
W_ROUNDS = NHG * CT


def proj_block(s):
    return (s % 3) * CT + s // 3 if s < 3 * CT else s


def expert_block(e):
    return (CT + FT) * ((e + 2) % 3)


def one(ap):
    return ap.rearrange("p o c -> p (o c)")


def rows_of(ap):
    return ap.rearrange("o p c -> (o p) c")


def attention_phase(nc, sem, x_t, w_all, qk_w, consts, y_scratch, ident, w_raw, w_hi, w_lo, early_loaded, subln_d, subln, yn):
    ident_d, dist_d, slopes_d = consts
    y_of_tile = y_scratch[1:1 + NHG * NT, :, :].rearrange("(g t) p c -> t p g c", g=NHG)
    ctx = ExitStack()
    with ctx:
        def sb(name, shape, dtype=F32):
            return ctx.enter_context(nc.sbuf_tensor(name, shape, dtype))

        dist = sb("dist", [P, T])
        slopes = sb("slopes", [P, H])
        qkw = sb("qkw", [P, 2])
        q_scale = sb("q_scale", [P, 1])
        half = sb("half", [P, HG])
        x_raw = sb("x_raw", [P, 2, CT * P])
        x_hi = sb("x_hi", [P, 2, CT * P], F32R)
        x_lo = sb("x_lo", [P, 2, CT * P], F32R)
        kt_hi = sb("kt_hi", [P, 2, HG, T], F32R)
        kt_lo = sb("kt_lo", [P, 2, HG, T], F32R)
        vs = sb("vs", [P, 2, TB, GW])
        qt_hi = sb("qt_hi", [P, HG, P], F32R)
        qt_lo = sb("qt_lo", [P, HG, P], F32R)
        ksq = sb("ksq", [P, HG, D + 1])
        qsq = sb("qsq", [P, HG, D + 1])
        ysq = sb("ysq", [P, HG, D + 1])
        kn = sb("kn", [P, GW])
        qn = sb("qn", [P, GW])
        bias = sb("bias", [P, HG, T])
        logit = sb("logit", [P, T])
        prob = sb("prob", [P, T])
        prob_t = sb("prob_t", [P, T])
        small = sb("small", [P, 64])
        k_ms, q_ms, y_ms = small[:, 0:4], small[:, 4:8], small[:, 8:12]
        k_r, q_r, y_r = small[:, 24:28], small[:, 28:32], small[:, 32:36]
        least = small[:, 36:40]
        row_sum = small[:, 40:48]

        def ps(name):
            return ctx.enter_context(nc.psum_tensor(name, [P, GW], F32))

        k_ps, q_ps, v_ps = ps("k_ps"), ps("q_ps"), ps("v_ps")
        kt_ps, qt_ps = ps("kt_ps"), ps("qt_ps")
        score_ps, prob_ps, y_ps = ps("score_ps"), ps("prob_ps"), ps("y_ps")

        const_loaded = sem("const_loaded")
        x_loaded = [sem("x_loaded0"), sem("x_loaded1")]
        w_loaded, w_first = sem("w_loaded"), [sem(f"w_first{m}") for m in range(3)]
        k_first = [sem(f"k_first{c}") for c in range(CT)]
        w_rounded, w_ready = sem("w_rounded"), sem("w_ready")
        x_rounded, x_ready = sem("x_rounded"), sem("x_ready")
        k_projected, q_projected, v_projected = sem("k_projected"), sem("q_projected"), sem("v_projected")
        k_squared, q_squared, y_squared = sem("k_squared"), sem("q_squared"), sem("y_squared")
        k_summed, q_summed, y_summed = sem("k_summed"), sem("q_summed"), sem("y_summed")
        k_rstd, q_rstd, y_rstd = sem("k_rstd"), sem("q_rstd"), sem("y_rstd")
        k_normed, q_normed, y_normed = sem("k_normed"), sem("q_normed"), sem("y_normed")
        k_turned, q_turned = sem("k_turned"), sem("q_turned")
        k_rounded, q_rounded = sem("k_rounded"), sem("q_rounded")
        k_ready, q_ready, v_ready = sem("k_ready"), sem("q_ready"), sem("v_ready")
        scored, logits_ready, probs_ready = sem("scored"), sem("logits_ready"), sem("probs_ready")
        probs_turned, prob_t_ready = sem("probs_turned"), sem("prob_t_ready")
        y_done = sem("y_done")
        y_stored = [sem("y_stored0"), sem("y_stored1")]
        set_up, scale_set, biases_set = sem("set_up"), sem("scale_set"), sem("biases_set")

        block = ctx.enter_context(nc.Block())
        its = NHG * B

        def w_block(group_parity, m, c):
            return group_parity * 3 * CT + m * CT + c

        def raw_block(it, m):
            return ((it + 1) % 2) * CT + m

        FIRST = ((1, 0), (0, CT), (2, 0))
        last_it = its - 1

        @block.sync
        def _(sp):
            for b in range(2):
                sp.nop(nofuse=True).then_inc(y_stored[b], 16)
            first = w_all[0:CT, :, :].rearrange("c p (m j) -> m p c j", m=3)
            sp.dma_start(x_raw[:, 0, :], x_t[0]).then_inc(x_loaded[0], 16)
            for m, at in FIRST[0:2]:
                if m == 1:
                    for c in range(CT):
                        sp.dma_start(w_raw[:, at + c, :], first[m][:, c, :]).then_inc(k_first[c], 16)
                else:
                    sp.dma_start(w_raw[:, at:at + CT, :], first[m]).then_inc(w_first[m], 16)
            sp.dma_start(ident[:, :], ident_d).then_inc(const_loaded, 16)
            sp.dma_start(qkw[:, :], qk_w).then_inc(const_loaded, 16)
            sp.dma_start(dist[:, :], dist_d).then_inc(const_loaded, 16)
            sp.dma_start(slopes[:, :], slopes_d).then_inc(const_loaded, 16)
            sp.dma_start(x_raw[:, 1, :], x_t[1]).then_inc(x_loaded[1], 16)
            sp.dma_start(subln[:, :], subln_d).then_inc(early_loaded, 16)
            sp.wait_ge(w_ready, CT)
            sp.dma_start(w_raw[:, 0:CT, :], first[2]).then_inc(w_first[2], 16)
            for n in (2, 3):
                sp.wait_ge(x_ready, n - 1)
                sp.dma_start(x_raw[:, n % 2, :], x_t[n]).then_inc(x_loaded[n % 2], 16)

            def body(it, last):
                sp.wait_ge(w_ready, it * 3 + 3 * (CT - 1) + 1)
                sp.dma_start(w_raw[:, bass.ds(raw_block(it, 0), 3), :].rearrange("p m j -> p (m j)"),
                             rows_of(w_all[bass.ds(it + CT, 1), :, :])).then_inc(w_loaded, 16)
                for i in range(TB):
                    if last and i == 1:
                        sp.wait_ge(w_ready, last_it * 3 + 3 * CT)
                        sp.wait_ge(y_stored[1], 16 * (((NHG - 1) * NT + 1) // 2 + 2))
                        sp.dma_start(w_raw[:, CT:2 * CT, :], y_of_tile[0]).then_inc(early_loaded, 16)
                    if not last:
                        sp.wait_ge(x_ready, it * TB + i + 3)
                        sp.dma_start(x_raw[:, i % 2, :], rows_of(x_t[bass.ds((it * TB + i + 4) % NT, 1), :, :]))\
                            .then_inc(x_loaded[i % 2], 16)
                    sp.wait_ge(y_normed, it * TB + i + 1)
                    sp.dma_start(rows_of(y_scratch[bass.ds(it * TB + i, 1), :, :]),
                                 yn[:, i % 2, :]).then_inc(y_stored[i % 2], 16)

            with sp.Fori(0, last_it) as it:
                body(it, False)
            body(last_it, True)
            sp.wait_ge(y_normed, its * TB + 1)
            sp.dma_start(y_scratch[its * TB, :, :], yn[:, 0, :]).then_inc(y_stored[0], 16)

        @block.scalar
        def _(act):
            def square(out, src, projected, count, done):
                if projected is not None:
                    act.wait_ge(projected, count)
                nc.scalar.activation(out[:, :, 0:D], src[:, :].rearrange("p (h d) -> p h d", h=HG), ACT.Square,
                                     scale=float(D) ** -0.5).then_inc(done, 1)

            def round_x(parity, loaded):
                act.wait_ge(x_loaded[parity], loaded)
                nc.scalar.activation(x_hi[:, parity, :], x_raw[:, parity, :], ACT.Copy).then_inc(x_rounded, 1)

            def round_k(parity, i, count):
                act.wait_ge(k_turned, count)
                nc.scalar.activation(
                    kt_hi[:, bass.ds(parity, 1), :, i * P:(i + 1) * P].rearrange("p a h t -> p (a h) t"),
                    kt_ps[:, :].rearrange("p (h t) -> p h t", h=HG), ACT.Copy).then_inc(k_rounded, 1)

            def round_q(count):
                act.wait_ge(q_turned, count)
                nc.scalar.activation(qt_hi[:, :, :], qt_ps[:, :].rearrange("p (h t) -> p h t", h=HG),
                                     ACT.Copy, scale=q_scale[:, 0:1]).then_inc(q_rounded, 1)

            def keep_v(parity, i, count):
                act.wait_ge(v_projected, count)
                nc.scalar.activation(one(vs[:, bass.ds(parity, 1), i, :]), v_ps[:, :], ACT.Copy)\
                    .then_inc(v_ready, 1)

            def round_first(m, at):
                for c in range(CT):
                    if m == 1:
                        act.wait_ge(k_first[c], 16)
                    else:
                        act.wait_ge(w_first[m], 16)
                    nc.scalar.activation(w_hi[:, w_block(0, m, c), :], w_raw[:, at + c, :], ACT.Copy)\
                        .then_inc(w_rounded, 1)

            act.wait_ge(set_up, 1)
            for sq in (ksq, qsq):
                nc.scalar.activation(sq[:, :, D], half[:, :], ACT.Copy, scale=-2 * EPS).then_inc(set_up, 1)
            round_x(0, 16)
            round_first(*FIRST[0])
            round_first(*FIRST[1])
            square(ksq, k_ps, k_projected, 1, k_squared)
            round_x(1, 16)
            square(qsq, q_ps, q_projected, 1, q_squared)
            round_first(*FIRST[2])
            round_k(0, 0, 1)
            act.wait_ge(scale_set, 2)
            round_q(1)
            keep_v(0, 0, 1)
            act.wait_ge(set_up, 5)
            nc.scalar.activation(ysq[:, :, D], row_sum[:, 4:8], ACT.Square, scale=EPS ** 0.5)
            square(ysq, y_ps, None, 0, y_squared)

            def body(it, last):
                for i in range(TB):
                    n = it * TB + i
                    width = P * (i + 1)
                    nxt, nxt_i = (it % 2, i + 1) if i < TB - 1 else ((it + 1) % 2, 0)
                    ahead = not (last and i == TB - 1)

                    def softmax(h):
                        act.wait_ge(logits_ready, n * HG + h + 1)
                        nc.scalar.activation(prob[:, 0:width], logit[:, 0:width], ACT.Exp, scale=-1.0,
                                             bias=least[:, h:h + 1],
                                             accum_out=row_sum[:, (i % 2) * HG + h:(i % 2) * HG + h + 1])\
                            .then_inc(probs_ready, 1)

                    def keep_prob_t(h):
                        act.wait_ge(probs_turned, n * HG + h + 1)
                        nc.scalar.activation(prob_t[:, 0:width], prob_ps[:, 0:width], ACT.Copy)\
                            .then_inc(prob_t_ready, 1)

                    softmax(0)
                    if ahead:
                        square(ksq, k_ps, k_projected, n + 2, k_squared)
                    keep_prob_t(0)
                    if not (last and i >= 2):
                        round_x(i % 2, it * 32 + 16 * (i // 2 + 2))
                    softmax(1)
                    if ahead:
                        square(qsq, q_ps, q_projected, n + 2, q_squared)
                    keep_prob_t(1)
                    if i < 3:
                        act.wait_ge(w_loaded, it * 16 + 16)
                        nc.scalar.activation(
                            one(w_hi[:, bass.ds(w_block((it // CT + 1) % 2, i, it % CT), 1), :]),
                            one(w_raw[:, bass.ds(raw_block(it, i), 1), :]), ACT.Copy).then_inc(w_rounded, 1)
                    softmax(2)
                    if ahead:
                        round_k(nxt, nxt_i, n + 2)
                    keep_prob_t(2)
                    softmax(3)
                    if ahead:
                        round_q(n + 2)
                    keep_prob_t(3)
                    if ahead:
                        keep_v(nxt, nxt_i, n + 2)
                    now_half = slice((i % 2) * HG, (i % 2 + 1) * HG)
                    act.wait_ge(probs_ready, n * HG + HG)
                    nc.scalar.activation(ysq[:, :, D], row_sum[:, now_half], ACT.Square, scale=EPS ** 0.5)
                    square(ysq, y_ps, y_done, n + 1, y_squared)

            with act.Fori(0, last_it) as it:
                body(it, False)
            body(last_it, True)

        @block.gpsimd
        def _(pool):
            def rstd(ms, r, summed, ready, count):
                pool.wait_ge(summed, count)
                nc.gpsimd.tensor_tensor(r, ms, half[:, :], ALU.pow).then_inc(ready, 1)

            def rstd_y(count):
                rstd(y_ms, y_r, y_summed, y_rstd, count)

            def rstd_kq(count):
                rstd(k_ms, k_r, k_summed, k_rstd, count)
                rstd(q_ms, q_r, q_summed, q_rstd, count)

            def body(it, last):
                for i in range(TB):
                    rstd_y(it * TB + i + 1)
                    if not (last and i == TB - 1):
                        rstd_kq(it * TB + i + 2)

            pool.wait_ge(set_up, 5)
            rstd_kq(1)
            with pool.Fori(0, last_it) as it:
                body(it, False)
            body(last_it, True)
            rstd_y(its * TB + 1)

        @block.vector
        def _(dve):
            def heads(ap):
                return ap.rearrange("p (h d) -> p h d", h=HG)

            def row_means(sq, ms, squared, count, done):
                dve.wait_ge(squared, count)
                nc.vector.tensor_reduce(ms, sq[:, :, :], AX.X, ALU.add).then_inc(done, 1)

            def normalise(out, src, r, ready, count, done):
                dve.wait_ge(ready, count)
                nc.vector.tensor_tensor(heads(out), heads(src[:, :]),
                                        r.unsqueeze(2).to_broadcast([P, HG, D]), ALU.mult).then_inc(done, 1)

            def split_x(parity, count):
                dve.wait_ge(x_rounded, count)
                nc.vector.tensor_tensor(x_lo[:, parity, :], x_raw[:, parity, :], x_hi[:, parity, :],
                                        ALU.subtract).then_inc(x_ready, 1)

            def split_q(count):
                dve.wait_ge(q_rounded, count)
                nc.vector.scalar_tensor_tensor(qt_lo[:, :, :].rearrange("p h t -> p (h t)"), qt_ps[:, :], q_scale[:, 0:1],
                                               qt_hi[:, :, :].rearrange("p h t -> p (h t)"), ALU.mult, ALU.subtract)\
                    .then_inc(q_ready, 1)

            def split_k(parity, i, count):
                dve.wait_ge(k_rounded, count)
                hi, lo = (t[:, bass.ds(parity, 1), :, i * P:(i + 1) * P].rearrange("p a h t -> p (a h) t")
                          for t in (kt_hi, kt_lo))
                nc.vector.tensor_tensor(lo, kt_ps[:, :].rearrange("p (h t) -> p h t", h=HG), hi, ALU.subtract)\
                    .then_inc(k_ready, 1)

            nc.vector.memset(half[:, :], -0.5).then_inc(set_up, 1)
            nc.vector.memset(y_ps[:, :], 0.0).then_inc(set_up, 1)
            nc.vector.memset(row_sum, 1.0).then_inc(set_up, 1)
            def split_first(s, m, at):
                for c in range(CT):
                    dve.wait_ge(w_rounded, s * CT + c + 1)
                    blk = w_block(0, m, c)
                    nc.vector.tensor_tensor(w_lo[:, blk, :], w_raw[:, at + c, :], w_hi[:, blk, :],
                                            ALU.subtract).then_inc(w_ready, 1)

            split_x(0, 1)
            split_first(0, *FIRST[0])
            split_first(1, *FIRST[1])
            dve.wait_ge(const_loaded, 64)
            nc.vector.tensor_tensor(q_scale[:, :], qkw[:, 0:1], qkw[:, 1:2], ALU.mult).then_inc(scale_set, 1)
            dve.wait_ge(scale_set, 1)
            nc.vector.tensor_scalar(q_scale[:, :], q_scale[:, :], -float(D) ** -0.5, None, ALU.mult)\
                .then_inc(scale_set, 1)
            row_means(ksq, k_ms, k_squared, 1, k_summed)
            split_x(1, 2)
            row_means(qsq, q_ms, q_squared, 1, q_summed)
            normalise(kn[:, :], k_ps, k_r, k_rstd, 1, k_normed)
            normalise(qn[:, :], q_ps, q_r, q_rstd, 1, q_normed)
            split_first(2, *FIRST[2])
            split_k(0, 0, 1)
            dve.wait_ge(scale_set, 2)
            split_q(1)

            def set_biases(hg):
                for h in range(HG):
                    nc.vector.tensor_scalar(bias[:, h, :], dist[:, :], slopes[:, bass.ds(hg * HG + h, 1)], None,
                                            ALU.mult).then_inc(biases_set, 1)
                dve.wait_ge(biases_set, hg * HG + HG)
                dve.nop(nofuse=True)

            def body(hg, b, last):
                it = hg * B + b
                for i in range(TB):
                    n = it * TB + i
                    width = P * (i + 1)
                    nxt, nxt_i = (it % 2, i + 1) if i < TB - 1 else ((it + 1) % 2, 0)
                    ahead = not (last and i == TB - 1)

                    def logits(h):
                        dve.wait_ge(scored, n * HG + h + 1)
                        dve.nop(nofuse=True)
                        nc.vector.tensor_tensor_reduce(
                            out=logit[:, 0:width], in0=score_ps[:, 0:width],
                            in1=bias[:, h, T - width:T], scale=1.0, scalar=3e38,
                            op0=ALU.add, op1=ALU.min, accum_out=least[:, h:h + 1]).then_inc(logits_ready, 1)

                    logits(0)
                    row_means(ysq, y_ms, y_squared, n + 1, y_summed)
                    dve.wait_ge(y_stored[i % 2], it * 32 + 16 * (i // 2 + 1))
                    normalise(yn[:, i % 2, :], y_ps, y_r, y_rstd, n + 1, y_normed)
                    if ahead:
                        row_means(ksq, k_ms, k_squared, n + 2, k_summed)
                    logits(1)
                    if ahead:
                        normalise(kn[:, :], k_ps, k_r, k_rstd, n + 2, k_normed)
                    if not (last and i >= 2):
                        split_x(i % 2, n + 3)
                    if ahead:
                        row_means(qsq, q_ms, q_squared, n + 2, q_summed)
                    logits(2)
                    if ahead:
                        normalise(qn[:, :], q_ps, q_r, q_rstd, n + 2, q_normed)
                    logits(3)
                    if ahead:
                        split_k(nxt, nxt_i, n + 2)
                        split_q(n + 2)
                    if i < 3:
                        dve.wait_ge(w_rounded, it * 3 + 3 * CT + i + 1)
                        blk = w_block((hg + 1) % 2, i, b)
                        nc.vector.tensor_tensor(
                            one(w_lo[:, bass.ds(blk, 1), :]), one(w_raw[:, bass.ds(raw_block(it, i), 1), :]),
                            one(w_hi[:, bass.ds(blk, 1), :]), ALU.subtract).then_inc(w_ready, 1)

            with dve.Fori(0, NHG - 1) as hg:
                set_biases(hg)
                with dve.Fori(0, B) as b:
                    body(hg, b, False)
            set_biases(NHG - 1)
            with dve.Fori(0, B - 1) as b:
                body(NHG - 1, b, False)
            body(NHG - 1, B - 1, True)
            row_means(ysq, y_ms, y_squared, its * TB + 1, y_summed)
            dve.wait_ge(y_stored[0], 16 * (its * TB // 2 + 1))
            normalise(yn[:, 0, :], y_ps, y_r, y_rstd, its * TB + 1, y_normed)

        @block.tensor
        def _(pe):
            def project(out, m, x_buf, parity, first=0, last=3 * CT):
                for s in range(first, last):
                    c, part = divmod(s, 3)
                    xs = (x_hi, x_hi, x_lo)[part][:, x_buf, c * P:(c + 1) * P]
                    ws = one((w_hi, w_lo, w_hi)[part][:, bass.ds(w_block(parity, m, c), 1), :])
                    mm = nc.tensor.matmul(out[:, :], xs, ws, start=(s == 0), stop=(s == 3 * CT - 1))
                return mm

            def turn(out, src, done):
                for h in range(HG):
                    mm = nc.tensor.transpose(out[:, h * P:(h + 1) * P], src[:, h * D:(h + 1) * D], ident[:, :])
                mm.then_inc(done, 1)

            pe.wait_ge(set_up, 5)
            pe.wait_ge(x_ready, 1)
            for s, ((m, _), out, done) in enumerate(zip(FIRST, (k_ps, q_ps, v_ps),
                                                          (k_projected, q_projected, v_projected))):
                if s == 2:
                    pe.wait_ge(const_loaded, 64)
                    pe.wait_ge(k_normed, 1)
                    turn(kt_ps, kn, k_turned)
                    pe.wait_ge(q_normed, 1)
                    turn(qt_ps, qn, q_turned)
                for c in range(CT):
                    pe.wait_ge(w_ready, s * CT + c + 1)
                    mm = project(out, m, 0, 0, 3 * c, 3 * c + 3)
                mm.then_inc(done, 1)

            def body(it, last):
                for i in range(TB):
                    n = it * TB + i
                    now = it % 2
                    xb = (i + 1) % 2
                    wp = (it // B) % 2 if i < TB - 1 else ((it + 1) // B) % 2
                    width = P * (i + 1)
                    ahead = not (last and i == TB - 1)

                    def score(h):
                        for part in range(3):
                            qs = (qt_hi, qt_hi, qt_lo)[part][:, h, :]
                            ks = (kt_hi, kt_lo, kt_hi)[part]
                            keys = ks[:, bass.ds(now, 1), h, 0:width]
                            keys = keys.to_broadcast([P, 2, P]) if i == 0 else one(keys)
                            mm = nc.tensor.matmul(score_ps[:, 0:max(width, 2 * P)], qs, keys,
                                                  start=(part == 0), stop=(part == 2))
                        mm.then_inc(scored, 1)

                    def turn_probs(h):
                        pe.wait_ge(probs_ready, n * HG + h + 1)
                        for j in range(i + 1):
                            mm = nc.tensor.transpose(prob_ps[:, j * P:(j + 1) * P], prob[:, j * P:(j + 1) * P],
                                                     ident[:, :])
                        mm.then_inc(probs_turned, 1)

                    def attend(h):
                        pe.wait_ge(prob_t_ready, n * HG + h + 1)
                        for j in range(i + 1):
                            mm = nc.tensor.matmul(
                                y_ps[:, h * D:(h + 1) * D], prob_t[:, j * P:(j + 1) * P],
                                one(vs[:, bass.ds(now, 1), j, h * D:(h + 1) * D]),
                                start=(j == 0), stop=(j == i))
                        return mm

                    pe.wait_ge(k_ready, n + 1)
                    pe.wait_ge(q_ready, n + 1)
                    score(0)
                    if ahead:
                        pe.wait_ge(x_ready, n + 2)
                        if i == TB - 1:
                            pe.wait_ge(w_ready, it * 3 + (CT + 1) * 3)
                        project(k_ps, 1, xb, wp).then_inc(k_projected, 1)
                    turn_probs(0)
                    score(1)
                    if ahead:
                        project(q_ps, 0, xb, wp).then_inc(q_projected, 1)
                    pe.wait_ge(v_ready, n + 1)
                    pe.wait_ge(y_normed, n + 1)
                    attend(0)
                    turn_probs(1)
                    score(2)
                    if ahead:
                        pe.wait_ge(k_normed, n + 2)
                        turn(kt_ps, kn, k_turned)
                        project(v_ps, 2, xb, wp, 0, 4)
                    attend(1)
                    turn_probs(2)
                    score(3)
                    if ahead:
                        project(v_ps, 2, xb, wp, 4, 8)
                        pe.wait_ge(q_normed, n + 2)
                        turn(qt_ps, qn, q_turned)
                    attend(2)
                    turn_probs(3)
                    if ahead:
                        project(v_ps, 2, xb, wp, 8, 12).then_inc(v_projected, 1)
                    attend(3).then_inc(y_done, 1)

            with pe.Fori(0, last_it) as it:
                body(it, False)
            body(last_it, True)

    def wait_for_y(engine):
        engine.wait_ge(y_stored[0], 16 * (its * TB // 2 + 2))
        engine.wait_ge(y_stored[1], 16 * (its * TB // 2 + 1))

    return wait_for_y


def token_steps(engine, step):
    for s in (0, 1):
        step(s, s, 0)
    with engine.Fori(1, NT // 2 - 1) as half:
        for b in range(2):
            step(half * 2 + b, b, half)
    for s in (NT - 2, NT - 1):
        step(s, s % 2, s // 2)


def s_between(s, first, last):
    return first <= s <= last if isinstance(s, int) else first <= 2 and last >= NT - 3


def before_step(s, limit):
    return isinstance(s, int) and s < limit


def residual_phase(nc, sem, y_scratch, w_last, subln, early_loaded, wait_for_y, x_d, w_router, route_consts, w_experts,
                   x1_now, slot_now, run_i, zeros, slots_x, slots_y, y_cleared, tables, shared):
    ident, w_raw, w_hi, w_lo, x1, gap, slot, we_split, raw_loaded, dispatched = shared
    end_i, n_tiles, bases, owner, from_tile, tables_known, padded, pad = tables
    ctx = ExitStack()
    with ctx:
        def sb(name, shape, dtype=F32):
            return ctx.enter_context(nc.sbuf_tensor(name, shape, dtype))

        w_r = sb("w_r", [P, CT, E])
        before = sb("before", [P, P])
        experts = sb("experts", [P, E])
        run = sb("run", [P, E])
        y_raw = sb("y_raw", [P, 2, NHG, GW])
        yt_hi = sb("yt_hi", [P, NHG, GW], F32R)
        yt_lo = sb("yt_lo", [P, NHG, GW], F32R)
        x_nat = sb("x_nat", [P, 2, C])
        res = sb("res", [P, C])
        stats = sb("stats", [P, 6])
        mean_var = sb("mean_var", [P, 2])
        var_eps = sb("var_eps", [P, 1])
        rstd = sb("rstd", [P, 1])
        half = sb("half2", [P, 1])
        eps = sb("eps2", [P, 1])
        x1_t = sb("x1_t", [P, C])
        before_b = sb("before_b", [P, P], dt.bfloat16)
        ones_b = sb("ones_b", [P, P], dt.bfloat16)
        ones = sb("ones", [P, E])
        floors = sb("floors", [P, E * NT])
        tiles = sb("tiles", [P, SLOT_TILES * E])
        over = sb("over", [P, E, NT])
        end_tile = sb("end_tile", [P, E])
        past = sb("past", [P, SLOT_TILES, E])
        past_n = sb("past_n", [P, SLOT_TILES, E])
        owner_f = sb("owner_f", [P, SLOT_TILES])
        start_f = sb("start_f", [P, SLOT_TILES])
        place_f = sb("place_f", [P, SLOT_TILES])
        logits = sb("logits", [P, E])
        best = sb("best", [P, 8])
        best_at = sb("best_at", [P, 8], dt.uint32)
        choice = sb("choice", [P, 2])
        taken = sb("taken", [P, 2, E])
        both = sb("both", [P, E], dt.bfloat16)
        next_slot = sb("next_slot", [P, E])
        pick = sb("pick", [P, 2, E])
        slot_f = sb("slot_f", [P, 2])

        def ps(name):
            return ctx.enter_context(nc.psum_tensor(name, [P, C], F32))

        turn_ps = [ps(f"turn_ps{g}") for g in range(NHG)]
        out_ps = [ps("out_ps0"), ps("out_ps1")]
        x1_ps, router_ps = ps("x1_ps"), ps("router_ps")
        rank_ps, total_ps = router_ps[:, E:2 * E], router_ps[:, 2 * E:3 * E]

        const_loaded, table_step = sem("p_const_loaded"), sem("table_step")
        wp_loaded, wp_rounded, wp_ready = sem("wp_loaded"), sem("wp_rounded"), sem("wp_ready")
        y_loaded = [sem("y_loaded0"), sem("y_loaded1")]
        x_loaded = [sem("xn_loaded0"), sem("xn_loaded1")]
        set_up = sem("p_set_up")
        y_turned, yt_rounded, yt_ready = sem("y_turned"), sem("yt_rounded"), sem("yt_ready")
        projected, summed, stats_done = sem("projected"), sem("res_summed"), sem("stats_done")
        var_ready, var_biased, rstd_ready = sem("var_ready"), sem("var_biased"), sem("rstd_ready")
        x1_ready, x1_turned, x1_t_ready = sem("x1_ready"), sem("x1_turned"), sem("x1_t_ready")
        x1_kept = sem("x1_kept")
        routed, logits_kept, best_found = sem("routed"), sem("logits_kept"), sem("best_found")
        best_placed, chosen, taken_set = sem("best_placed"), sem("chosen"), sem("taken_set")
        both_ready, ranked, run_ready = sem("both_ready"), sem("ranked"), sem("run_ready")
        next_ready, picked, slot_summed = sem("next_ready"), sem("picked"), sem("slot_summed")
        ends_known = sem("ends_known")
        slots_ready, we_loaded = sem("slots_ready"), [sem("we0_loaded0"), sem("we0_loaded1")]
        block = ctx.enter_context(nc.Block())

        y_tiles = y_scratch[1:1 + NHG * NT, :, :].rearrange("(g t) p c -> t p g c", g=NHG)
        x_tiles = x_d.rearrange("(t p) c -> t p c", p=P)
        y_slots = slots_y.rearrange("(k p) c -> p k c", p=P)
        x_slots = slots_x.rearrange("(k p) c -> k p c", p=P)
        LAST = NHG - 1

        def tile_of(tiles, t):
            return tiles[t] if isinstance(t, int) else rows_of(tiles[bass.ds(t, 1), :, :])

        @block.sync
        def _(sp):
            def load_y(t, b):
                src = y_tiles[t] if isinstance(t, int) else \
                    y_tiles[bass.ds(t, 1), :, :, :].rearrange("o p g c -> (o p) g c")
                sp.dma_start(y_raw[:, b, :, :], src).then_inc(y_loaded[b], 16)

            def load_x(t, b):
                sp.dma_start(x_nat[:, b, :], tile_of(x_tiles, t)).then_inc(x_loaded[b], 16)

            sp.dma_start(w_raw[:, 0:CT, :], w_last).then_inc(wp_loaded, 16)
            load_y(1, 1)
            load_x(0, 0)
            load_x(1, 1)
            load_y(2, 0)
            sp.dma_start(w_r[:, :, :], w_router.rearrange("(c p) e -> p c e", p=P)).then_inc(const_loaded, 16)
            for dst, src in zip((before, experts, run, floors, tiles), route_consts):
                sp.dma_start(dst[:, :], src).then_inc(const_loaded, 16)

            def step(s, b, h):
                if not before_step(s, 1) and not (isinstance(s, int) and s >= NT - 2):
                    sp.wait_ge(y_turned, s * NHG + NHG)
                    if isinstance(s, int) and s == NT - 3:
                        wait_for_y(sp)
                    load_y(s + 2, b)
                if not before_step(s, 1) and not (isinstance(s, int) and s == NT - 1):
                    sp.wait_ge(summed, s)
                    sp.nop(nofuse=True)
                    load_x(s + 1, 1 - b)

                if s_between(s, 1, CLEAR_STEPS):
                    dst = y_slots[:, (s - 1) * CLEARED:s * CLEARED, :] if isinstance(s, int) else \
                        y_slots[:, bass.ds((s - 1) * CLEARED, CLEARED), :]
                    sp.dma_start(dst, zeros[:, :].unsqueeze(1).to_broadcast([P, CLEARED, C])).then_inc(y_cleared, 16)

            sp.wait_ge(set_up, 6)
            token_steps(sp, step)
            sp.dma_start(x_slots[SPARE_TILE], zeros[:, :]).then_inc(padded[EARLY_PADS], 16)
            sp.wait_ge(ends_known, 1)
            for e in range(EARLY_PADS):
                pad(sp, e)

        @block.scalar
        def _(act):
            def round_y(g, count):
                act.wait_ge(y_turned, count)
                nc.scalar.activation(yt_hi[:, g, :], turn_ps[g][:, :], ACT.Copy, scale=subln[:, 0:1])\
                    .then_inc(yt_rounded, 1)

            def keep_x1(t, b):
                act.wait_ge(x1_turned, t + 1)
                nc.scalar.activation(x1_t[:, :], x1_ps[:, :], ACT.Copy).then_inc(x1_t_ready, 1)
                out = x1[:, t, :] if isinstance(t, int) else one(x1[:, bass.ds(t, 1), :])
                nc.scalar.activation(out, x1_now[:, b, :], ACT.Copy).then_inc(x1_kept, 1)

            act.wait_ge(early_loaded, 32)
            for g in range(NHG):
                round_y(g, g + 1)
            act.wait_ge(wp_loaded, 16)
            for h in range(HG):
                nc.scalar.activation(w_hi[:, proj_block(LAST * HG + h), :], w_raw[:, h, :], ACT.Copy)\
                    .then_inc(wp_rounded, 1)

            def step(s, b, h):
                for g in range(NHG):
                    if not (isinstance(s, int) and s == NT - 1):
                        round_y(g, s * NHG + NHG + g + 1)
                    if g == 1 and not before_step(s, 1):
                        keep_x1(s - 1, 1 - b)

            token_steps(act, step)
            keep_x1(NT - 1, 1)

        @block.gpsimd
        def _(pool):
            def load_expert(m):
                part = slice(expert_block(0) + m * CT, expert_block(0) + (m + 1) * CT)
                src = w_experts[0, :, m * CT * F:(m + 1) * CT * F].rearrange("p (c f) -> p c f", c=CT)
                pool.dma_start(w_hi[:, part, :], src).then_inc(we_loaded[m], 16)
                pool.dma_start(w_raw[:, (1 - m) * CT:(2 - m) * CT, :], src).then_inc(we_loaded[m], 16)

            def split_expert(m):
                pool.wait_ge(we_loaded[m], 32)
                for c in range(CT):
                    blk = expert_block(0) + m * CT + c
                    nc.gpsimd.tensor_tensor(w_lo[:, blk, :], w_raw[:, (1 - m) * CT + c, :], w_hi[:, blk, :],
                                            ALU.subtract).then_inc(we_split, 1)

            pool.wait_ge(y_turned, NHG)
            load_expert(0)
            pool.wait_ge(wp_ready, HG)
            load_expert(1)

            def inverse_std(t):
                pool.wait_ge(var_ready, t + 1)
                nc.gpsimd.tensor_tensor(var_eps[:, :], mean_var[:, 1:2], eps[:, :], ALU.add).then_inc(var_biased, 1)
                pool.wait_ge(var_biased, t + 1)
                nc.gpsimd.tensor_tensor(rstd[:, :], var_eps[:, :], half[:, :], ALU.pow).then_inc(rstd_ready, 1)

            def dispatch(t, b):
                pool.wait_ge(slots_ready, t + 1)
                pool.nop(nofuse=True)
                for j in range(2):
                    pool.indirect_dma_start(slots_x, bass.IndirectOffsetOnAxis(ap=slot_now[:, b, j:j + 1], axis=0),
                                            x1_now[:, b, :], None).then_inc(dispatched[b], 16)

            def step(s, b, h):
                if not before_step(s, 1):
                    inverse_std(s - 1)
                if isinstance(s, int) and s == 1:
                    split_expert(0)
                    split_expert(1)
                if isinstance(s, int) and s == NT - 2:
                    pool.wait_ge(we_split, CT + FT)
                    pool.dma_start(w_raw[:, :, :].rearrange("p s f -> p (s f)"), w_experts[1])\
                        .then_inc(raw_loaded, 16)
                if not before_step(s, 2):
                    dispatch(s - 2, b)

            pool.wait_ge(set_up, 6)
            token_steps(pool, step)
            inverse_std(NT - 1)
            dispatch(NT - 2, 0)
            dispatch(NT - 1, 1)

        @block.vector
        def _(dve):
            def split_y(g, count):
                dve.wait_ge(yt_rounded, count)
                nc.vector.scalar_tensor_tensor(yt_lo[:, g, :], turn_ps[g][:, :], subln[:, 0:1],
                                               yt_hi[:, g, :], ALU.mult, ALU.subtract).then_inc(yt_ready, 1)

            def add_residual(t, b, loaded):
                dve.wait_ge(projected, t + 1)
                dve.wait_ge(x_loaded[b], loaded)
                nc.vector.tensor_tensor(res[:, :], out_ps[b][:, :], x_nat[:, b, :], ALU.add).then_inc(summed, 1)
                dve.wait_ge(summed, t + 1)
                nc.vector.bn_stats(stats[:, :], res[:, :]).then_inc(stats_done, 1)
                dve.wait_ge(stats_done, t + 1)
                dve.nop(nofuse=True)
                nc.vector.bn_aggr(mean_var[:, :], stats[:, :]).then_inc(var_ready, 1)

            def layernorm(t, b, sent):
                dve.wait_ge(rstd_ready, t + 1)
                if isinstance(t, int) and t == 0:
                    wait_for_y(dve)
                if sent is not None:
                    dve.wait_ge(x1_kept, t - 1)
                    dve.wait_ge(dispatched[b], sent)
                nc.vector.tensor_scalar(x1_now[:, b, :], res[:, :], mean_var[:, 0:1], rstd[:, 0:1],
                                        ALU.subtract, ALU.mult).then_inc(x1_ready, 1)

            def choose(t):
                dve.wait_ge(routed, t + 1)
                nc.vector.tensor_copy(logits[:, :], router_ps[:, 0:E]).then_inc(logits_kept, 1)
                dve.wait_ge(logits_kept, t + 1)
                dve.nop(nofuse=True)
                nc.vector.max(best[:, :], logits[:, :]).then_inc(best_found, 1)
                dve.wait_ge(best_found, t + 1)
                dve.nop(nofuse=True)
                nc.vector.max_index(best_at[:, :], best[:, :], logits[:, :]).then_inc(best_placed, 1)
                out = gap[:, t:t + 1] if isinstance(t, int) else gap[:, bass.ds(t, 1)]
                nc.vector.tensor_tensor(out, best[:, 1:2], best[:, 0:1], ALU.subtract)
                dve.wait_ge(best_placed, t + 1)
                nc.vector.tensor_copy(choice[:, :], best_at[:, 0:2]).then_inc(chosen, 1)
                dve.wait_ge(chosen, t + 1)
                nc.vector.tensor_tensor(taken[:, :, :], experts[:, :].unsqueeze(1).to_broadcast([P, 2, E]),
                                        choice[:, :].unsqueeze(2).to_broadcast([P, 2, E]), ALU.is_equal)\
                    .then_inc(taken_set, 1)
                dve.wait_ge(taken_set, t + 1)
                nc.vector.tensor_tensor(both[:, :], taken[:, 0, :], taken[:, 1, :], ALU.add).then_inc(both_ready, 1)

            def place(t, b):
                dve.wait_ge(ranked, t + 1)
                dve.wait_ge(run_ready, t + 1)
                nc.vector.tensor_tensor(next_slot[:, :], rank_ps, run[:, :], ALU.add).then_inc(next_ready, 1)
                nc.vector.tensor_tensor(run[:, :], total_ps, run[:, :], ALU.add).then_inc(run_ready, 1)
                dve.wait_ge(next_ready, t + 1)
                nc.vector.tensor_tensor(pick[:, :, :], taken[:, :, :],
                                        next_slot[:, :].unsqueeze(1).to_broadcast([P, 2, E]), ALU.mult)\
                    .then_inc(picked, 1)
                dve.wait_ge(picked, t + 1)
                nc.vector.tensor_reduce(slot_f[:, :], pick[:, :, :], AX.X, ALU.add).then_inc(slot_summed, 1)
                dve.wait_ge(slot_summed, t + 1)
                nc.vector.tensor_copy(slot_now[:, b, :], slot_f[:, :]).then_inc(slots_ready, 1)
                out = slot[:, t, :] if isinstance(t, int) else one(slot[:, bass.ds(t, 1), :])
                nc.vector.tensor_copy(out, slot_f[:, :])

            def slot_tables():
                steps = [0]

                def then(op):
                    steps[0] += 1
                    op.then_inc(table_step, 1)
                    dve.wait_ge(table_step, steps[0])

                dve.wait_ge(run_ready, NT + 1)
                nc.vector.tensor_copy(run_i[:, :], run[:, :]).then_inc(ends_known, 1)
                then(nc.vector.tensor_tensor(over[:, :, :], run[:, :].unsqueeze(2).to_broadcast([P, E, NT]),
                                             floors[:, :].rearrange("p (e t) -> p e t", e=E), ALU.is_gt))
                then(nc.vector.tensor_reduce(n_tiles[:, :], over[:, :, :], AX.X, ALU.add))
                then(nc.vector.tensor_tensor_scan(end_tile[:, :], ones[:, 0:E], n_tiles[:, :], 0.0,
                                                  ALU.mult, ALU.add))
                tile_numbers = tiles[:, :].rearrange("p (k e) -> p k e", e=E)
                then(nc.vector.tensor_tensor(past[:, :, :], tile_numbers,
                                             end_tile[:, :].unsqueeze(1).to_broadcast([P, SLOT_TILES, E]), ALU.is_ge))
                then(nc.vector.tensor_tensor(past_n[:, :, :], past[:, :, :],
                                             n_tiles[:, :].unsqueeze(1).to_broadcast([P, SLOT_TILES, E]), ALU.mult))
                nc.vector.tensor_reduce(owner_f[:, :], past[:, :, :], AX.X, ALU.add)
                then(nc.vector.tensor_reduce(start_f[:, :], past_n[:, :, :], AX.X, ALU.add))
                then(nc.vector.tensor_tensor(start_f[:, :], tile_numbers[:, :, 0], start_f[:, :], ALU.subtract))
                then(nc.vector.scalar_tensor_tensor(place_f[:, :], owner_f[:, :], float(REGION_TILES), start_f[:, :],
                                                    ALU.mult, ALU.add))
                nc.vector.tensor_scalar(from_tile[:, :], place_f[:, :], float(SPARE_TILE), None, ALU.min)
                nc.vector.tensor_scalar(owner[:, :], owner_f[:, :], float(E - 1), None, ALU.min)
                nc.vector.tensor_copy(end_i[:, :], end_tile[:, :]).then_inc(tables_known, 1)
                nc.vector.tensor_copy(bases[:, :], floors[:, :].rearrange("p (e t) -> p e t", e=E)[:, :, 0])

            nc.vector.memset(half[:, :], -0.5).then_inc(set_up, 1)
            nc.vector.memset(eps[:, :], EPS).then_inc(set_up, 1)
            nc.vector.memset(ones[:, :], 1.0).then_inc(set_up, 1)
            nc.vector.memset(ones_b[:, :], 1.0).then_inc(set_up, 1)
            nc.vector.memset(zeros[:, :], 0.0).then_inc(set_up, 1)
            dve.wait_ge(early_loaded, 32)
            for g in range(NHG):
                split_y(g, g + 1)
            for h in range(HG):
                dve.wait_ge(wp_rounded, h + 1)
                blk = proj_block(LAST * HG + h)
                nc.vector.tensor_tensor(w_lo[:, blk, :], w_raw[:, h, :], w_hi[:, blk, :],
                                        ALU.subtract).then_inc(wp_ready, 1)
            dve.wait_ge(const_loaded, 96)
            dve.nop(nofuse=True).then_inc(run_ready, 1)
            nc.vector.tensor_copy(before_b[:, :], before[:, :]).then_inc(set_up, 1)

            def step(s, b, h):
                turning = not (isinstance(s, int) and s == NT - 1)
                if not before_step(s, 1):
                    add_residual(s - 1, 1 - b, 16 * h + 16 * b)
                if not before_step(s, 2):
                    place(s - 2, b)
                if turning:
                    split_y(0, s * NHG + NHG + 1)
                if not before_step(s, 1):
                    layernorm(s - 1, 1 - b, None if before_step(s, 3) else 32 * h - 32 + 32 * b)
                if turning:
                    split_y(1, s * NHG + NHG + 2)
                    split_y(2, s * NHG + NHG + 3)
                if not before_step(s, 1):
                    choose(s - 1)
                if turning:
                    split_y(3, s * NHG + NHG + 4)

            token_steps(dve, step)
            add_residual(NT - 1, 1, 16 * (NT // 2))
            place(NT - 2, 0)
            layernorm(NT - 1, 1, 32 * (NT // 2 - 1))
            choose(NT - 1)
            place(NT - 1, 1)
            slot_tables()

        @block.tensor
        def _(pe):
            def turn_y(src, g):
                for h in range(HG):
                    mm = nc.tensor.transpose(turn_ps[g][:, h * P:(h + 1) * P],
                                             src[:, h * P:(h + 1) * P], ident[:, :])
                mm.then_inc(y_turned, 1)

            def project(b, g):
                for h in range(HG):
                    for part in range(3):
                        ys = (yt_hi, yt_hi, yt_lo)[part][:, g, h * P:(h + 1) * P]
                        ws = (w_hi, w_lo, w_hi)[part][:, proj_block(g * HG + h), :]
                        mm = nc.tensor.matmul(out_ps[b][:, :], ys, ws, start=(g == h == part == 0),
                                              stop=(g == NHG - 1 and h == HG - 1 and part == 2))
                return mm

            def turn_x1(t, b):
                pe.wait_ge(x1_ready, t + 1)
                for c in range(CT):
                    mm = nc.tensor.transpose(x1_ps[:, c * P:(c + 1) * P], x1_now[:, b, c * P:(c + 1) * P], ident[:, :])
                mm.then_inc(x1_turned, 1)

            def route(t):
                pe.wait_ge(x1_t_ready, t + 1)
                for c in range(CT):
                    mm = nc.tensor.matmul(router_ps[:, 0:E], x1_t[:, c * P:(c + 1) * P], w_r[:, c, :],
                                          start=(c == 0), stop=(c == CT - 1))
                mm.then_inc(routed, 1)

            def rank(t):
                pe.wait_ge(both_ready, t + 1)
                nc.tensor.matmul(rank_ps, before_b[:, :], both[:, :], start=True, stop=True)
                nc.tensor.matmul(total_ps, ones_b[:, :], both[:, :], start=True, stop=True).then_inc(ranked, 1)

            pe.wait_ge(early_loaded, 32)
            for g in range(NHG):
                turn_y(w_raw[:, CT + g, :], g)

            def step(s, b, h):
                for g in range(NHG):
                    pe.wait_ge(yt_ready, s * NHG + g + 1)
                    if before_step(s, 1) and g == LAST:
                        pe.wait_ge(wp_ready, HG)
                    mm = project(b, g)
                    if g == NHG - 1:
                        mm.then_inc(projected, 1)
                    if not (isinstance(s, int) and s == NT - 1):
                        if g == 0:
                            pe.wait_ge(y_loaded[1 - b], 16 * h + 16)
                        turn_y(y_raw[:, 1 - b, g, :], g)
                    if not before_step(s, 1):
                        if g == 1:
                            turn_x1(s - 1, 1 - b)
                        if g == 2:
                            if before_step(s, 2):
                                pe.wait_ge(const_loaded, 96)
                                pe.wait_ge(set_up, 6)
                            route(s - 1)
                        if g == 3:
                            rank(s - 1)

            token_steps(pe, step)
            turn_x1(NT - 1, 1)
            route(NT - 1)
            rank(NT - 1)


def expert_phase(nc, sem, w_experts, slots_x, slots_y, y_cleared, out_d, tables, shared):
    ident, w_raw, w_hi, w_lo, x1, gap, slot, we_split, raw_loaded, dispatched = shared
    end_i, n_tiles, bases, owner, from_tile, tables_known, padded, pad = tables
    ctx = ExitStack()
    with ctx:
        def sb(name, shape, dtype=F32):
            return ctx.enter_context(nc.sbuf_tensor(name, shape, dtype))

        WT = CT + FT
        gate = sb("gate", [P, 2, NT])
        beyond = sb("beyond", [P, 2 * NT, E - 1])
        shrink = sb("shrink", [P, E - 1])
        shift = sb("shift", [P, 2 * NT])
        slot_f = sb("slot_f3", [P, 2 * NT])
        slot_y = sb("slot_y", [P, 2, NT], dt.uint32)
        lower = sb("lower", [P, 2, NT])
        part = sb("part", [P, 2, 2, NT])
        xs = sb("xs", [P, 2, C])
        xt_hi = sb("xt_hi", [P, 2, C], F32R)
        xt_lo = sb("xt_lo", [P, 2, C], F32R)
        relu = sb("relu", [P, F])
        hid = sb("hid", [P, 2, F])
        ht_hi = sb("ht_hi", [P, 2, F], F32R)
        ht_lo = sb("ht_lo", [P, 2, F], F32R)
        yo = sb("yo", [P, 2, C])
        GB = RAW
        RB = 6
        res = sb("res3", [P, RB, C])
        stats = sb("stats3", [P, 6])
        mean_var = sb("mean_var3", [P, RB, 2])
        var_eps = sb("var_eps3", [P, RB])
        half = sb("half3", [P, 2])
        rstd = sb("rstd3", [P, RB])
        minus_mean = sb("minus_mean", [P, RB])
        FB = 4
        fin = sb("fin", [P, FB, C])

        def first_rows(t):
            return (w_hi, w_lo)[t % 2][:, expert_block(E - 3) + t // 2, :].bitcast(F32)

        def ps(name):
            return ctx.enter_context(nc.psum_tensor(name, [P, C], F32))

        xt_ps, h_ps, ht_ps, ye_ps = ([ps(f"{n}{b}") for b in range(2)] for n in ("xt_ps", "h_ps", "ht_ps", "ye_ps"))

        set_up = sem("e_set_up")
        step = sem("slot_step")
        slots_known = sem("slots_known")
        gap_exp, gates_known = sem("gap_exp"), sem("gates_known")
        we_loaded = sem("we_loaded")
        xs_loaded = [sem("xs_loaded0"), sem("xs_loaded1")]
        xs_turned, xt_rounded, xt_ready = sem("xs_turned"), sem("xt_rounded"), sem("xt_ready")
        up_done, relu_done, hid_ready = sem("up_done"), sem("relu_done"), sem("hid_ready")
        hid_turned, ht_rounded, ht_ready = sem("hid_turned"), sem("ht_rounded"), sem("ht_ready")
        down_done, yo_ready = sem("down_done"), sem("yo_ready")
        yo_stored = [sem("yo_stored0"), sem("yo_stored1")]
        gathered = [sem(f"gathered{b}") for b in range(GB)]
        first_gathered, first_added = sem("first_gathered"), sem("first_added")
        summed, stats_done = sem("e_summed"), sem("e_stats_done")
        var_ready, var_biased, rstd_ready = sem("e_var_ready"), sem("e_var_biased"), sem("e_rstd_ready")
        mean_ready, fin_ready = sem("mean_ready"), sem("fin_ready")
        fin_stored = [sem(f"fin_stored{i}") for i in range(FB)]
        block = ctx.enter_context(nc.Block())
        x_slots = slots_x.rearrange("(k p) c -> k p c", p=P)
        y_slots = slots_y.rearrange("(k p) c -> k p c", p=P)
        out_tiles = out_d.rearrange("(t p) c -> t p c", p=P)

        LOOPED = (SLOT_TILES - 4) // 2

        def slot_steps(engine, slot_step):
            with engine.Fori(0, LOOPED) as pair:
                for b in range(2):
                    slot_step(pair * 2 + b, b, pair)
            for k in range(2 * LOOPED, SLOT_TILES):
                slot_step(k, k % 2, k // 2)

        def more(k, ahead):
            return (k if isinstance(k, int) else 2 * LOOPED - 1) + ahead < SLOT_TILES

        @block.sync
        def _(sp):
            for b in range(2):
                sp.nop(nofuse=True).then_inc(yo_stored[b], 16)
            def load(k, b):
                at = sp.value_load(from_tile[0:1, k:k + 1] if isinstance(k, int) else from_tile[0:1, bass.ds(k, 1)],
                                   min_val=0, max_val=SPARE_TILE)
                return lambda: sp.dma_start(xs[:, b, :], rows_of(x_slots[bass.ds(at, 1), :, :]))\
                    .then_inc(xs_loaded[b], 16)

            for b in range(2):
                sp.wait_ge(dispatched[b], 32 * (NT // 2))
            sp.wait_ge(tables_known, 1)
            for k in range(4):
                if k < EARLY_PADS:
                    sp.wait_ge(padded[k], 16)
                else:
                    sp.wait_ge(padded[EARLY_PADS], 16 * (E - EARLY_PADS + 1))
                start = load(k, k % 2)
                if k >= 2:
                    sp.wait_ge(xs_turned, k - 1)
                start()
                if k == 1:
                    for e in range(EARLY_PADS, E):
                        pad(sp, e)

            def slot_step(k, b, h):
                if more(k, 4):
                    start = load(k + 4, b)
                if more(k, 4):
                    sp.wait_ge(xs_turned, k + 3)
                    sp.nop(nofuse=True)
                    start()
                sp.wait_ge(yo_ready, k + 1)
                sp.nop(nofuse=True)
                out = y_slots[k] if isinstance(k, int) else rows_of(y_slots[bass.ds(k, 1), :, :])
                sp.dma_start(out, yo[:, b, :]).then_inc(yo_stored[b], 16)

            sp.wait_ge(y_cleared, 16 * CLEAR_STEPS)
            slot_steps(sp, slot_step)
            for t in range(NT):
                sp.wait_ge(fin_ready, t + 1)
                sp.dma_start(out_tiles[t], fin[:, t % FB, :]).then_inc(fin_stored[t % FB], 16)
            for b in range(FB):
                sp.wait_ge(fin_stored[b], 16 * (NT // FB))

        @block.gpsimd
        def _(pool):
            def load_and_split(e, end):
                blk = expert_block(e)
                src = w_experts[e] if isinstance(e, int) else rows_of(w_experts[bass.ds(e, 1), :, :])
                if not (isinstance(e, int) and e == 1):
                    pool.dma_start(w_raw[:, :, :].rearrange("p s f -> p (s f)"), src).then_inc(raw_loaded, 16)
                pool.wait_ge(raw_loaded, 16 * e)
                if end is not None:
                    pool.wait_ge(down_done, end)
                    pool.nop(nofuse=True)
                hi = w_hi[:, blk:blk + WT, :] if isinstance(e, int) else w_hi[:, bass.ds(blk, WT), :]
                pool.dma_start(hi.rearrange("p s f -> p (s f)"), src).then_inc(we_loaded, 16)
                pool.wait_ge(we_loaded, 16 * e)
                for s in range(WT):
                    hi, lo = (w[:, blk + s, :] if isinstance(e, int) else one(w[:, bass.ds(blk + s, 1), :])
                              for w in (w_hi, w_lo))
                    nc.gpsimd.tensor_tensor(lo, w_raw[:, s, :], hi, ALU.subtract).then_inc(we_split, 1)
                pool.wait_ge(we_split, WT * e + WT)

            for b in range(2):
                pool.wait_ge(xs_loaded[b], 16)
            for e in (1, 2):
                load_and_split(e, None)
            pool.wait_ge(tables_known, 1)
            with pool.Fori(3, E) as e:
                end = pool.value_load(end_i[0:1, bass.ds(e - 3, 1)], min_val=1, max_val=SLOT_TILES)
                load_and_split(e, end)
            pool.wait_ge(slots_known, 1)
            end = pool.value_load(end_i[0:1, E - 2:E - 1], min_val=1, max_val=SLOT_TILES)
            pool.wait_ge(yo_stored[0], (end + 1) // 2 * 16 + 16)
            pool.wait_ge(yo_stored[1], end // 2 * 16 + 16)
            pool.nop(nofuse=True)
            for t in range(NT):
                pool.indirect_dma_start(first_rows(t), None, slots_y,
                                        bass.IndirectOffsetOnAxis(ap=slot_y[:, 0, t:t + 1], axis=0))\
                    .then_inc(first_gathered, 16)
            pool.wait_ge(yo_stored[0], 16 * ((SLOT_TILES + 1) // 2 + 1))
            pool.wait_ge(yo_stored[1], 16 * (SLOT_TILES // 2 + 1))

            def gather(t):
                if t >= GB:
                    pool.wait_ge(summed, t - GB + 1)
                pool.indirect_dma_start(w_raw[:, t % GB, :], None, slots_y,
                                        bass.IndirectOffsetOnAxis(ap=slot_y[:, 1, t:t + 1], axis=0))\
                    .then_inc(gathered[t % GB], 16)

            for t in range(GB - 1):
                gather(t)
            pool.wait_ge(set_up, 1)
            for t in range(NT):
                if t + GB - 1 < NT:
                    gather(t + GB - 1)
                if t % 2 == 1 and t < NT - 2 or t >= NT - 2:
                    n = 2 if t < NT - 2 else 1
                    part = slice((t + 1 - n) % RB, (t + 1 - n) % RB + n)
                    pool.wait_ge(var_biased, t + 1)
                    nc.gpsimd.tensor_tensor(rstd[:, part], var_eps[:, part], half[:, 0:n], ALU.pow)\
                        .then_inc(rstd_ready, n)

        @block.scalar
        def _(act):
            act.nop(nofuse=True).then_inc(hid_ready, 1)
            nc.scalar.activation(gate[:, 1, :], gap[:, :], ACT.Exp).then_inc(gap_exp, 1)

            def round_x(b, count):
                act.wait_ge(xs_turned, count)
                nc.scalar.activation(xt_hi[:, b, :], xt_ps[b][:, :], ACT.Copy).then_inc(xt_rounded, 1)

            def rectify(b, k):
                act.wait_ge(up_done, k + 1)
                act.wait_ge(hid_ready, k + 1)
                nc.scalar.activation(relu[:, :], h_ps[b][:, :], ACT.Relu).then_inc(relu_done, 1)

            round_x(0, 1)
            rectify(0, 0)
            round_x(1, 2)

            def slot_step(k, b, h):
                act.wait_ge(hid_turned, k + 1)
                nc.scalar.activation(ht_hi[:, b, :], ht_ps[b][:, :], ACT.Copy).then_inc(ht_rounded, 1)
                if more(k, 1):
                    rectify(1 - b, k + 1)
                if more(k, 2):
                    round_x(b, k + 3)
                act.wait_ge(down_done, k + 1)
                act.wait_ge(yo_stored[b], h * 16 + 16)
                nc.scalar.activation(yo[:, b, :], ye_ps[b][:, :], ACT.Copy).then_inc(yo_ready, 1)

            slot_steps(act, slot_step)
            for t in range(NT):
                b, q = t % FB, t % RB
                act.wait_ge(mean_ready, t + 1)
                if t >= FB:
                    act.wait_ge(fin_stored[b], 16 * (t // FB))
                nc.scalar.activation(fin[:, b, :], res[:, q, :], ACT.Identity, scale=rstd[:, q:q + 1],
                                     bias=minus_mean[:, q:q + 1]).then_inc(fin_ready, 1)

        @block.vector
        def _(dve):
            steps = [0]

            def then(op):
                steps[0] += 1
                op.then_inc(step, 1)
                dve.wait_ge(step, steps[0])

            nc.vector.memset(half[:, :], -0.5).then_inc(set_up, 1)
            all_slots = slot[:, :, :].rearrange("p t j -> p (t j)")
            then(nc.vector.tensor_tensor(beyond[:, :, :], all_slots.unsqueeze(2).to_broadcast([P, 2 * NT, E - 1]),
                                         bases[:, 1:E].unsqueeze(1)
                                         .to_broadcast([P, 2 * NT, E - 1]), ALU.is_gt))
            then(nc.vector.tensor_scalar(shrink[:, :], n_tiles[:, 0:E - 1], -float(REGION_TILES), float(P),
                                         ALU.add, ALU.mult))
            then(nc.vector.tensor_tensor(beyond[:, :, :], beyond[:, :, :],
                                         shrink[:, :].unsqueeze(1).to_broadcast([P, 2 * NT, E - 1]), ALU.mult))
            then(nc.vector.tensor_reduce(shift[:, :], beyond[:, :, :], AX.X, ALU.add))
            then(nc.vector.tensor_tensor(slot_f[:, :], all_slots, shift[:, :], ALU.add))
            by_rank = slot_f[:, :].rearrange("p (t j) -> p t j", j=2)
            nc.vector.tensor_tensor(slot_y[:, 0, :], by_rank[:, :, 0], by_rank[:, :, 1], ALU.min)
            nc.vector.tensor_tensor(slot_y[:, 1, :], by_rank[:, :, 0], by_rank[:, :, 1], ALU.max)\
                .then_inc(slots_known, 1)
            nc.vector.tensor_tensor(lower[:, 0, :], by_rank[:, :, 0], by_rank[:, :, 1], ALU.is_lt)
            then(nc.vector.tensor_tensor(lower[:, 1, :], by_rank[:, :, 0], by_rank[:, :, 1], ALU.is_gt))
            dve.wait_ge(gap_exp, 1)
            then(nc.vector.tensor_scalar(gap[:, :], gate[:, 1, :], 1.0, None, ALU.add))
            then(nc.vector.reciprocal(gate[:, 0, :], gap[:, :]))
            then(nc.vector.tensor_tensor(gate[:, 1, :], gate[:, 1, :], gate[:, 0, :], ALU.mult))
            for j in range(2):
                nc.vector.tensor_tensor(part[:, j, 0, :], gate[:, 0, :], lower[:, j, :], ALU.mult)
                op = nc.vector.tensor_tensor(part[:, j, 1, :], gate[:, 1, :], lower[:, 1 - j, :], ALU.mult)
            then(op)
            nc.vector.tensor_tensor(gate[:, :, :], part[:, :, 0, :], part[:, :, 1, :], ALU.add).then_inc(gates_known, 1)

            def split_x(b, count):
                dve.wait_ge(xt_rounded, count)
                nc.vector.tensor_tensor(xt_lo[:, b, :], xt_ps[b][:, :], xt_hi[:, b, :], ALU.subtract)\
                    .then_inc(xt_ready, 1)

            def square(b, count):
                dve.wait_ge(relu_done, count)
                nc.vector.tensor_tensor(hid[:, b, :], relu[:, :], relu[:, :], ALU.mult).then_inc(hid_ready, 1)

            split_x(0, 1)
            square(0, 1)
            split_x(1, 2)

            def slot_step(k, b, h):
                dve.wait_ge(ht_rounded, k + 1)
                nc.vector.tensor_tensor(ht_lo[:, b, :], ht_ps[b][:, :], ht_hi[:, b, :], ALU.subtract)\
                    .then_inc(ht_ready, 1)
                if more(k, 1):
                    square(1 - b, k + 2)
                if more(k, 2):
                    split_x(b, k + 3)

            slot_steps(dve, slot_step)
            dve.wait_ge(gates_known, 1)

            def scale_mean(t):
                q = t % RB
                dve.wait_ge(rstd_ready, t + 1)
                nc.vector.scalar_tensor_tensor(minus_mean[:, q:q + 1], mean_var[:, q, 0:1], -1.0, rstd[:, q:q + 1],
                                               ALU.mult, ALU.mult).then_inc(mean_ready, 1)

            dve.wait_ge(first_gathered, 16 * NT)
            for t in range(NT):
                nc.vector.scalar_tensor_tensor(x1[:, t, :], first_rows(t), gate[:, 0, t:t + 1],
                                               x1[:, t, :], ALU.mult, ALU.add).then_inc(first_added, 1)

            def add_second(t):
                dve.wait_ge(first_added, t + 1)
                dve.wait_ge(gathered[t % GB], 16 * (t // GB + 1))
                if t >= RB:
                    dve.wait_ge(fin_ready, t - RB + 1)
                nc.vector.scalar_tensor_tensor(res[:, t % RB, :], w_raw[:, t % GB, :], gate[:, 1, t:t + 1],
                                               x1[:, t, :], ALU.mult, ALU.add).then_inc(summed, 1)

            def bias_variance(t):
                dve.wait_ge(var_ready, t + 1)
                nc.vector.tensor_scalar(var_eps[:, t % RB:t % RB + 1], mean_var[:, t % RB, 1:2], EPS, None, ALU.add)\
                    .then_inc(var_biased, 1)

            for t in range(NT):
                add_second(t)
                if t >= 1:
                    bias_variance(t - 1)
                dve.wait_ge(summed, t + 1)
                nc.vector.bn_stats(stats[:, :], res[:, t % RB, :]).then_inc(stats_done, 1)
                if t >= 3:
                    scale_mean(t - 3)
                dve.wait_ge(stats_done, t + 1)
                nc.vector.bn_aggr(mean_var[:, t % RB, :], stats[:, :]).then_inc(var_ready, 1)
            bias_variance(NT - 1)
            for t in range(NT - 3, NT):
                scale_mean(t)

        @block.tensor
        def _(pe):
            def turn_x(b, loaded):
                pe.wait_ge(xs_loaded[b], loaded)
                for c in range(CT):
                    mm = nc.tensor.transpose(xt_ps[b][:, c * P:(c + 1) * P], xs[:, b, c * P:(c + 1) * P], ident[:, :])
                mm.then_inc(xs_turned, 1)

            def times(out, b, hi, lo, first_block):
                for c in range(CT):
                    for part in range(3):
                        a = (hi, hi, lo)[part][:, b, c * P:(c + 1) * P]
                        w = one((w_hi, w_lo, w_hi)[part][:, bass.ds(first_block + c, 1), :])
                        mm = nc.tensor.matmul(out[:, :], a, w, start=(c == part == 0), stop=(c == CT - 1 and part == 2))
                return mm

            def load_owner(k):
                at = owner[0:1, k:k + 1] if isinstance(k, int) else owner[0:1, bass.ds(k, 1)]
                return pe.value_load(at, min_val=0, max_val=E - 1)

            def up(b, e, count):
                pe.wait_ge(xt_ready, count)
                pe.wait_ge(we_split, WT * e + WT)
                times(h_ps[b], b, xt_hi, xt_lo, expert_block(e)).then_inc(up_done, 1)

            pe.wait_ge(tables_known, 1)
            turn_x(0, 16)
            up(0, load_owner(0), 1)
            turn_x(1, 16)

            def slot_step(k, b, h):
                pe.wait_ge(hid_ready, k + 2)
                for c in range(FT):
                    mm = nc.tensor.transpose(ht_ps[b][:, c * P:(c + 1) * P], hid[:, b, c * P:(c + 1) * P], ident[:, :])
                mm.then_inc(hid_turned, 1)
                if more(k, 1):
                    up(1 - b, load_owner(k + 1), k + 2)
                if more(k, 2):
                    turn_x(b, h * 16 + 32)
                e = load_owner(k)
                pe.wait_ge(ht_ready, k + 1)
                times(ye_ps[b], b, ht_hi, ht_lo, expert_block(e) + CT).then_inc(down_done, 1)

            slot_steps(pe, slot_step)


def build(nc, a, out_d):
    y_scratch = nc.dram_tensor("y_scratch", [NHG * NT + 1, P, GW], F32).ap()
    slots_x = nc.dram_tensor("slots_x", [(SPARE_TILE + 1) * P, C], F32).ap()
    slots_y = nc.dram_tensor("slots_y", [SLOT_TILES * P, C], F32).ap()
    ctx = ExitStack()
    with ctx:
        def sem(name):
            return ctx.enter_context(nc.semaphore(name))

        def sb(name, shape, dtype=F32):
            return ctx.enter_context(nc.sbuf_tensor(name, shape, dtype))

        w_raw = sb("w_raw", [P, RAW, GW])
        w_hi = sb("w_hi", [P, WB, GW], F32R)
        w_lo = sb("w_lo", [P, WB, GW], F32R)
        ident = sb("ident", [P, P])
        subln = sb("subln", [P, 1])
        x1_now = sb("x1_now", [P, 2, C])
        early_loaded = sem("early_loaded")
        wait_for_y = attention_phase(nc, sem, a["x_t"], a["w_all"], a["qk_w"], (a["ident"], a["dist"], a["slopes"]),
                                     y_scratch, ident, w_raw, w_hi, w_lo, early_loaded, a["subln_w"], subln, x1_now)
        run_i = sb("run_i", [P, E], dt.int32)
        slot_now = sb("slot_now", [P, 2, 2], dt.uint32)
        zeros = sb("zeros", [P, C])
        y_cleared = sem("y_cleared")
        padded = [sem(f"padded{i}") for i in range(EARLY_PADS + 1)]

        def pad(engine, e):
            at = engine.value_load(run_i[0:1, e:e + 1], min_val=0, max_val=(SPARE_TILE - 1) * P)
            engine.dma_start(slots_x[bass.ds(at, P), :], zeros[:, :]).then_inc(padded[min(e, EARLY_PADS)], 16)

        tables = (sb("end_i", [P, E], dt.int32),
                  sb("n_tiles", [P, E]),
                  sb("bases", [P, E]),
                  sb("owner", [P, SLOT_TILES], dt.int32),
                  sb("from_tile", [P, SLOT_TILES], dt.int32),
                  sem("tables_known"), padded, pad)
        shared = (ident, w_raw, w_hi, w_lo,
                  sb("x1", [P, NT, C]),
                  sb("gap", [P, NT]),
                  sb("slot", [P, NT, 2]),
                  sem("we_split"), sem("raw_loaded"), [sem("dispatched0"), sem("dispatched1")])
        residual_phase(nc, sem, y_scratch, a["w_last"], subln, early_loaded, wait_for_y, a["x"], a["w_router"],
                       (a["before"], a["experts"], a["bases"], a["floors"], a["tiles"]), a["w_experts"],
                       x1_now, slot_now, run_i, zeros, slots_x, slots_y, y_cleared, tables, shared)
        expert_phase(nc, sem, a["w_experts"], slots_x, slots_y, y_cleared, out_d, tables, shared)


def layout(inputs):
    x = np.ascontiguousarray(inputs["L0_attn_x"]).reshape(B * T, C)
    row, col = np.arange(P)[:, None], np.arange(T)[None, :]
    dist = (T - P + row - col).astype(np.float32)
    dist[dist < 0] = MASKED
    slopes = np.array([2.0 ** (-(i + 1) / 2) for i in range(H)], np.float32)

    def rows(v):
        return np.ascontiguousarray(np.broadcast_to(np.asarray(v, np.float32).reshape(1, -1), (P, np.size(v))))

    qkv = np.stack([np.asarray(inputs["L0_attn_W" + m]).reshape(CT, P, NHG, GW) for m in "qkv"])
    proj = np.asarray(inputs["L0_attn_Wproj"]).reshape(NHG * HG, P, C)
    w_all = np.concatenate([qkv.transpose(3, 1, 2, 0, 4).reshape(W_ROUNDS, P, 3 * GW),
                            proj[:3 * CT].reshape(CT, 3, P, C).transpose(0, 2, 1, 3).reshape(CT, P, 3 * C)])
    experts = np.concatenate([np.asarray(inputs["L0_ffn_w_fc"]).reshape(E, CT, P, F),
                              np.asarray(inputs["L0_ffn_w_proj"]).reshape(E, FT, P, C)], axis=1)
    bases = np.arange(E) * REGION_TILES * P
    floors = bases[:, None] + np.concatenate([[-1], P * np.arange(1, NT)])[None, :]
    return {
        "x_t": np.ascontiguousarray(x.reshape(NT, P, CT, P).transpose(0, 3, 2, 1)).reshape(NT, P, CT * P),
        "x": x,
        "w_all": np.ascontiguousarray(w_all),
        "w_last": np.ascontiguousarray(proj[3 * CT:].transpose(1, 0, 2)),
        "w_experts": np.ascontiguousarray(experts.transpose(0, 2, 1, 3)).reshape(E, P, (CT + FT) * F),
        "qk_w": np.ascontiguousarray(np.stack([inputs["L0_attn_q_rms_w"], inputs["L0_attn_k_rms_w"]], axis=1)),
        "subln_w": np.ascontiguousarray(inputs["L0_attn_subln_w"]).reshape(D, 1),
        "w_router": np.ascontiguousarray(inputs["L0_ffn_w_router"]),
        "ident": np.eye(P, dtype=np.float32), "dist": dist, "slopes": rows(slopes),
        "before": np.triu(np.ones((P, P), np.float32), 1),
        "experts": rows(np.arange(E)), "bases": rows(bases), "floors": rows(floors),
        "tiles": rows(np.repeat(np.arange(SLOT_TILES), E)),
    }


def kernel(**inputs):
    from concourse import bacc
    from concourse.bass_utils import run_bass_kernel_spmd

    nc = bacc.Bacc("TRN2", target_bir_lowering=False, num_devices=1)
    arrays = layout(inputs)
    aps = {n: nc.dram_tensor(f"in_{n}", v.shape, F32, kind="ExternalInput").ap() for n, v in arrays.items()}
    out_d = nc.dram_tensor("out", [B * T, C], F32, kind="ExternalOutput").ap()
    build(nc, aps, out_d)
    result = run_bass_kernel_spmd(nc, [{f"in_{n}": v for n, v in arrays.items()}], core_ids=[0])
    return result.results[0]["out"].reshape(B, T, C)
```
